# Optimizing a Trainium2 kernel written in Bass

```python
import numpy as np
import jax
import jax.numpy as jnp

def _softmax(x, axis=-1):
    return jax.nn.softmax(x, axis=axis)

def _gelu(x):
    return jax.nn.gelu(x, approximate=True)

def _silu(x):
    return jax.nn.silu(x)

def _sigmoid(x):
    return jax.nn.sigmoid(x)

def _layernorm(x, axis=-1, eps=1e-05):
    m = jnp.mean(x, axis=axis, keepdims=True)
    v = jnp.var(x, axis=axis, keepdims=True)
    return (x - m) / jnp.sqrt(v + eps)

def _scatter_add(tgt, idx, src, axis=0):
    return tgt.at[idx].add(src)

def _segment_sum(src, seg, n):
    return jax.ops.segment_sum(src, seg, n)
kernel_name = 'mk_gnn_resnorm_d2_gnn_r8_a830a1'

def setup_inputs(seed: int=0):
    np.random.seed(seed)
    _w = jnp.asarray

    def _rec_inputs():
        import jax
        import jax.numpy as jnp
        _gk = jax.random.key(seed)
        x = -0.0008691 + 1 * jax.random.normal(jax.random.fold_in(_gk, 1), (12500, 128), jnp.float32)
        _s = jax.random.randint(jax.random.fold_in(_gk, 2), (100000,), 0, 12500, jnp.int32)
        _d = jax.random.randint(jax.random.fold_in(_gk, 3), (100000,), 0, 12500, jnp.int32)
        _loop = jnp.arange(12500, dtype=jnp.int32)
        src = jnp.concatenate([_s, _d, _loop])
        dst = jnp.concatenate([_d, _s, _loop])
        _o = jnp.argsort(dst, stable=True)
        src = src[_o]
        dst = dst[_o]
        edge_attr_128 = -5.16925e-05 + 1.00005 * jax.random.normal(jax.random.fold_in(_gk, 11), (212500, 128), jnp.float32)
        return (x, src, dst, edge_attr_128)
    x, src, dst, edge_attr_128 = _rec_inputs()

    def _L0_gnn_setup():
        import jax, jax.numpy as jnp
        import numpy as np
        N_NODES = 1250
        N_EDGES = 80000
        D_IN = 128
        D_OUT = 128
        ALPHA = 0.5

        def _mean_aggregate(feats, seg_ids, num_segments):
            s = jax.ops.segment_sum(feats, seg_ids, num_segments=num_segments)
            cnt = jax.ops.segment_sum(jnp.ones((feats.shape[0],), feats.dtype), seg_ids, num_segments=num_segments)
            return s / jnp.maximum(cnt, 1.0)[:, None]
        key = jax.random.key(seed)
        ks = jax.random.split(key, 8)
        x = jax.random.normal(ks[0], (N_NODES, D_IN), dtype=jnp.float32)
        edge_index = jax.random.randint(ks[1], (2, N_EDGES), 0, N_NODES, dtype=jnp.int64)
        sc = 1.0 / np.sqrt(D_IN)
        W_s2d = jax.random.uniform(ks[2], (D_IN, D_OUT), jnp.float32, -sc, sc)
        b_s2d = jax.random.uniform(ks[3], (D_OUT,), jnp.float32, -sc, sc)
        W_d2s = jax.random.uniform(ks[4], (D_IN, D_OUT), jnp.float32, -sc, sc)
        b_d2s = jax.random.uniform(ks[5], (D_OUT,), jnp.float32, -sc, sc)
        W_self = jax.random.uniform(ks[6], (D_IN, D_OUT), jnp.float32, -sc, sc)
        b_self = jax.random.uniform(ks[7], (D_OUT,), jnp.float32, -sc, sc)
        return {'x': x, 'edge_index': edge_index, 'W_s2d': W_s2d, 'b_s2d': b_s2d, 'W_d2s': W_d2s, 'b_d2s': b_d2s, 'W_self': W_self, 'b_self': b_self}
    _L0_gnn_all = _L0_gnn_setup()
    _L0_gnn_in = {k: v for k, v in _L0_gnn_all.items() if k in ('W_s2d', 'b_s2d', 'W_d2s', 'b_d2s', 'W_self', 'b_self')}
    del _L0_gnn_all

    def _L1_gnn_setup():
        import jax, jax.numpy as jnp
        import numpy as np
        N, E, H, NH, HD = (6250, 100000, 128, 8, 16)

        def _layernorm(x, g, b, eps=1e-05):
            mu = jnp.mean(x, axis=-1, keepdims=True)
            var = jnp.mean(jnp.square(x - mu), axis=-1, keepdims=True)
            return (x - mu) * jax.lax.rsqrt(var + eps) * g + b
        key = jax.random.key(seed)
        ks = jax.random.split(key, 24)
        w = lambda k, shape, s=0.05: jax.random.normal(k, shape, jnp.float32) * s
        return {'x': jax.random.normal(ks[0], (N, H), jnp.float32), 'edge_index': jax.random.randint(ks[1], (2, E), 0, N, dtype=jnp.int64), 'curv': jax.random.normal(ks[2], (E, H), jnp.float32), 'Wq': w(ks[3], (H, H)), 'bq': jnp.zeros((H,), jnp.float32), 'Wk': w(ks[4], (H, H)), 'bk': jnp.zeros((H,), jnp.float32), 'Wv': w(ks[5], (H, H)), 'bv': jnp.zeros((H,), jnp.float32), 'Wo': w(ks[6], (H, H)), 'bo': jnp.zeros((H,), jnp.float32), 'Wc': w(ks[7], (H, NH)), 'bc': jnp.zeros((NH,), jnp.float32), 'W1': w(ks[8], (H, 4 * H)), 'b1': jnp.zeros((4 * H,), jnp.float32), 'W2': w(ks[9], (4 * H, H)), 'b2': jnp.zeros((H,), jnp.float32), 'g1': jnp.ones((H,), jnp.float32), 'be1': jnp.zeros((H,), jnp.float32), 'g2': jnp.ones((H,), jnp.float32), 'be2': jnp.zeros((H,), jnp.float32)}
    _L1_gnn_all = _L1_gnn_setup()
    _L1_gnn_in = {k: v for k, v in _L1_gnn_all.items() if k in ('Wq', 'bq', 'Wk', 'bk', 'Wv', 'bv', 'Wo', 'bo', 'Wc', 'bc', 'W1', 'b1', 'W2', 'b2', 'g1', 'be1', 'g2', 'be2')}
    del _L1_gnn_all
    return {'x': x, 'src': src, 'dst': dst, 'edge_attr_128': edge_attr_128, 'L0_gnn_W_s2d': _L0_gnn_in['W_s2d'], 'L0_gnn_b_s2d': _L0_gnn_in['b_s2d'], 'L0_gnn_W_d2s': _L0_gnn_in['W_d2s'], 'L0_gnn_b_d2s': _L0_gnn_in['b_d2s'], 'L0_gnn_W_self': _L0_gnn_in['W_self'], 'L0_gnn_b_self': _L0_gnn_in['b_self'], 'L1_gnn_Wq': _L1_gnn_in['Wq'], 'L1_gnn_bq': _L1_gnn_in['bq'], 'L1_gnn_Wk': _L1_gnn_in['Wk'], 'L1_gnn_bk': _L1_gnn_in['bk'], 'L1_gnn_Wv': _L1_gnn_in['Wv'], 'L1_gnn_bv': _L1_gnn_in['bv'], 'L1_gnn_Wo': _L1_gnn_in['Wo'], 'L1_gnn_bo': _L1_gnn_in['bo'], 'L1_gnn_Wc': _L1_gnn_in['Wc'], 'L1_gnn_bc': _L1_gnn_in['bc'], 'L1_gnn_W1': _L1_gnn_in['W1'], 'L1_gnn_b1': _L1_gnn_in['b1'], 'L1_gnn_W2': _L1_gnn_in['W2'], 'L1_gnn_b2': _L1_gnn_in['b2'], 'L1_gnn_g1': _L1_gnn_in['g1'], 'L1_gnn_be1': _L1_gnn_in['be1'], 'L1_gnn_g2': _L1_gnn_in['g2'], 'L1_gnn_be2': _L1_gnn_in['be2']}

def reference(x, src, dst, edge_attr_128, L0_gnn_W_s2d, L0_gnn_b_s2d, L0_gnn_W_d2s, L0_gnn_b_d2s, L0_gnn_W_self, L0_gnn_b_self, L1_gnn_Wq, L1_gnn_bq, L1_gnn_Wk, L1_gnn_bk, L1_gnn_Wv, L1_gnn_bv, L1_gnn_Wo, L1_gnn_bo, L1_gnn_Wc, L1_gnn_bc, L1_gnn_W1, L1_gnn_b1, L1_gnn_W2, L1_gnn_b2, L1_gnn_g1, L1_gnn_be1, L1_gnn_g2, L1_gnn_be2):
    import jax
    import jax.numpy as jnp

    def _L0_gnn_ref(x, edge_index, W_s2d, b_s2d, W_d2s, b_d2s, W_self, b_self):
        import jax, jax.numpy as jnp
        import numpy as np
        N_NODES = 1250
        N_EDGES = 80000
        D_IN = 128
        D_OUT = 128
        ALPHA = 0.5

        def _mean_aggregate(feats, seg_ids, num_segments):
            s = jax.ops.segment_sum(feats, seg_ids, num_segments=num_segments)
            cnt = jax.ops.segment_sum(jnp.ones((feats.shape[0],), feats.dtype), seg_ids, num_segments=num_segments)
            return s / jnp.maximum(cnt, 1.0)[:, None]
        n = x.shape[0]
        src, dst = (edge_index[0], edge_index[1])
        agg_s2d = _mean_aggregate(x[src], dst, n)
        agg_d2s = _mean_aggregate(x[dst], src, n)
        out = x @ W_self + b_self + (1.0 - ALPHA) * (agg_s2d @ W_s2d + b_s2d) + ALPHA * (agg_d2s @ W_d2s + b_d2s)
        return out

    def _L1_gnn_ref(x, edge_index, curv, Wq, bq, Wk, bk, Wv, bv, Wo, bo, Wc, bc, W1, b1, W2, b2, g1, be1, g2, be2):
        import jax, jax.numpy as jnp
        import numpy as np
        N, E, H, NH, HD = (6250, 100000, 128, 8, 16)

        def _layernorm(x, g, b, eps=1e-05):
            mu = jnp.mean(x, axis=-1, keepdims=True)
            var = jnp.mean(jnp.square(x - mu), axis=-1, keepdims=True)
            return (x - mu) * jax.lax.rsqrt(var + eps) * g + b
        num_nodes = x.shape[0]
        src, tgt = (edge_index[0], edge_index[1])
        x_norm = _layernorm(x, g1, be1)
        q = (x_norm @ Wq + bq).reshape(num_nodes, NH, HD)
        k = (x_norm @ Wk + bk).reshape(num_nodes, NH, HD)
        v = (x_norm @ Wv + bv).reshape(num_nodes, NH, HD)
        scores = jnp.einsum('ehd,ehd->eh', q[src], k[tgt]) / np.sqrt(HD).astype(np.float32)
        scores = scores + (curv @ Wc + bc)
        smax = jax.ops.segment_max(scores, tgt, num_segments=num_nodes)
        p = jnp.exp(scores - smax[tgt])
        ssum = jax.ops.segment_sum(p, tgt, num_segments=num_nodes)
        probs = p / ssum[tgt]
        messages = (probs[:, :, None] * v[tgt]).reshape(scores.shape[0], -1)
        out = jnp.zeros_like(x).at[src].add(messages)
        out = out @ Wo + bo
        x = x + out
        x_norm2 = _layernorm(x, g2, be2)
        ffn_out = jax.nn.relu(x_norm2 @ W1 + b1) @ W2 + b2
        return x + ffn_out
    edge_index = jnp.stack([src, dst])
    x = _layernorm(x + _L0_gnn_ref(x, edge_index, L0_gnn_W_s2d, L0_gnn_b_s2d, L0_gnn_W_d2s, L0_gnn_b_d2s, L0_gnn_W_self, L0_gnn_b_self), axis=-1)
    x = _layernorm(x + _L1_gnn_ref(x, edge_index, edge_attr_128, L1_gnn_Wq, L1_gnn_bq, L1_gnn_Wk, L1_gnn_bk, L1_gnn_Wv, L1_gnn_bv, L1_gnn_Wo, L1_gnn_bo, L1_gnn_Wc, L1_gnn_bc, L1_gnn_W1, L1_gnn_b1, L1_gnn_W2, L1_gnn_b2, L1_gnn_g1, L1_gnn_be1, L1_gnn_g2, L1_gnn_be2), axis=-1)
    return x

_drawn_inputs = setup_inputs


def setup_inputs(seed=0):
    import zlib

    import numpy as np

    out = dict(_drawn_inputs(seed))
    spreads = {'L1_gnn_bq': (0.0, 0.8),
     'L1_gnn_bk': (0.0, 0.8),
     'L1_gnn_bv': (0.0, 0.1),
     'L1_gnn_bo': (0.0, 0.1),
     'L1_gnn_bc': (0.0, 0.8),
     'L1_gnn_b1': (0.0, 0.1),
     'L1_gnn_b2': (0.0, 0.1),
     'L1_gnn_g1': (1.0, 0.6),
     'L1_gnn_be1': (0.0, 0.503),
     'L1_gnn_g2': (1.0, 0.2),
     'L1_gnn_be2': (0.0, 0.35)}
    factors = {'L1_gnn_Wq': 3.117, 'L1_gnn_Wk': 3.119}
    for name, (base, spread) in spreads.items():
        noise = np.random.default_rng([zlib.crc32(name.encode()), seed]).standard_normal(out[name].shape)
        drawn = base * np.exp(spread * noise) if base else spread * noise
        out[name] = jnp.asarray(drawn.astype(out[name].dtype))
    for name, factor in factors.items():
        out[name] = (out[name] * factor).astype(out[name].dtype)
    return out
```

```python
from contextlib import ExitStack

import numpy as np

import concourse.bass as bass
from concourse import mybir

ALU = mybir.AluOpType
ACT = mybir.ActivationFunctionType
AX = mybir.AxisListType
F32 = mybir.dt.float32
I32 = mybir.dt.int32
BF16 = mybir.dt.bfloat16
I16 = mybir.dt.int16

P = 128
HALF = P // 2
N_NODES = 12500
N_EDGES = 212500
D = 128
HEADS = 8
HEAD_D = D // HEADS
FF = 4 * D
FFC = FF // P
BLOCKS = -(-N_NODES // P)
LAST_ROWS = N_NODES - (BLOCKS - 1) * P
NODES_PAD = BLOCKS * P
CHUNKS = P // HEADS
TILES = 1664
EDGES_PAD = TILES * P
CHUNK_TILES = TILES // CHUNKS
CHUNK_EDGES = CHUNK_TILES * P
FULL_TILES = N_EDGES // P
LAST_EDGES = N_EDGES - FULL_TILES * P
U = 4
ITERS = TILES // U
ROW = D + 4
TABS = 4
TAB_ROWS = NODES_PAD + P
LOAD_BLOCKS = 14
BIG = 1.5e38
EPS = 1e-5


class Pass:

    def __init__(self, eng, q, counts=(1, 2), dmas=(), several=()):
        self.q = q
        self.known = {(1, 0): q}
        if not isinstance(q, int):
            for d in counts:
                self.known[1, d] = eng.snap(q + d)
            for d in dmas:
                self.known[16, d] = eng.snap((q + d) * 16)
            for times, d in several:
                self.known[times, d] = eng.snap((q + d) * times)

    def before(self, d=0, times=1):
        return (self.q + d) * times if isinstance(self.q, int) else self.known[times, d]

    def after(self, d=0, times=1):
        return self.before(d + 1, times)


def wait(eng, sem, value):
    if not (isinstance(value, int) and value <= 0):
        eng.wait_ge(sem, value)


def settle(eng, counter):
    eng.sem_inc(counter, 1)


def ahead(k, lead):
    return (k + lead) // U, (k + lead) % U


def freed(sems, k, back, it, d=0):
    return (sems[k - back], it.after(d)) if k >= back else (sems[k - back + U], it.before(d))


def col(a, it, d, k):
    t = it.q * U + (d * U + k)
    return a[:, t:t + 1] if isinstance(it.q, int) else a[:, bass.ds(t, 1)]


def block_at(it, s, d=0, size=1):
    b = it.q * (2 * size) + (s + 2 * d) * size
    return slice(b, b + size) if isinstance(it.q, int) else bass.ds(b, size)


def run_passes(eng, passes, **values):
    passes(Pass(eng, 0))
    with eng.Fori(1, ITERS - 1) as q:
        passes(Pass(eng, q, **values))
    passes(Pass(eng, ITERS - 1), True)


def run_skewed(eng, front, back, passes, **values):
    def both(it):
        front(it, 1)
        back(it)
    front(Pass(eng, 0), 0)
    both(Pass(eng, 0))
    with eng.Fori(1, passes - 1) as q:
        both(Pass(eng, q, **values))
    back(Pass(eng, passes - 1))


def run_woven(eng, early, front, late, passes, **values):
    def both(it):
        early(it)
        front(it, 1)
        late(it)
    front(Pass(eng, 0), 0)
    both(Pass(eng, 0))
    with eng.Fori(1, passes - 1) as q:
        both(Pass(eng, q, **values))
    early(Pass(eng, passes - 1))
    late(Pass(eng, passes - 1))


def load_steps(nc, eng, window, it, rows, most):
    at = slice(it.q, it.q + 1) if isinstance(it.q, int) else bass.ds(it.q, 1)
    _, values = nc.values_load_multi_w_load_instructions(
        window[0:1, at, rows, :].rearrange("o i a u -> o (i a u)"), engines=[eng.engine], min_val=0, max_val=most,
        skip_runtime_bounds_check_because="the table is made in range, whatever the edges")
    return values


def load_windows(nc, eng, window, it):
    values = load_steps(nc, eng, window, it, slice(0, 2), BLOCKS - 1)
    return values[0:U], values[U:2 * U]


def load_places(nc, eng, window, it):
    return load_steps(nc, eng, window, it, slice(2, 3), TILES - 1)



def dram(nc, name, shape, dt=F32):
    return nc.dram_tensor(name, shape, dt, kind="Internal").ap()


class Scope(ExitStack):

    def __init__(self, nc, tag):
        super().__init__()
        self.nc, self.tag = nc, tag
        self.sems = []

    def __exit__(self, *exc):
        super().__exit__(*exc)
        if self.sems:
            self.nc.clear_and_free_semaphores(self.sems)
            self.nc.all_engine_barrier()

    def sb(self, name, shape, dt=F32):
        return self.enter_context(self.nc.sbuf_tensor(self.tag + name, shape, dt))

    def ps(self, name, shape=(P, 512)):
        return self.enter_context(self.nc.psum_tensor(self.tag + name, list(shape), F32))

    def sem(self, name):
        self.sems.append(self.nc.alloc_semaphore(self.tag + name))
        return self.sems[-1]

    def sem_each(self, name, n=U):
        return [self.sem(f"{name}{i}") for i in range(n)]


class Shared:

    def __init__(self, nc, scope):
        self.sum_tabs = [dram(nc, f"sum_tab{i}", (TAB_ROWS, ROW)) for i in range(TABS)]
        self.msg_tabs = [dram(nc, f"msg_tab{i}", (TAB_ROWS, D)) for i in range(TABS)]
        self.q_tab = dram(nc, "q_tab", (NODES_PAD, D))
        self.kvy = dram(nc, "kvy", (P, BLOCKS, 3, D))
        self.curv_dram = dram(nc, "curv_dram", (P, TILES, HEADS))
        self.ident = scope.sb("ident", [P, P])
        self.iota = scope.sb("iota", [P, P])
        self.src_cols = scope.sb("src_cols", [P, TILES])
        self.rel_cols = scope.sb("rel_cols", [P, TILES])
        self.scat_cols = scope.sb("scat_cols", [P, TILES], I32)
        self.window = scope.sb("window", [1, ITERS, 3, U], I16)
        self.trash = scope.sb("trash", [P, 1])


def build(nc, x, src, dst, edge_attr, w, out):
    with Scope(nc, "") as whole:
        sh = Shared(nc, whole)
        stage_tables(nc, sh, src, dst)
        with Scope(nc, "a_") as sc:
            x_tab = sc.sb("x_tab", [P, BLOCKS, ROW])
            in_sum = sc.sb("in_sum", [P, BLOCKS, ROW])
            stage_aggregate(nc, sh, x, edge_attr, w, x_tab, in_sum)
            stage_first_nodes(nc, sh, w, x_tab, in_sum)
        with Scope(nc, "s_") as sc:
            scores = sc.sb("scores", [P, TILES, HEADS])
            stage_scores(nc, sh, scores)
            stage_softmax(nc, sh, dst, scores)
            stage_messages(nc, sh, scores)
        stage_last_nodes(nc, sh, w, out)


def stage_tables(nc, sh, src, dst):
    groups = TILES // P
    with Scope(nc, "t_") as sc:
        src_rows = sc.sb("src_rows", [P, groups, P], I32)
        dst_rows = sc.sb("dst_rows", [P, groups, P], I32)
        src_f = sc.sb("src_f", [P, groups, P])
        rel_i = sc.sb("rel_i", [P, groups, P], I32)
        rel_f = sc.sb("rel_f", [P, groups, P])
        first = sc.sb("first", [1, TILES], I32)
        half = sc.sb("half", [1, TILES], I32)
        half1 = sc.sb("half1", [1, TILES], I32)
        low = sc.sb("low", [1, TILES], I32)
        high = sc.sb("high", [1, TILES], I32)
        place = sc.sb("place", [1, TILES], I32)
        iota_i = sc.sb("iota_i", [P, P], I32)
        trash_i = sc.sb("trash_i", [P, 1], I32)
        zeros = sc.sb("zeros", [P, 9 * ROW])
        ps = [sc.ps(f"turn{i}", (P, 4, P)) for i in range(4)]
        loaded, made, cast, turned, copied, bits, zero_set, zeroed = (sc.sem(n) for n in (
            "loaded", "made", "cast", "turned", "copied", "bits", "zero_set", "zeroed"))
        block = sc.enter_context(nc.Block())
        quads = [(a, g0) for a in range(2) for g0 in range(0, groups, 4)]

        @block.sync
        def _(sp):
            sp.dma_start(src_rows[:], src.rearrange("(g p) e -> p g e", p=P)).then_inc(loaded, 16)
            sp.dma_start(dst_rows[:], dst[1:1 + EDGES_PAD].rearrange("(g p e) -> p g e", p=P, e=P)).then_inc(loaded, 16)
            with nc.allow_non_contiguous_dma(reason="one number of each tile"):
                sp.dma_start(first[:], dst[1:1 + EDGES_PAD].rearrange("(o t e) -> o t e", o=1, e=P)[:, :, 0])\
                    .then_inc(loaded, 16)
            sp.wait_ge(zero_set, 1)
            for tab in sh.sum_tabs + sh.msg_tabs:
                width = tab.shape[1] * 9
                sp.dma_start(tab.rearrange("(p a r) c -> p a (r c)", p=P, r=9),
                             zeros[:, None, 0:width].to_broadcast([P, TAB_ROWS // P // 9, width])).then_inc(zeroed, 16)
            sp.wait_ge(zeroed, 16 * 2 * TABS)

        @block.gpsimd
        def _(pool):
            pool.memset(sh.ident[:], 0.0).then_inc(made, 1)
            pool.iota(iota_i[:], [[1, P]], base=0, channel_multiplier=0).then_inc(made, 1)
            pool.iota(trash_i[:], [[0, 1]], base=NODES_PAD, channel_multiplier=1).then_inc(made, 1)
            pool.iota(place[:].rearrange("o (c j) -> o c j", c=CHUNKS), [[1, CHUNKS], [CHUNKS, CHUNK_TILES]], base=0,
                      channel_multiplier=0).then_inc(made, 1)
            pool.wait_ge(made, 1)
            pool.affine_select(out=sh.ident[:], in_=sh.ident[:], compare_op=ALU.not_equal, fill=1.0, base=0,
                               pattern=[[-1, P]], channel_multiplier=1).then_inc(made, 1)

        @block.vector
        def _(dve):
            dve.memset(zeros[:], 0.0).then_inc(zero_set, 1)
            dve.wait_ge(loaded, 48)
            dve.tensor_copy(src_f[:], src_rows[:]).then_inc(cast, 1)
            dve.tensor_scalar(rel_i[:], dst_rows[:], P - 1, None, ALU.bitwise_and).then_inc(bits, 1)
            dve.tensor_scalar(half[:], first[:], 6, None, ALU.arith_shift_right).then_inc(bits, 1)
            dve.wait_ge(bits, 1)
            dve.tensor_copy(rel_f[:], rel_i[:]).then_inc(cast, 1)
            dve.wait_ge(bits, 2)

            def steps(row):
                return row[:].rearrange("o (i u) -> o i u", u=U)
            dve.tensor_scalar(half1[:], half[:], 1, None, ALU.add).then_inc(bits, 1)
            dve.tensor_scalar(high[:], half[:], 1, None, ALU.arith_shift_right).then_inc(bits, 1)
            dve.wait_ge(bits, 3)
            dve.tensor_scalar(low[:], half1[:], 1, None, ALU.arith_shift_right).then_inc(bits, 1)
            dve.wait_ge(bits, 5)
            dve.tensor_scalar(sh.window[:, :, 0, :], steps(low), BLOCKS - 1, None, ALU.min)
            dve.tensor_scalar(sh.window[:, :, 1, :], steps(high), BLOCKS - 1, None, ALU.min)
            dve.wait_ge(made, 5)
            dve.tensor_copy(sh.iota[:], iota_i[:]).then_inc(cast, 1)
            dve.tensor_copy(sh.trash[:], trash_i[:]).then_inc(cast, 1)
            dve.tensor_copy(sh.window[:, :, 2, :], steps(place)).then_inc(cast, 1)
            for n, (a, g0) in enumerate(quads):
                m = min(4, groups - g0)
                to = (sh.src_cols, sh.rel_cols)[a]
                dve.wait_ge(turned, n + 1)
                dve.tensor_copy(to[:, g0 * P:(g0 + m) * P].rearrange("p (g t) -> p g t", t=P),
                                ps[n % 4][:, 0:m, :]).then_inc(copied, 1)

        @block.tensor
        def _(pe):
            pe.wait_ge(cast, 2)
            pe.wait_ge(made, 5)
            for n, (a, g0) in enumerate(quads):
                m = min(4, groups - g0)
                if n >= 4:
                    pe.wait_ge(copied, n - 3)
                for j in range(m):
                    ins = pe.transpose(ps[n % 4][:, j, :], (src_f, rel_f)[a][:, g0 + j, :], sh.ident[:])
                ins.then_inc(turned, 1)


def stage_aggregate(nc, sh, x, edge_attr, w, x_tab, in_sum):
    with Scope(nc, "a_") as sc:
        xs = sc.sb("xs", [P, U, ROW])
        onehot = sc.sb("onehot", [P, U, P])
        same = sc.sb("same", [P, 2, P])
        below = sc.sb("below", [P, P])
        junk = sc.sb("junk", [P, 2, P])
        dups = sc.sb("dups", [P, U])
        trash_row = sc.sb("trash_row", [P, U])
        pick = sc.sb("pick", [P, 2, 2, P])
        comb = sc.sb("comb", [P, U, ROW])
        gat_idx = sc.sb("gat_idx", [P, U], I32)
        scat_idx = sc.sb("scat_idx", [P, U], I32)
        src_slot = sc.sb("src_slot", [P, U])
        curv = sc.sb("curv", [P, U, D])
        curv_t = sc.sb("curv_t", [P, U, P])
        curv_s = sc.sb("curv_s", [P, U, HEADS])
        wc = sc.sb("wc", [P, HEADS])
        bc = sc.sb("bc", [P, U, HEADS])

        src_ps = [sc.ps(f"src_ps{i}") for i in range(2)]
        pick_ps = sc.ps("pick_ps")
        comb_ps = [sc.ps(f"comb_ps{i}") for i in range(2)]
        sum_ps = sc.ps("sum_ps")
        curv_ps = sc.ps("curv_ps", (P, U, P))
        score_ps = sc.ps("score_ps")

        laid, ready, loaded, issued = (sc.sem(n) for n in ("laid", "ready", "loaded", "issued"))
        (idx_set, slot_set, onehot_set, src_spread, same_set, dup_set, trash_set, scat_set, scat_kept, picked,
         pick_out, combined, comb_out, summed, sum_added, gathered, scattered) = (sc.sem_each(n) for n in (
             "idx_set", "slot_set", "onehot_set", "src_spread", "same_set", "dup_set", "trash_set", "scat_set",
             "scat_kept", "picked", "pick_out", "combined", "comb_out", "summed", "sum_added", "gathered",
             "scattered"))
        curv_in, curv_turned, curv_copied, curv_scored, curv_biased, curv_stored = (sc.sem(n) for n in (
            "curv_in", "curv_turned", "curv_copied", "curv_scored", "curv_biased", "curv_stored"))
        block = sc.enter_context(nc.Block())

        @block.sync
        def _(sp):
            sp.dma_start(wc[:], w["L1_gnn_Wc"]).then_inc(loaded, 16)
            sp.dma_start(bc[:], w["L1_gnn_bc"].rearrange("(o r h) -> o r h", o=1, r=1).to_broadcast([P, U, HEADS]))\
                .then_inc(loaded, 16)
            for b in range(0, BLOCKS, LOAD_BLOCKS):
                sp.dma_start(x_tab[:, b:b + LOAD_BLOCKS, 0:D], x[b * P:(b + LOAD_BLOCKS) * P]
                             .rearrange("(b p) c -> p b c", p=P)).then_inc(loaded, 16)
            sp.dma_start(curv[:], edge_attr[0:U * P, :].rearrange("(u p) c -> p u c", p=P)).then_inc(curv_in, 16)
            sp.wait_ge(loaded, 16 * (2 + BLOCKS // LOAD_BLOCKS))

            def store(it):
                wait(sp, curv_biased, it.after())
                at = it.q * U
                sp.dma_start(sh.curv_dram[:, at:at + U, :] if isinstance(it.q, int) else
                             sh.curv_dram[:, bass.ds(at, U), :], curv_s[:]).then_inc(curv_stored, 16)
            with sp.Fori(0, ITERS - 2) as q:
                it = Pass(sp, q, counts=(1,))
                sp.wait_ge(curv_turned, it.after())
                sp.dma_start(curv[:], edge_attr[bass.ds(q * (U * P) + U * P, U * P), :]
                             .rearrange("(u p) c -> p u c", p=P)).then_inc(curv_in, 16)
                store(it)
            sp.wait_ge(curv_turned, ITERS - 1)
            sp.dma_start(curv[0:LAST_EDGES, 0, :], edge_attr[FULL_TILES * P:N_EDGES, :]).then_inc(curv_in, 16)
            store(Pass(sp, ITERS - 2))
            store(Pass(sp, ITERS - 1))
            sp.wait_ge(curv_stored, 16 * ITERS)

        @block.gpsimd
        def _(pool):
            pool.memset(below[:], 0.0).then_inc(laid, 1)
            pool.wait_ge(laid, 1)
            pool.affine_select(out=below[:], in_=below[:], compare_op=ALU.is_ge, fill=1.0, base=0,
                               pattern=[[1, P]], channel_multiplier=-1).then_inc(ready, 1)

            def gather(it, d, k):
                wait(pool, idx_set[k], it.after(d))
                wait(pool, summed[k], it.before(d))
                settle(pool, issued)
                pool.indirect_dma_start(xs[:, k, 0:D], None, x, bass.IndirectOffsetOnAxis(
                    ap=gat_idx[:, k:k + 1], axis=0)).then_inc(gathered[k], 16)

            def scatter(it, k):
                wait(pool, scat_set[k], it.after())
                wait(pool, comb_out[k], it.after())
                wait(pool, scattered[k], it.before(0, 16))
                settle(pool, issued)
                pool.indirect_dma_start(sh.sum_tabs[k], bass.IndirectOffsetOnAxis(ap=scat_idx[:, k:k + 1], axis=0),
                                        comb[:, k, :], None, compute_op=ALU.add).then_inc(scattered[k], 16)

            def passes(it, last=False):
                for k in range(U):
                    d, kk = ahead(k, 2)
                    if not (last and d):
                        gather(it, d, kk)
                    scatter(it, k)
            pool.wait_ge(ready, 7)
            for k in range(2):
                gather(Pass(pool, 0), 0, k)
            run_passes(pool, passes, dmas=(0,))
            for k in range(U):
                pool.wait_ge(scattered[k], 16 * ITERS)

        @block.tensor
        def _(pe):
            pe.wait_ge(loaded, 16 * (2 + BLOCKS // LOAD_BLOCKS))
            pe.wait_ge(ready, 7)

            def spread(it, d, k):
                wait(pe, slot_set[k], it.after(d))
                wait(pe, *freed(dup_set, k, 2, it, d))
                pe.transpose(src_ps[k % 2][:, 0:P], src_slot[:, k:k + 1].to_broadcast([P, P]), sh.ident[:])\
                    .then_inc(src_spread[k], 1)

            def picks(it, d, k):
                wait(pe, same_set[k], it.after(d))
                wait(pe, onehot_set[k], it.after(d))
                wait(pe, *freed(pick_out, k, 1, it, d))
                pe.matmul(pick_ps[:, 0:P], onehot[:, k, :], same[:, k % 2, :], start=True, stop=True)\
                    .then_inc(picked[k], 1)

            def combine(it, k, low, high):
                wait(pe, pick_out[k], it.after())
                wait(pe, *freed(comb_out, k, 2, it))
                pe.matmul(comb_ps[k % 2][:, 0:ROW], pick[:, k % 2, 0, :], x_tab[:, bass.ds(low, 1), :],
                          start=True, stop=False)
                pe.matmul(comb_ps[k % 2][:, 0:ROW], pick[:, k % 2, 1, :], x_tab[:, bass.ds(high, 1), :],
                          start=False, stop=True).then_inc(combined[k], 1)

            def sums(it, k):
                wait(pe, gathered[k], it.after(0, 16))
                wait(pe, *freed(sum_added, k, 1, it))
                pe.matmul(sum_ps[:, 0:ROW], onehot[:, k, :], xs[:, k, :], start=True, stop=True)\
                    .then_inc(summed[k], 1)

            def turn_curvature(it):
                wait(pe, curv_in, it.after(0, 16))
                wait(pe, curv_copied, it.before())
                for u in range(U):
                    ins = pe.transpose(curv_ps[:, u, :], curv[:, u, :], sh.ident[:])
                ins.then_inc(curv_turned, 1)

            def score_curvature(it):
                wait(pe, curv_copied, it.after())
                wait(pe, curv_biased, it.before())
                for u in range(U):
                    ins = pe.matmul(score_ps[:, u * HEADS:(u + 1) * HEADS], curv_t[:, u, :], wc[:], start=True,
                                    stop=True)
                ins.then_inc(curv_scored, 1)

            def passes(it, last=False):
                low, high = load_windows(nc, pe, sh.window, it)
                for k in range(U):
                    combine(it, k, low[k], high[k])
                    sums(it, k)
                    for stage, lead in ((picks, 1), (spread, 2)):
                        d, kk = ahead(k, lead)
                        if not (last and d):
                            stage(it, d, kk)
                    if k == 0:
                        turn_curvature(it)
                    if k == 2:
                        score_curvature(it)
            first = Pass(pe, 0)
            spread(first, 0, 0)
            spread(first, 0, 1)
            picks(first, 0, 0)
            run_passes(pe, passes, dmas=(1,))

        @block.scalar
        def _(act):
            def pick_evac(it, d, k):
                wait(act, picked[k], it.after(d))
                wait(act, *freed(combined, k, 2, it, d))
                act.activation(pick[0:HALF, k % 2, 0, :], pick_ps[0:HALF, 0:P], ACT.Copy)
                act.activation(pick[HALF:P, k % 2, 1, :], pick_ps[HALF:P, 0:P], ACT.Copy).then_inc(pick_out[k], 1)

            def comb_evac(it, k):
                wait(act, combined[k], it.after())
                wait(act, scattered[k], it.before(0, 16))
                act.activation(comb[:, k, :], comb_ps[k % 2][:, 0:ROW], ACT.Copy).then_inc(comb_out[k], 1)

            def keep_rows(it, k):
                wait(act, scat_set[k], it.after())
                act.activation(col(sh.scat_cols, it, 0, k), scat_idx[:, k:k + 1], ACT.Copy).then_inc(scat_kept[k], 1)

            def curv_evac(it):
                wait(act, curv_turned, it.after())
                wait(act, curv_scored, it.before())
                act.activation(curv_t[:], curv_ps[:], ACT.Copy).then_inc(curv_copied, 1)

            def passes(it, last=False):
                for k in range(U):
                    comb_evac(it, k)
                    d, kk = ahead(k, 1)
                    if not (last and d):
                        pick_evac(it, d, kk)
                    keep_rows(it, k)
                    if k == 1:
                        curv_evac(it)
            act.wait_ge(ready, 7)
            pick_evac(Pass(act, 0), 0, 0)
            run_passes(act, passes, dmas=(0,))

        @block.vector
        def _(dve):
            dve.memset(x_tab[:, :, D:D + 1], 1.0).then_inc(ready, 1)
            dve.memset(x_tab[:, :, D + 1:ROW], 0.0).then_inc(ready, 1)
            dve.memset(xs[:, :, D:D + 1], 1.0).then_inc(ready, 1)
            dve.memset(xs[:, :, D + 1:ROW], 0.0).then_inc(ready, 1)
            dve.memset(pick[:], 0.0).then_inc(ready, 1)
            dve.memset(in_sum[:], 0.0).then_inc(ready, 1)
            dve.wait_ge(ready, 7)
            dve.wait_ge(loaded, 16 * (2 + BLOCKS // LOAD_BLOCKS))

            def index(it, d, k):
                wait(dve, gathered[k], it.before(d, 16))
                dve.tensor_scalar(gat_idx[:, k:k + 1], col(sh.src_cols, it, d, k), 0.0, None, ALU.max).then_inc(idx_set[k], 1)
                wait(dve, src_spread[k], it.before(d))
                dve.tensor_scalar(src_slot[:, k:k + 1], col(sh.src_cols, it, d, k), 0.0, None, ALU.max).then_inc(slot_set[k], 1)

            def hot(it, d, k):
                wait(dve, summed[k], it.before(d))
                wait(dve, picked[k], it.before(d))
                dve.tensor_scalar(onehot[:, k, :], sh.iota[:], col(sh.rel_cols, it, d, k), None, ALU.is_equal)\
                    .then_inc(onehot_set[k], 1)

            def match(it, d, k):
                wait(dve, src_spread[k], it.after(d))
                wait(dve, *freed(picked, k, 2, it, d))
                dve.tensor_scalar(same[:, k % 2, :], src_ps[k % 2][:, 0:P], col(sh.src_cols, it, d, k), None,
                                  ALU.is_equal).then_inc(same_set[k], 1)
                wait(dve, trash_set[k], it.before(d))
                wait(dve, *freed(dup_set, k, 2, it, d))
                dve.scalar_tensor_tensor(out=junk[:, k % 2, :], in0=src_ps[k % 2][:, 0:P],
                                         scalar=col(sh.src_cols, it, d, k), in1=below[:], op0=ALU.is_equal,
                                         op1=ALU.mult, accum_out=dups[:, k:k + 1]).then_inc(dup_set[k], 1)

            def rows(it, d, k):
                wait(dve, dup_set[k], it.after(d))
                wait(dve, scat_set[k], it.before(d))
                dve.tensor_scalar(trash_row[:, k:k + 1], dups[:, k:k + 1], 1.0, sh.trash[:], ALU.min, ALU.mult)\
                    .then_inc(trash_set[k], 1)
                wait(dve, trash_set[k], it.after(d))
                wait(dve, scattered[k], it.before(d, 16))
                wait(dve, scat_kept[k], it.before(d))
                dve.tensor_scalar(scat_idx[:, k:k + 1], trash_row[:, k:k + 1], col(sh.src_cols, it, d, k), None,
                                  ALU.max).then_inc(scat_set[k], 1)

            def add(it, k, low, high):
                wait(dve, summed[k], it.after())
                wait(dve, *freed(sum_added, k, 1, it))
                to = in_sum[0:HALF, bass.ds(low, 1), :].rearrange("p o c -> p (o c)")
                dve.tensor_tensor(to, to, sum_ps[0:HALF, 0:ROW], ALU.add)
                to = in_sum[HALF:P, bass.ds(high, 1), :].rearrange("p o c -> p (o c)")
                dve.tensor_tensor(to, to, sum_ps[HALF:P, 0:ROW], ALU.add).then_inc(sum_added[k], 1)

            def bias(it):
                wait(dve, curv_scored, it.after())
                wait(dve, curv_stored, it.before(0, 16))
                dve.tensor_tensor(curv_s[:], score_ps[:, 0:U * HEADS].rearrange("p (u h) -> p u h", h=HEADS), bc[:],
                                  ALU.add).then_inc(curv_biased, 1)

            def passes(it, last=False):
                low, high = load_windows(nc, dve, sh.window, it)
                for k in range(U):
                    for stage, lead in ((index, 3), (hot, 2), (match, 2), (rows, 1)):
                        d, kk = ahead(k, lead)
                        if not (last and d):
                            stage(it, d, kk)
                    add(it, k, low[k], high[k])
                    if k == 3:
                        bias(it)
            first = Pass(dve, 0)
            for k in range(3):
                index(first, 0, k)
            for k in range(2):
                hot(first, 0, k)
                match(first, 0, k)
            rows(first, 0, 0)
            run_passes(dve, passes, dmas=(0, 1))


NODE_PASSES = BLOCKS // 2


def stage_first_nodes(nc, sh, w, x_tab, in_sum):
    with Scope(nc, "n_") as sc:
        out_parts = sc.sb("out_parts", [P, 2, TABS, ROW])
        pair_sum = sc.sb("pair_sum", [P, 2, 2, ROW])
        out_sum = sc.sb("out_sum", [P, 2, ROW])
        count = sc.sb("count", [P, 2, 2])
        inv = sc.sb("inv", [P, 2, 2])
        terms = sc.sb("terms", [P, 2, 3, D])
        turned = sc.sb("turned", [P, 2, 3, P])
        stats = sc.sb("stats", [P, 2, 2, 6])
        mean_var = sc.sb("mean_var", [P, 2, 2, 2])
        std = sc.sb("std", [P, 2, 2])
        rstd = sc.sb("rstd", [P, 2, 2])
        eps = sc.sb("eps", [P, 1])
        normed = sc.sb("normed", [P, 2, D])
        normed_t = sc.sb("normed_t", [P, 2, P])
        q_out = sc.sb("q_out", [P, 2, D])
        kvy_out = sc.sb("kvy_out", [P, 2, 3, D])
        w_first = sc.sb("w_first", [P, 3, D])
        b_first = sc.sb("b_first", [1, 3, D])
        b_part = sc.sb("b_part", [1, D])
        b_all = sc.sb("b_all", [1, D])
        w_qkv = sc.sb("w_qkv", [P, 3, D])
        w_qkv_g = sc.sb("w_qkv_g", [P, 3, D])
        b_qkv = sc.sb("b_qkv", [1, 3, D])
        b_qkv_g = sc.sb("b_qkv_g", [1, 3, D])
        g1 = sc.sb("g1", [P, 1])
        be1 = sc.sb("be1", [P, 1])
        ones = sc.sb("ones", [1, P])
        turn_ps = [sc.ps(f"turn_ps{i}", (P, 4, P)) for i in range(2)]
        out_ps = [sc.ps(f"out_ps{i}") for i in range(2)]
        norm_ps = [sc.ps(f"norm_ps{i}") for i in range(2)]
        qkv_ps = [sc.ps(f"qkv_ps{i}") for i in range(2)]

        weights, ready, bias_made, bias_kept, bias_half, aggregated = (sc.sem(n) for n in (
            "weights", "ready", "bias_made", "bias_kept", "bias_half", "aggregated"))
        (parts_in, paired, summed, x_copied, in_count, counted, inverted, in_mean, out_mean, turned_ps, turned_sb,
         first_out, stat1, agg1, std1, rstd1, y_out, stat2, agg2, std2, rstd2, norm_out, norm_turned, norm_t_out, qkv_out,
         q_copied, kv_copied, q_stored, kvy_stored) = (sc.sem_each(n, 2) for n in (
             "parts_in", "paired", "summed", "x_copied", "in_count", "counted", "inverted", "in_mean", "out_mean",
             "turned_ps", "turned_sb", "first_out", "stat1", "agg1", "std1", "rstd1", "y_out", "stat2", "agg2", "std2", "rstd2",
             "norm_out", "norm_turned", "norm_t_out", "qkv_out", "q_copied", "kv_copied", "q_stored", "kvy_stored"))
        block = sc.enter_context(nc.Block())
        n_weights = 16 * 14
        n_ready = 4

        def row(name):
            return w[name].rearrange("(o c) -> o c", o=1)

        def column(name):
            return w[name].rearrange("(c o) -> c o", o=1)

        @block.sync
        def _(sp):
            for i, n in enumerate(("s2d", "d2s", "self")):
                sp.dma_start(w_first[:, i, :], w["L0_gnn_W_" + n]).then_inc(weights, 16)
                sp.dma_start(b_first[:, i, :], row("L0_gnn_b_" + n)).then_inc(weights, 16)
            for i, n in enumerate("qkv"):
                sp.dma_start(w_qkv[:, i, :], w["L1_gnn_W" + n]).then_inc(weights, 16)
                sp.dma_start(b_qkv[:, i, :], row("L1_gnn_b" + n)).then_inc(weights, 16)
            sp.dma_start(g1[:], column("L1_gnn_g1")).then_inc(weights, 16)
            sp.dma_start(be1[:], column("L1_gnn_be1")).then_inc(weights, 16)

            def front(it, d):
                for s in range(2):
                    wait(sp, summed[s], it.before(d))
                    for t in range(TABS):
                        sp.dma_start(out_parts[:, s, t, :], sh.sum_tabs[t][block_at(it, s, d, P), :])\
                            .then_inc(parts_in[s], 16)

            def back(it):
                for s in range(2):
                    wait(sp, q_copied[s], it.after())
                    sp.dma_start(sh.q_tab[block_at(it, s, 0, P), :], q_out[:, s, :]).then_inc(q_stored[s], 16)
                    wait(sp, kv_copied[s], it.after())
                    wait(sp, y_out[s], it.after())
                    at = block_at(it, s)
                    sp.dma_start(sh.kvy[:, at].rearrange("p o i c -> p (o i c)"),
                                 kvy_out[:, s].rearrange("p i c -> p (i c)")).then_inc(kvy_stored[s], 16)
            run_skewed(sp, front, back, NODE_PASSES)
            for s in range(2):
                sp.wait_ge(q_stored[s], 16 * NODE_PASSES)
                sp.wait_ge(kvy_stored[s], 16 * NODE_PASSES)

        @block.gpsimd
        def _(pool):
            def front(it, d):
                for s in range(2):
                    wait(pool, parts_in[s], it.after(d, 16 * TABS))
                    wait(pool, summed[s], it.before(d))
                    pool.tensor_tensor(pair_sum[:, s], out_parts[:, s, 0:2, :], out_parts[:, s, 2:4, :], ALU.add)\
                        .then_inc(paired[s], 1)
                    wait(pool, turned_ps[s], it.before(d))
                    wait(pool, first_out[s], it.before(d))
                    pool.tensor_copy(terms[:, s, 2, :], x_tab[:, block_at(it, s, d), 0:D]
                                     .rearrange("p o c -> p (o c)")).then_inc(x_copied[s], 1)
                    wait(pool, paired[s], it.after(d))
                    wait(pool, out_mean[s], it.before(d))
                    pool.tensor_tensor(out_sum[:, s], pair_sum[:, s, 0, :], pair_sum[:, s, 1, :], ALU.add)\
                        .then_inc(summed[s], 1)

            run_skewed(pool, front, lambda it: None, NODE_PASSES, several=((16 * TABS, 2),))

        @block.tensor
        def _(pe):
            pe.wait_ge(weights, n_weights)
            pe.wait_ge(ready, n_ready)
            pe.matmul(qkv_ps[0][0:1, 0:3 * D], be1[:], w_qkv[:], start=True, stop=False)
            pe.matmul(qkv_ps[0][0:1, 0:3 * D], ones[0:1, 0:1], b_qkv[:], start=False, stop=True)\
                .then_inc(bias_made, 1)
            pe.wait_ge(bias_kept, 1)

            def front(it, d):
                for s in range(2):
                    wait(pe, x_copied[s], it.after(d))
                    wait(pe, in_mean[s], it.after(d))
                    wait(pe, out_mean[s], it.after(d))
                    wait(pe, turned_sb[s], it.before(d))
                    for i in range(3):
                        ins = pe.transpose(turn_ps[s][:, i, :], terms[:, s, i, :], sh.ident[:])
                    ins.then_inc(turned_ps[s], 1)
                for s in range(2):
                    wait(pe, turned_sb[s], it.after(d))
                    wait(pe, y_out[s], it.before(d))
                    for i in range(3):
                        pe.matmul(out_ps[s][:, 0:D], turned[:, s, i, :], w_first[:, i, :], start=(i == 0), stop=False)
                    pe.matmul(out_ps[s][:, 0:D], ones[:], b_all[:], start=False, stop=False)
                    pe.matmul(out_ps[s][:, 0:D], sh.ident[:], terms[:, s, 2, :], start=False, stop=True)\
                        .then_inc(first_out[s], 1)

            def back(it):
                for s in range(2):
                    wait(pe, norm_out[s], it.after())
                    wait(pe, norm_t_out[s], it.before())
                    pe.transpose(norm_ps[s][:, 0:P], normed[:, s, :], sh.ident[:]).then_inc(norm_turned[s], 1)
                for s in range(2):
                    wait(pe, norm_t_out[s], it.after())
                    wait(pe, q_copied[s], it.before())
                    wait(pe, kv_copied[s], it.before())
                    pe.matmul(qkv_ps[s][:, 0:3 * D], normed_t[:, s, :], w_qkv_g[:], start=True, stop=False)
                    pe.matmul(qkv_ps[s][:, 0:3 * D], ones[:], b_qkv_g[:], start=False, stop=True)\
                        .then_inc(qkv_out[s], 1)
            run_skewed(pe, front, back, NODE_PASSES)

        @block.scalar
        def _(act):
            act.wait_ge(ready, n_ready)
            act.wait_ge(bias_made, 1)
            act.activation(b_qkv_g[:].rearrange("o i c -> o (i c)"), qkv_ps[0][0:1, 0:3 * D], ACT.Copy)\
                .then_inc(bias_kept, 1)

            def front(it, d):
                for s in range(2):
                    wait(act, inverted[s], it.after(d))
                    wait(act, turned_ps[s], it.before(d))
                    act.activation(terms[:, s, 0, :], in_sum[:, block_at(it, s, d), 0:D]
                                   .rearrange("p o c -> p (o c)"), ACT.Copy, scale=inv[:, s, 0:1])\
                        .then_inc(in_mean[s], 1)
                    act.activation(terms[:, s, 1, :], out_sum[:, s, 0:D], ACT.Copy, scale=inv[:, s, 1:2])\
                        .then_inc(out_mean[s], 1)
                for s in range(2):
                    wait(act, turned_ps[s], it.after(d))
                    wait(act, first_out[s], it.before(d))
                    act.activation(turned[:, s], turn_ps[s][:, 0:3, :], ACT.Copy).then_inc(turned_sb[s], 1)

            def back(it):
                for i, (agg, root, inverse) in enumerate(((agg1, std1, rstd1), (agg2, std2, rstd2))):
                    for s in range(2):
                        wait(act, agg[s], it.after())
                        wait(act, inverse[s], it.before())
                        act.activation(std[:, s, i:i + 1], mean_var[:, s, i, 1:2], ACT.Sqrt, bias=eps[:])\
                            .then_inc(root[s], 1)
                for s in range(2):
                    wait(act, norm_turned[s], it.after())
                    wait(act, qkv_out[s], it.before())
                    act.activation(normed_t[:, s, :], norm_ps[s][:, 0:P], ACT.Copy).then_inc(norm_t_out[s], 1)
                for s in range(2):
                    wait(act, qkv_out[s], it.after())
                    wait(act, q_stored[s], it.before(0, 16))
                    act.activation(q_out[:, s, :], qkv_ps[s][:, 0:D], ACT.Copy, scale=HEAD_D ** -0.5)\
                        .then_inc(q_copied[s], 1)
                    wait(act, kvy_stored[s], it.before(0, 16))
                    act.activation(kvy_out[:, s, 0:2, :], qkv_ps[s][:, D:3 * D].rearrange("p (i c) -> p i c", c=D),
                                   ACT.Copy).then_inc(kv_copied[s], 1)
            run_skewed(act, front, back, NODE_PASSES, dmas=(0,))

        @block.vector
        def _(dve):
            dve.wait_ge(weights, n_weights)
            dve.memset(ones[:], 1.0).then_inc(ready, 1)
            dve.memset(eps[:], EPS).then_inc(ready, 1)
            dve.tensor_scalar(w_qkv_g[:], w_qkv[:], g1[:], None, ALU.mult).then_inc(ready, 1)
            dve.scalar_tensor_tensor(out=b_part[:], in0=b_first[:, 0, :], scalar=0.5, in1=b_first[:, 2, :],
                                     op0=ALU.mult, op1=ALU.add).then_inc(bias_half, 1)
            dve.wait_ge(bias_half, 1)
            dve.scalar_tensor_tensor(out=b_all[:], in0=b_first[:, 1, :], scalar=0.5, in1=b_part[:],
                                     op0=ALU.mult, op1=ALU.add).then_inc(ready, 1)

            def front(it, d):
                for s in range(2):
                    wait(dve, inverted[s], it.before(d))
                    dve.tensor_scalar(count[:, s, 0:1], in_sum[:, block_at(it, s, d), D:D + 1]
                                      .rearrange("p o c -> p (o c)"), 1.0, 2.0, ALU.max, ALU.mult)\
                        .then_inc(in_count[s], 1)
                    wait(dve, summed[s], it.after(d))
                    dve.tensor_scalar(count[:, s, 1:2], out_sum[:, s, D:D + 1], 1.0, 2.0, ALU.max, ALU.mult)\
                        .then_inc(counted[s], 1)
                for s in range(2):
                    wait(dve, counted[s], it.after(d))
                    wait(dve, out_mean[s], it.before(d))
                    dve.reciprocal(inv[:, s, :], count[:, s, :]).then_inc(inverted[s], 1)

            def back(it):
                for s in range(2):
                    wait(dve, first_out[s], it.after())
                    wait(dve, agg1[s], it.before())
                    dve.bn_stats(stats[:, s, 0, :], out_ps[s][:, 0:D]).then_inc(stat1[s], 1)
                for s in range(2):
                    wait(dve, stat1[s], it.after())
                    wait(dve, y_out[s], it.before())
                    settle(dve, aggregated)
                    dve.bn_aggr(mean_var[:, s, 0, :], stats[:, s, 0, :]).then_inc(agg1[s], 1)
                for s in range(2):
                    wait(dve, std1[s], it.after())
                    wait(dve, y_out[s], it.before())
                    dve.reciprocal(rstd[:, s, 0:1], std[:, s, 0:1]).then_inc(rstd1[s], 1)
                for s in range(2):
                    wait(dve, rstd1[s], it.after())
                    wait(dve, kvy_stored[s], it.before(0, 16))
                    wait(dve, norm_out[s], it.before())
                    dve.tensor_scalar(kvy_out[:, s, 2, :], out_ps[s][:, 0:D], mean_var[:, s, 0, 0:1],
                                      rstd[:, s, 0:1], ALU.subtract, ALU.mult).then_inc(y_out[s], 1)
                for s in range(2):
                    wait(dve, y_out[s], it.after())
                    wait(dve, agg2[s], it.before())
                    dve.bn_stats(stats[:, s, 1, :], kvy_out[:, s, 2, :]).then_inc(stat2[s], 1)
                for s in range(2):
                    wait(dve, stat2[s], it.after())
                    wait(dve, norm_out[s], it.before())
                    settle(dve, aggregated)
                    dve.bn_aggr(mean_var[:, s, 1, :], stats[:, s, 1, :]).then_inc(agg2[s], 1)
                for s in range(2):
                    wait(dve, std2[s], it.after())
                    wait(dve, norm_out[s], it.before())
                    dve.reciprocal(rstd[:, s, 1:2], std[:, s, 1:2]).then_inc(rstd2[s], 1)
                for s in range(2):
                    wait(dve, rstd2[s], it.after())
                    wait(dve, norm_turned[s], it.before())
                    dve.tensor_scalar(normed[:, s, :], kvy_out[:, s, 2, :], mean_var[:, s, 1, 0:1],
                                      rstd[:, s, 1:2], ALU.subtract, ALU.mult).then_inc(norm_out[s], 1)
            run_skewed(dve, front, back, NODE_PASSES, dmas=(0,))


def stage_scores(nc, sh, scores):
    with Scope(nc, "b_") as sc:
        k_tab = sc.sb("k_tab", [P, BLOCKS, D])
        qs = sc.sb("qs", [P, U, D])
        onehot = sc.sb("onehot", [P, U, P])
        onehot_t = sc.sb("onehot_t", [P, 2, 2, P])
        prod = sc.sb("prod", [P, U, D])
        dots = sc.sb("dots", [P, U, HEADS])
        gat_idx = sc.sb("gat_idx", [P, U], I32)
        curv = sc.sb("curv", [P, 2, CHUNK_TILES, HEADS])
        turn_ps = [sc.ps(f"turn_ps{i}") for i in range(2)]
        kd_ps = [sc.ps(f"kd_ps{i}") for i in range(4)]

        loaded, ready, placed, issued = (sc.sem(n) for n in ("loaded", "ready", "placed", "issued"))
        curv_in = sc.sem_each("curv_in", 2)
        (idx_set, gathered, onehot_set, turned, turn_out, expanded, prod_set, dot_set, scored) = (
            sc.sem_each(n) for n in ("idx_set", "gathered", "onehot_set", "turned", "turn_out", "expanded",
                                     "prod_set", "dot_set", "scored"))
        block = sc.enter_context(nc.Block())
        n_loaded = 16 * (BLOCKS // LOAD_BLOCKS)

        @block.sync
        def _(sp):
            for b in range(0, BLOCKS, LOAD_BLOCKS):
                sp.dma_start(k_tab[:, b:b + LOAD_BLOCKS, :], sh.kvy[:, b:b + LOAD_BLOCKS, 0, :]).then_inc(loaded, 16)
            for c in range(CHUNKS):
                if c >= 2:
                    sp.wait_ge(placed, c - 1)
                sp.dma_start(curv[:, c % 2], sh.curv_dram[:, c * CHUNK_TILES:(c + 1) * CHUNK_TILES, :])\
                    .then_inc(curv_in[c % 2], 16)
            sp.wait_ge(loaded, n_loaded)

        @block.gpsimd
        def _(pool):
            def gather(it, d, k):
                wait(pool, idx_set[k], it.after(d))
                wait(pool, prod_set[k], it.before(d))
                settle(pool, issued)
                pool.indirect_dma_start(qs[:, k, :], None, sh.q_tab, bass.IndirectOffsetOnAxis(
                    ap=gat_idx[:, k:k + 1], axis=0)).then_inc(gathered[k], 16)
            for k in range(3):
                gather(Pass(pool, 0), 0, k)

            def passes(it, last=False):
                for k in range(U):
                    d, kk = ahead(k, 3)
                    if not (last and d):
                        gather(it, d, kk)
            run_passes(pool, passes)

        @block.tensor
        def _(pe):
            pe.wait_ge(loaded, n_loaded)

            def turn(it, d, k):
                wait(pe, onehot_set[k], it.after(d))
                wait(pe, *freed(turn_out, k, 2, it, d))
                pe.transpose(turn_ps[k % 2][:, 0:P], onehot[:, k, :], sh.ident[:]).then_inc(turned[k], 1)

            def expand(it, k, low, high):
                wait(pe, turn_out[k], it.after())
                wait(pe, prod_set[k], it.before())
                pe.matmul(kd_ps[k][:, 0:D], onehot_t[:, k % 2, 0, :], k_tab[:, bass.ds(low, 1), :], start=True,
                          stop=False)
                pe.matmul(kd_ps[k][:, 0:D], onehot_t[:, k % 2, 1, :], k_tab[:, bass.ds(high, 1), :], start=False,
                          stop=True).then_inc(expanded[k], 1)

            def passes(it, last=False):
                low, high = load_windows(nc, pe, sh.window, it)
                for k in range(U):
                    d, kk = ahead(k, 2)
                    if not (last and d):
                        turn(it, d, kk)
                    expand(it, k, low[k], high[k])
            turn(Pass(pe, 0), 0, 0)
            turn(Pass(pe, 0), 0, 1)
            run_passes(pe, passes)

        @block.scalar
        def _(act):
            for c in range(CHUNKS):
                act.wait_ge(curv_in[c % 2], 16 * (c // 2 + 1))
                act.activation(scores[:].rearrange("p (j c) h -> p j c h", c=CHUNKS)[:, :, c, :], curv[:, c % 2],
                               ACT.Copy).then_inc(placed, 1)
            act.wait_ge(ready, 1)

            def turn_evac(it, d, k):
                wait(act, turned[k], it.after(d))
                wait(act, *freed(expanded, k, 2, it, d))
                act.activation(onehot_t[0:HALF, k % 2, 0, :], turn_ps[k % 2][0:HALF, 0:P], ACT.Copy)
                act.activation(onehot_t[HALF:P, k % 2, 1, :], turn_ps[k % 2][HALF:P, 0:P], ACT.Copy)\
                    .then_inc(turn_out[k], 1)
            turn_evac(Pass(act, 0), 0, 0)

            def passes(it, last=False):
                for k in range(U):
                    d, kk = ahead(k, 1)
                    if not (last and d):
                        turn_evac(it, d, kk)
            run_passes(act, passes)

        @block.vector
        def _(dve):
            dve.memset(onehot_t[:], 0.0).then_inc(ready, 1)
            dve.wait_ge(placed, CHUNKS)

            def index(it, d, k):
                wait(dve, gathered[k], it.before(d, 16))
                dve.tensor_scalar(gat_idx[:, k:k + 1], col(sh.src_cols, it, d, k), 0.0, None, ALU.max).then_inc(idx_set[k], 1)

            def hot(it, d, k):
                wait(dve, turned[k], it.before(d))
                dve.tensor_scalar(onehot[:, k, :], sh.iota[:], col(sh.rel_cols, it, d, k), None, ALU.is_equal)\
                    .then_inc(onehot_set[k], 1)

            def product(it, k):
                wait(dve, expanded[k], it.after())
                wait(dve, gathered[k], it.after(0, 16))
                wait(dve, dot_set[k], it.before())
                dve.tensor_tensor(prod[:, k, :], kd_ps[k][:, 0:D], qs[:, k, :], ALU.mult).then_inc(prod_set[k], 1)

            def dot(it, k):
                wait(dve, prod_set[k], it.after())
                wait(dve, scored[k], it.before())
                dve.tensor_reduce(dots[:, k, :], prod[:, k, :].rearrange("p (h c) -> p h c", c=HEAD_D), AX.X,
                                  ALU.add).then_inc(dot_set[k], 1)

            def score(it, k, place):
                wait(dve, dot_set[k], it.after())
                to = scores[:, bass.ds(place, 1), :].rearrange("p o h -> p (o h)")
                dve.tensor_tensor(to, to, dots[:, k, :], ALU.add).then_inc(scored[k], 1)

            def passes(it, last=False):
                places = load_places(nc, dve, sh.window, it)
                for k in range(U):
                    for stage, lead in ((index, 3), (hot, 3)):
                        d, kk = ahead(k, lead)
                        if not (last and d):
                            stage(it, d, kk)
                    product(it, k)
                    if k:
                        score(it, k - 1, places[k - 1])
                    dot(it, k)
                score(it, U - 1, places[U - 1])
            for k in range(3):
                index(Pass(dve, 0), 0, k)
                hot(Pass(dve, 0), 0, k)
            run_passes(dve, passes, dmas=(0, 1))


def stage_softmax(nc, sh, dst, scores):
    with Scope(nc, "m_") as sc:
        PIECES = 4
        WIDTH = CHUNK_EDGES // PIECES
        rows = sc.sb("rows", [P, CHUNK_EDGES + 2])
        keep = sc.sb("keep", [P, CHUNK_EDGES + 1], BF16)
        drop = sc.sb("drop", [P, CHUNK_EDGES + 1], BF16)
        ends = sc.sb("ends", [1, 3, CHUNKS], I32)
        links = sc.sb("links", [1, CHUNKS + 1])
        single = sc.sb("single", [1, CHUNKS])
        go_on = sc.sb("go_on", [1, 2, CHUNKS])
        chain_keep = sc.sb("chain_keep", [1, 2, HEADS, CHUNKS])
        chain_drop = sc.sb("chain_drop", [1, 2, HEADS, CHUNKS])
        chain = sc.sb("chain", [1, HEADS, CHUNKS])
        start_row = sc.sb("start_row", [1, CHUNKS, HEADS])
        start_col = sc.sb("start_col", [P, 1])
        edge_col = sc.sb("edge_col", [P, 1])
        one = sc.sb("one", [1, 1])
        turn_ps = [sc.ps(f"turn_ps{i}", (P, 4, P)) for i in range(6)]
        row_ps, col_ps = sc.ps("row_ps"), sc.ps("col_ps")
        work = scores[:].rearrange("p t h -> p (t h)")

        loaded, ends_in, masks, vec, rows_turned, rows_by_act, rows_by_dve = (sc.sem(n) for n in (
            "loaded", "ends_in", "masks", "vec", "rows_turned", "rows_by_act", "rows_by_dve"))
        edge_turned, start_turned, shifted, exped, back_turned, back_by_act, back_by_dve, divided = (
            sc.sem(n) for n in ("edge_turned", "start_turned", "shifted", "exped", "back_turned", "back_by_act",
                                "back_by_dve", "divided"))
        block = sc.enter_context(nc.Block())
        GROUPS = CHUNK_TILES // 4
        CHAIN_AT = [10 + 8 * i for i in range(4)]
        dst_rows = rows[:].bitcast(I32)

        @block.sync
        def _(sp):
            cut = dst[0:EDGES_PAD].rearrange("(c i) -> c i", i=CHUNK_EDGES)
            cut2 = dst[2:2 + EDGES_PAD].rearrange("(c i) -> c i", i=CHUNK_EDGES)
            for h in range(HEADS):
                to = dst_rows[h::HEADS, :]
                sp.dma_start(to[:, 2:], cut2).then_inc(loaded, 16)
                sp.dma_start(to[:, 0:2], cut[:, 0:2]).then_inc(loaded, 16)
            with nc.allow_non_contiguous_dma(reason="one number of each chunk"):
                for i, (a, at) in enumerate(((cut, 0), (cut, 1), (cut2, CHUNK_EDGES - 2))):
                    sp.dma_start(ends[:, i, :], a[:, at:at + 1].rearrange("c o -> o c")).then_inc(ends_in, 16)
            sp.wait_ge(loaded, 16 * 2 * HEADS)
            sp.wait_ge(ends_in, 48)

        @block.tensor
        def _(pe):
            pe.wait_ge(masks, 2)
            by_column = scores[:].rearrange("p (j c) h -> p j (c h)", c=CHUNKS)
            for g in range(GROUPS):
                if g >= 6:
                    pe.wait_ge((rows_by_act, rows_by_dve)[g % 2], (g - 6) // 2 + 1)
                for u in range(4):
                    ins = pe.transpose(turn_ps[g % 6][:, u, :], by_column[:, 4 * g + u], sh.ident[:])
                ins.then_inc(rows_turned, 1)
            for n in range(4):
                pe.wait_ge(vec, CHAIN_AT[n])
                pe.transpose(row_ps[0:1, 0:P], edge_col[:], sh.ident[:]).then_inc(edge_turned, 1)
                pe.wait_ge(vec, CHAIN_AT[n] + 4)
                pe.matmul(col_ps[:, 0:1], start_row[:].rearrange("o c h -> o (c h)"), one[:], start=True, stop=True)\
                    .then_inc(start_turned, 1)
            for g in range(GROUPS):
                pe.wait_ge(divided, 4 * g // (CHUNK_TILES // PIECES) + 1)
                if (4 * g + 3) // (CHUNK_TILES // PIECES) != 4 * g // (CHUNK_TILES // PIECES):
                    pe.wait_ge(divided, (4 * g + 3) // (CHUNK_TILES // PIECES) + 1)
                if g >= 6:
                    pe.wait_ge((back_by_act, back_by_dve)[g % 2], (g - 6) // 2 + 1)
                for u in range(4):
                    at = (4 * g + u) * P
                    ins = pe.transpose(turn_ps[g % 6][:, u, :], rows[:, at:at + P], sh.ident[:])
                ins.then_inc(back_turned, 1)

        def rows_out(eng, copy, g, done):
            eng.wait_ge(rows_turned, g + 1)
            copy(rows[:, 4 * P * g:4 * P * (g + 1)], turn_ps[g % 6][:].rearrange("p u e -> p (u e)")).then_inc(done, 1)

        def back_out(eng, copy, g, done):
            eng.wait_ge(back_turned, g + 1)
            to = scores[:].rearrange("p (j c) h -> p j (c h)", c=CHUNKS)[:, 4 * g:4 * g + 4]
            copy(to, turn_ps[g % 6][:]).then_inc(done, 1)

        @block.scalar
        def _(act):
            def copy(to, frm):
                return act.activation(to, frm, ACT.Copy)
            for g in range(0, GROUPS, 2):
                rows_out(act, copy, g, rows_by_act)
            for i in range(PIECES):
                part = rows[:, i * WIDTH:(i + 1) * WIDTH]
                act.wait_ge(shifted, i + 1)
                act.activation(part, part, ACT.Exp).then_inc(exped, 1)
            act.wait_ge(divided, PIECES)
            for g in range(0, GROUPS, 2):
                back_out(act, copy, g, back_by_act)

        @block.vector
        def _(dve):
            n = [0]

            def then(ins):
                n[0] += 1
                ins.then_inc(vec, 1)
                dve.wait_ge(vec, n[0])

            dve.wait_ge(loaded, 16 * 2 * HEADS)
            a, b = dst_rows[:, 1:CHUNK_EDGES + 2], dst_rows[:, 0:CHUNK_EDGES + 1]
            dve.tensor_tensor(keep[:], a, b, ALU.is_equal).then_inc(masks, 1)
            dve.wait_ge(masks, 1)
            dve.tensor_scalar(drop[:], keep[:], 1.0, BIG, ALU.subtract, ALU.mult).then_inc(masks, 1)
            dve.wait_ge(ends_in, 48)
            dve.memset(one[:], 1.0)
            then(dve.memset(links[:], 0.0))
            then(dve.tensor_tensor(links[:, 0:CHUNKS], ends[:, 0, :], ends[:, 1, :], ALU.is_equal))
            then(dve.tensor_tensor(single[:], ends[:, 1, :], ends[:, 2, :], ALU.is_equal))
            then(dve.tensor_tensor(go_on[:, 0, :], single[:], links[:, 0:CHUNKS], ALU.mult))
            then(dve.tensor_tensor(go_on[:, 1, :], single[:], links[:, 1:CHUNKS + 1], ALU.mult))
            for i in range(2):
                then(dve.tensor_copy(chain_keep[:, i], go_on[:, i:i + 1, :].to_broadcast([1, HEADS, CHUNKS])))
            then(dve.tensor_scalar(chain_drop[:], chain_keep[:], 1.0, BIG, ALU.subtract, ALU.mult))
            assert n[0] == 8
            for g in range(1, GROUPS, 2):
                rows_out(dve, dve.tensor_copy, g, rows_by_dve)
            dve.wait_ge(rows_by_act, (GROUPS + 1) // 2)
            dve.wait_ge(rows_by_dve, GROUPS // 2)
            dve.wait_ge(masks, 2)
            r = rows[:, 0:CHUNK_EDGES]
            last = CHUNK_EDGES - 1

            def scan(to, frm, back, mask, start, op0, op1):
                if back:
                    return dve.tensor_tensor_scan(to[:, ::-1], mask[:, CHUNK_EDGES:0:-1], frm[:, ::-1], start, op0, op1)
                return dve.tensor_tensor_scan(to, mask[:, 0:CHUNK_EDGES], frm, start, op0, op1)

            def spread(i, frm, back, mask, chain_mask, rest, op0, op1):
                then(scan(work, frm, back, mask, rest, op0, op1))
                at = 0 if back else last
                then(dve.tensor_copy(edge_col[:], work[:, at:at + 1]))
                assert n[0] == CHAIN_AT[i], n[0]
                dve.wait_ge(edge_turned, i + 1)
                ordered = row_ps[0:1, 0:P].rearrange("o (c h) -> o h c", h=HEADS)
                then(dve.tensor_copy(chain[:], ordered))
                flat, m = chain[:].rearrange("o h c -> o (h c)"), chain_mask[:, int(back)].rearrange("o h c -> o (h c)")
                if back:
                    flat, m = flat[:, ::-1], m[:, ::-1]
                then(dve.tensor_tensor_scan(flat, m, flat, rest, op0, op1))
                then(dve.memset(start_row[:], rest))
                if back:
                    then(dve.tensor_copy(start_row[:, 0:CHUNKS - 1, :].rearrange("o c h -> o h c"), chain[:, :, 1:]))
                else:
                    then(dve.tensor_copy(start_row[:, 1:, :].rearrange("o c h -> o h c"), chain[:, :, 0:CHUNKS - 1]))
                dve.wait_ge(start_turned, i + 1)
                then(dve.tensor_copy(start_col[:], col_ps[:, 0:1]))
                then(scan(work, frm, back, mask, start_col[:], op0, op1))
            spread(0, r, False, drop, chain_drop, -BIG, ALU.add, ALU.max)
            spread(1, work, True, drop, chain_drop, -BIG, ALU.add, ALU.max)
            for i in range(PIECES):
                part = slice(i * WIDTH, (i + 1) * WIDTH)
                dve.tensor_tensor(rows[:, part], rows[:, part], work[:, part], ALU.subtract).then_inc(shifted, 1)
            dve.wait_ge(exped, PIECES)
            spread(2, r, False, keep, chain_keep, 0.0, ALU.mult, ALU.add)
            spread(3, work, True, keep, chain_keep, 0.0, ALU.mult, ALU.max)
            then(dve.reciprocal(work, work))
            for i in range(PIECES):
                part = slice(i * WIDTH, (i + 1) * WIDTH)
                dve.tensor_tensor(rows[:, part], rows[:, part], work[:, part], ALU.mult).then_inc(divided, 1)
            dve.wait_ge(divided, PIECES)
            for g in range(1, GROUPS, 2):
                back_out(dve, dve.tensor_copy, g, back_by_dve)


def stage_messages(nc, sh, probs):
    with Scope(nc, "c_") as sc:
        v_tab = sc.sb("v_tab", [P, BLOCKS, D])
        onehot = sc.sb("onehot", [P, U, P])
        onehot_t = sc.sb("onehot_t", [P, 2, 2, P])
        same = sc.sb("same", [P, U, P])
        message = sc.sb("message", [P, U, D])
        comb = sc.sb("comb", [P, U, D])
        scat_idx = sc.sb("scat_idx", [P, U], I32)
        src_slot = sc.sb("src_slot", [P, U])
        src_ps = [sc.ps(f"src_ps{i}") for i in range(2)]
        turn_ps = [sc.ps(f"turn_ps{i}") for i in range(2)]
        vd_ps = [sc.ps(f"vd_ps{i}") for i in range(2)]
        comb_ps = [sc.ps(f"comb_ps{i}") for i in range(2)]

        loaded, ready, issued = (sc.sem(n) for n in ("loaded", "ready", "issued"))
        (idx_set, slot_set, onehot_set, turned, turn_out, src_spread, same_set, expanded, message_set, combined,
         comb_out, scattered) = (sc.sem_each(n) for n in (
             "idx_set", "slot_set", "onehot_set", "turned", "turn_out", "src_spread", "same_set", "expanded",
             "message_set", "combined", "comb_out", "scattered"))
        block = sc.enter_context(nc.Block())
        n_loaded = 16 * (BLOCKS // LOAD_BLOCKS)

        @block.sync
        def _(sp):
            for b in range(0, BLOCKS, LOAD_BLOCKS):
                sp.dma_start(v_tab[:, b:b + LOAD_BLOCKS, :], sh.kvy[:, b:b + LOAD_BLOCKS, 1, :]).then_inc(loaded, 16)
            sp.wait_ge(loaded, n_loaded)

        @block.gpsimd
        def _(pool):
            def scatter(it, k):
                wait(pool, idx_set[k], it.after())
                wait(pool, comb_out[k], it.after())
                wait(pool, scattered[k], it.before(0, 16))
                settle(pool, issued)
                pool.indirect_dma_start(sh.msg_tabs[k], bass.IndirectOffsetOnAxis(ap=scat_idx[:, k:k + 1], axis=0),
                                        comb[:, k, :], None, compute_op=ALU.add).then_inc(scattered[k], 16)

            def passes(it, last=False):
                for k in range(U):
                    scatter(it, k)
            run_passes(pool, passes, dmas=(0,))
            for k in range(U):
                pool.wait_ge(scattered[k], 16 * ITERS)

        @block.tensor
        def _(pe):
            pe.wait_ge(loaded, n_loaded)

            def spread(it, d, k):
                wait(pe, slot_set[k], it.after(d))
                wait(pe, *freed(same_set, k, 2, it, d))
                pe.transpose(src_ps[k % 2][:, 0:P], src_slot[:, k:k + 1].to_broadcast([P, P]), sh.ident[:])\
                    .then_inc(src_spread[k], 1)

            def turn(it, d, k):
                wait(pe, onehot_set[k], it.after(d))
                wait(pe, *freed(turn_out, k, 2, it, d))
                pe.transpose(turn_ps[k % 2][:, 0:P], onehot[:, k, :], sh.ident[:]).then_inc(turned[k], 1)

            def expand(it, d, k, low, high):
                wait(pe, turn_out[k], it.after(d))
                wait(pe, *freed(message_set, k, 2, it, d))
                pe.matmul(vd_ps[k % 2][:, 0:D], onehot_t[:, k % 2, 0, :], v_tab[:, bass.ds(low, 1), :], start=True,
                          stop=False)
                pe.matmul(vd_ps[k % 2][:, 0:D], onehot_t[:, k % 2, 1, :], v_tab[:, bass.ds(high, 1), :],
                          start=False, stop=True).then_inc(expanded[k], 1)

            def combine(it, k):
                wait(pe, same_set[k], it.after())
                wait(pe, message_set[k], it.after())
                wait(pe, *freed(comb_out, k, 2, it))
                pe.matmul(comb_ps[k % 2][:, 0:D], same[:, k, :], message[:, k, :], start=True, stop=True)\
                    .then_inc(combined[k], 1)

            def passes(it, last=False):
                low, high = load_windows(nc, pe, sh.window, it)
                for k in range(U):
                    for stage, lead in ((turn, 2), (spread, 2)):
                        d, kk = ahead(k, lead)
                        if not (last and d):
                            stage(it, d, kk)
                    expand(it, 0, k, low[k], high[k])
                    if k:
                        combine(it, k - 1)
                combine(it, U - 1)
            for k in range(2):
                turn(Pass(pe, 0), 0, k)
                spread(Pass(pe, 0), 0, k)
            run_passes(pe, passes)

        @block.scalar
        def _(act):
            act.wait_ge(ready, 1)

            def turn_evac(it, d, k):
                wait(act, turned[k], it.after(d))
                wait(act, *freed(expanded, k, 2, it, d))
                act.activation(onehot_t[0:HALF, k % 2, 0, :], turn_ps[k % 2][0:HALF, 0:P], ACT.Copy)
                act.activation(onehot_t[HALF:P, k % 2, 1, :], turn_ps[k % 2][HALF:P, 0:P], ACT.Copy)\
                    .then_inc(turn_out[k], 1)

            def comb_evac(it, k):
                wait(act, combined[k], it.after())
                wait(act, scattered[k], it.before(0, 16))
                act.activation(comb[:, k, :], comb_ps[k % 2][:, 0:D], ACT.Copy).then_inc(comb_out[k], 1)

            def passes(it, last=False):
                for k in range(U):
                    d, kk = ahead(k, 1)
                    if not (last and d):
                        turn_evac(it, d, kk)
                    comb_evac(it, k)
            turn_evac(Pass(act, 0), 0, 0)
            run_passes(act, passes, dmas=(0,))

        @block.vector
        def _(dve):
            dve.memset(onehot_t[:], 0.0).then_inc(ready, 1)

            def index(it, d, k):
                wait(dve, scattered[k], it.before(d, 16))
                dve.tensor_scalar(scat_idx[:, k:k + 1], col(sh.scat_cols, it, d, k), 0.0, None, ALU.max).then_inc(idx_set[k], 1)

            def slot(it, d, k):
                wait(dve, src_spread[k], it.before(d))
                dve.tensor_scalar(src_slot[:, k:k + 1], col(sh.src_cols, it, d, k), 0.0, None, ALU.max).then_inc(slot_set[k], 1)

            def hot(it, d, k):
                wait(dve, turned[k], it.before(d))
                dve.tensor_scalar(onehot[:, k, :], sh.iota[:], col(sh.rel_cols, it, d, k), None, ALU.is_equal)\
                    .then_inc(onehot_set[k], 1)

            def match(it, d, k):
                wait(dve, src_spread[k], it.after(d))
                wait(dve, combined[k], it.before(d))
                dve.tensor_scalar(same[:, k, :], src_ps[k % 2][:, 0:P], col(sh.src_cols, it, d, k), None,
                                  ALU.is_equal).then_inc(same_set[k], 1)

            def weigh(it, k, place):
                wait(dve, expanded[k], it.after())
                wait(dve, combined[k], it.before())
                p = probs[:, bass.ds(place, 1), :]
                dve.tensor_tensor(message[:, k, :].rearrange("p (h c) -> p h c", c=HEAD_D),
                                  vd_ps[k % 2][:, 0:D].rearrange("p (h c) -> p h c", c=HEAD_D),
                                  p.rearrange("p o h -> p h o").to_broadcast([P, HEADS, HEAD_D]), ALU.mult)\
                    .then_inc(message_set[k], 1)

            def passes(it, last=False):
                places = load_places(nc, dve, sh.window, it)
                for k in range(U):
                    index(it, 0, k)
                    for stage, lead in ((slot, 3), (hot, 3), (match, 1)):
                        d, kk = ahead(k, lead)
                        if not (last and d):
                            stage(it, d, kk)
                    weigh(it, k, places[k])
            for k in range(3):
                slot(Pass(dve, 0), 0, k)
                hot(Pass(dve, 0), 0, k)
            match(Pass(dve, 0), 0, 0)
            run_passes(dve, passes, dmas=(0,))


def stage_last_nodes(nc, sh, w, out):
    with Scope(nc, "f_") as sc:
        msg_parts = sc.sb("msg_parts", [P, 2, TABS, D])
        pair_sum = sc.sb("pair_sum", [P, 2, 2, D])
        msg = sc.sb("msg", [P, 2, D])
        y = sc.sb("y", [P, 2, D])
        msg_t = sc.sb("msg_t", [P, 2, P])
        xy = sc.sb("xy", [P, 2, D])
        stats = sc.sb("stats", [P, 2, 2, 6])
        mean_var = sc.sb("mean_var", [P, 2, 2, 2])
        std = sc.sb("std", [P, 2, 2])
        rstd = sc.sb("rstd", [P, 2, 2])
        eps = sc.sb("eps", [P, 1])
        normed = sc.sb("normed", [P, 2, D])
        normed_t = sc.sb("normed_t", [P, 2, P])
        hidden = sc.sb("hidden", [P, 2, FFC, P])
        result = sc.sb("result", [P, 2, D])
        wo = sc.sb("wo", [P, D])
        w1 = sc.sb("w1", [P, FF])
        w1_g = sc.sb("w1_g", [P, FF])
        w2 = sc.sb("w2", [P, FFC, D])
        bo = sc.sb("bo", [1, D])
        b2 = sc.sb("b2", [1, D])
        b1 = sc.sb("b1", [P, FFC])
        b1_g = sc.sb("b1_g", [P, FFC])
        g2 = sc.sb("g2", [P, 1])
        be2 = sc.sb("be2", [P, 1])
        ones = sc.sb("ones", [1, P])
        turn_ps = [sc.ps(f"turn_ps{i}") for i in range(2)]
        x1_ps = [sc.ps(f"x1_ps{i}") for i in range(2)]
        hid_ps = [sc.ps(f"hid_ps{i}", (P, FFC, P)) for i in range(2)]
        out_ps = [sc.ps(f"out_ps{i}") for i in range(2)]

        weights, ready, bias_made, aggregated = (sc.sem(n) for n in ("weights", "ready", "bias_made", "aggregated"))
        (parts_in, y_in, paired, summed, msg_turned, msg_t_out, attended, xy_out, stat1, agg1, std1, rstd1, norm_out,
         norm_turned, norm_t_out, hid_out, relu_out, final_out, stat2, agg2, std2, rstd2, result_out, stored) = (
             sc.sem_each(n, 2) for n in (
                 "parts_in", "y_in", "paired", "summed", "msg_turned", "msg_t_out", "attended", "xy_out", "stat1",
                 "agg1", "std1", "rstd1", "norm_out", "norm_turned", "norm_t_out", "hid_out", "relu_out", "final_out",
                 "stat2", "agg2", "std2", "rstd2", "result_out", "stored"))
        block = sc.enter_context(nc.Block())
        n_weights = 16 * 8
        n_ready = 4

        @block.sync
        def _(sp):
            sp.dma_start(wo[:], w["L1_gnn_Wo"]).then_inc(weights, 16)
            sp.dma_start(w1[:], w["L1_gnn_W1"]).then_inc(weights, 16)
            sp.dma_start(w2[:], w["L1_gnn_W2"].rearrange("(i f) c -> f i c", f=P)).then_inc(weights, 16)
            for to, n in ((bo, "bo"), (b2, "b2")):
                sp.dma_start(to[:], w["L1_gnn_" + n].rearrange("(o c) -> o c", o=1)).then_inc(weights, 16)
            for to, n in ((g2, "g2"), (be2, "be2")):
                sp.dma_start(to[:], w["L1_gnn_" + n].rearrange("(c o) -> c o", o=1)).then_inc(weights, 16)
            with nc.allow_non_contiguous_dma(reason="a column of each chunk"):
                sp.dma_start(b1[:], w["L1_gnn_b1"].rearrange("(i f) -> f i", f=P)).then_inc(weights, 16)

            def front(it, d):
                for s in range(2):
                    wait(sp, summed[s], it.before(d))
                    for t in range(TABS):
                        sp.dma_start(msg_parts[:, s, t, :], sh.msg_tabs[t][block_at(it, s, d, P), :])\
                            .then_inc(parts_in[s], 16)
                    wait(sp, xy_out[s], it.before(d))
                    sp.dma_start(y[:, s, :], sh.kvy[:, block_at(it, s, d), 2, :].rearrange("p o c -> p (o c)"))\
                        .then_inc(y_in[s], 16)

            def back(it):
                for s in range(2):
                    wait(sp, result_out[s], it.after())
                    last = isinstance(it.q, int) and it.q == NODE_PASSES - 1
                    n = LAST_ROWS if last and s else P
                    b = it.q * (2 * P) + s * P
                    rows = slice(b, b + n) if isinstance(it.q, int) else bass.ds(b, P)
                    sp.dma_start(out[rows, :], result[0:n, s, :]).then_inc(stored[s], 16)
            run_skewed(sp, front, back, NODE_PASSES)
            for s in range(2):
                sp.wait_ge(stored[s], 16 * NODE_PASSES)

        @block.gpsimd
        def _(pool):
            def front(it, d):
                for s in range(2):
                    wait(pool, parts_in[s], it.after(d, 16 * TABS))
                    wait(pool, summed[s], it.before(d))
                    pool.tensor_tensor(pair_sum[:, s], msg_parts[:, s, 0:2, :], msg_parts[:, s, 2:4, :], ALU.add)\
                        .then_inc(paired[s], 1)
                    wait(pool, paired[s], it.after(d))
                    wait(pool, msg_turned[s], it.before(d))
                    pool.tensor_tensor(msg[:, s, :], pair_sum[:, s, 0, :], pair_sum[:, s, 1, :], ALU.add)\
                        .then_inc(summed[s], 1)

            run_skewed(pool, front, lambda it: None, NODE_PASSES, several=((16 * TABS, 2),))

        @block.tensor
        def _(pe):
            pe.wait_ge(weights, n_weights)
            for i in range(FFC):
                ins = pe.matmul(out_ps[0][:, i:i + 1], w1[:, i * P:(i + 1) * P], be2[:], start=True, stop=True)
            ins.then_inc(bias_made, 1)
            pe.wait_ge(ready, n_ready)

            def front(it, d):
                for s in range(2):
                    wait(pe, summed[s], it.after(d))
                    wait(pe, norm_out[s], it.before(d))
                    wait(pe, xy_out[s], it.before(d))
                    pe.transpose(x1_ps[s][:, P:2 * P], msg[:, s, :], sh.ident[:]).then_inc(msg_turned[s], 1)
                for s in range(2):
                    wait(pe, msg_t_out[s], it.after(d))
                    wait(pe, y_in[s], it.after(d, 16))
                    pe.matmul(x1_ps[s][:, 0:D], msg_t[:, s, :], wo[:], start=True, stop=False)
                    pe.matmul(x1_ps[s][:, 0:D], ones[:], bo[:], start=False, stop=False)
                    pe.matmul(x1_ps[s][:, 0:D], sh.ident[:], y[:, s, :], start=False, stop=True)\
                        .then_inc(attended[s], 1)

            def early(it):
                for s in range(2):
                    wait(pe, norm_out[s], it.after())
                    wait(pe, norm_t_out[s], it.before())
                    pe.transpose(turn_ps[s][:, 0:P], normed[:, s, :], sh.ident[:]).then_inc(norm_turned[s], 1)

            def late(it):
                for s in range(2):
                    wait(pe, norm_t_out[s], it.after())
                    wait(pe, relu_out[s], it.before())
                    for i in range(FFC):
                        ins = pe.matmul(hid_ps[s][:, i, :], w1_g[:, i * P:(i + 1) * P], normed_t[:, s, :], start=True,
                                        stop=True)
                    ins.then_inc(hid_out[s], 1)
                for s in range(2):
                    wait(pe, relu_out[s], it.after())
                    wait(pe, result_out[s], it.before())
                    pe.matmul(out_ps[s][:, 0:D], ones[:], b2[:], start=True, stop=False)
                    pe.matmul(out_ps[s][:, 0:D], sh.ident[:], xy[:, s, :], start=False, stop=False)
                    for i in range(FFC):
                        ins = pe.matmul(out_ps[s][:, 0:D], hidden[:, s, i, :], w2[:, i, :], start=False,
                                        stop=(i == FFC - 1))
                    ins.then_inc(final_out[s], 1)
            run_woven(pe, early, front, late, NODE_PASSES, dmas=(2,))

        @block.scalar
        def _(act):
            act.wait_ge(ready, n_ready)

            def front(it, d):
                for s in range(2):
                    wait(act, msg_turned[s], it.after(d))
                    wait(act, attended[s], it.before(d))
                    act.activation(msg_t[:, s, :], x1_ps[s][:, P:2 * P], ACT.Copy).then_inc(msg_t_out[s], 1)

            def roots(it, i, agg, root, inverse):
                for s in range(2):
                    wait(act, agg[s], it.after())
                    wait(act, inverse[s], it.before())
                    act.activation(std[:, s, i:i + 1], mean_var[:, s, i, 1:2], ACT.Sqrt, bias=eps[:])\
                        .then_inc(root[s], 1)

            def early(it):
                roots(it, 0, agg1, std1, rstd1)
                for s in range(2):
                    wait(act, norm_turned[s], it.after())
                    wait(act, hid_out[s], it.before())
                    act.activation(normed_t[:, s, :], turn_ps[s][:, 0:P], ACT.Copy).then_inc(norm_t_out[s], 1)

            def late(it):
                for s in range(2):
                    wait(act, hid_out[s], it.after())
                    wait(act, final_out[s], it.before())
                    for i in range(FFC):
                        ins = act.activation(hidden[:, s, i, :], hid_ps[s][:, i, :], ACT.Relu, bias=b1_g[:, i:i + 1])
                    ins.then_inc(relu_out[s], 1)
                roots(it, 1, agg2, std2, rstd2)
            run_woven(act, early, front, late, NODE_PASSES)

        @block.vector
        def _(dve):
            dve.wait_ge(weights, n_weights)
            dve.memset(ones[:], 1.0).then_inc(ready, 1)
            dve.memset(eps[:], EPS).then_inc(ready, 1)
            dve.tensor_scalar(w1_g[:], w1[:], g2[:], None, ALU.mult).then_inc(ready, 1)
            dve.wait_ge(bias_made, 1)
            dve.tensor_tensor(b1_g[:], out_ps[0][:, 0:FFC], b1[:], ALU.add).then_inc(ready, 1)

            def normalise(it, z, i, stat, agg, root, rs, z_done, spent, to, done):
                for s in range(2):
                    wait(dve, z_done[s], it.after())
                    wait(dve, agg[s], it.before())
                    dve.bn_stats(stats[:, s, i, :], z(s)).then_inc(stat[s], 1)
                for s in range(2):
                    wait(dve, stat[s], it.after())
                    wait(dve, done[s], it.before())
                    settle(dve, aggregated)
                    dve.bn_aggr(mean_var[:, s, i, :], stats[:, s, i, :]).then_inc(agg[s], 1)
                for s in range(2):
                    wait(dve, root[s], it.after())
                    wait(dve, done[s], it.before())
                    dve.reciprocal(rstd[:, s, i:i + 1], std[:, s, i:i + 1]).then_inc(rs[s], 1)
                for s in range(2):
                    wait(dve, rs[s], it.after())
                    wait(dve, *spent(s))
                    dve.tensor_scalar(to(s), z(s), mean_var[:, s, i, 0:1], rstd[:, s, i:i + 1], ALU.subtract,
                                      ALU.mult).then_inc(done[s], 1)

            def back(it):
                for s in range(2):
                    wait(dve, attended[s], it.after())
                    wait(dve, final_out[s], it.before())
                    dve.tensor_tensor(xy[:, s, :], x1_ps[s][:, 0:D], y[:, s, :], ALU.add).then_inc(xy_out[s], 1)
                normalise(it, lambda s: x1_ps[s][:, 0:D], 0, stat1, agg1, std1, rstd1, attended,
                          lambda s: (norm_turned[s], it.before()), lambda s: normed[:, s, :], norm_out)
                normalise(it, lambda s: out_ps[s][:, 0:D], 1, stat2, agg2, std2, rstd2, final_out,
                          lambda s: (stored[s], it.before(0, 16)), lambda s: result[:, s, :], result_out)
            run_skewed(dve, lambda it, d: None, back, NODE_PASSES, dmas=(0,))


_OUT_SHAPE = (N_NODES, D)


def kernel(**inputs):
    import concourse.bacc as bacc
    from concourse.bass_utils import run_bass_kernel_spmd

    nc = bacc.Bacc("TRN2", target_bir_lowering=False, num_devices=1)
    arrays, aps = {}, {}
    for name, a in inputs.items():
        a = np.ascontiguousarray(a)
        if name == "x":
            a = np.pad(a, ((0, NODES_PAD - N_NODES), (0, 0)))
        elif name == "src":
            a = np.pad(a, (0, EDGES_PAD - N_EDGES), constant_values=NODES_PAD - 1).reshape(TILES, P)
        elif name == "dst":
            a = np.pad(a, (1, EDGES_PAD - N_EDGES + 1), constant_values=(-1, NODES_PAD - 1))
            a[-1] = NODES_PAD
        arrays[name] = a
        aps[name] = nc.dram_tensor(f"{name}", a.shape, mybir.dt.from_np(a.dtype), kind="ExternalInput").ap()
    out = nc.dram_tensor("out", _OUT_SHAPE, F32, kind="ExternalOutput").ap()
    x, src, dst, edge_attr = (aps.pop(n) for n in ("x", "src", "dst", "edge_attr_128"))
    build(nc, x, src, dst, edge_attr, aps, out)
    return run_bass_kernel_spmd(nc, [arrays], core_ids=[0]).results[0]["out"]
```

```python
from contextlib import ExitStack

import numpy as np

import concourse.bass as bass
from concourse import mybir

ALU = mybir.AluOpType
ACT = mybir.ActivationFunctionType
AX = mybir.AxisListType
F32 = mybir.dt.float32
I32 = mybir.dt.int32
BF16 = mybir.dt.bfloat16
I16 = mybir.dt.int16

P = 128
HALF = P // 2
N_NODES = 12500
N_EDGES = 212500
D = 128
HEADS = 8
HEAD_D = D // HEADS
FF = 4 * D
FFC = FF // P
BLOCKS = -(-N_NODES // P)
LAST_ROWS = N_NODES - (BLOCKS - 1) * P
NODES_PAD = BLOCKS * P
CHUNKS = P // HEADS
TILES = 1664
EDGES_PAD = TILES * P
CHUNK_TILES = TILES // CHUNKS
CHUNK_EDGES = CHUNK_TILES * P
FULL_TILES = N_EDGES // P
LAST_EDGES = N_EDGES - FULL_TILES * P
U = 8
QUAD = 4
ITERS = TILES // U
ROW = D + 4
TABS = 4
TAB_ROWS = NODES_PAD + P
LOAD_BLOCKS = 14
BIG = 1.5e38
EPS = 1e-5


class Pass:

    def __init__(self, eng, q, counts=(1, 2), dmas=(), several=()):
        self.q = q
        self.known = {(1, 0): q}
        if not isinstance(q, int):
            for d in counts:
                self.known[1, d] = eng.snap(q + d)
            for d in dmas:
                self.known[16, d] = eng.snap((q + d) * 16)
            for times, d in several:
                self.known[times, d] = eng.snap((q + d) * times)

    def before(self, d=0, times=1):
        return (self.q + d) * times if isinstance(self.q, int) else self.known[times, d]

    def after(self, d=0, times=1):
        return self.before(d + 1, times)


def wait(eng, sem, value):
    if not (isinstance(value, int) and value <= 0):
        eng.wait_ge(sem, value)


def settle(eng, counter):
    eng.sem_inc(counter, 1)


def ahead(k, lead):
    return (k + lead) // U, (k + lead) % U


def freed(sems, k, back, it, d=0, times=1):
    n = len(sems)
    return (sems[k - back], it.after(d, times)) if k >= back else (sems[k - back + n], it.before(d, times))


def col(a, it, d, k):
    t = it.q * U + (d * U + k)
    return a[:, t:t + 1] if isinstance(it.q, int) else a[:, bass.ds(t, 1)]


def block_at(it, s, d=0, size=1):
    b = it.q * (2 * size) + (s + 2 * d) * size
    return slice(b, b + size) if isinstance(it.q, int) else bass.ds(b, size)


def run_passes(eng, passes, **values):
    passes(Pass(eng, 0))
    with eng.Fori(1, ITERS - 1) as q:
        passes(Pass(eng, q, **values))
    passes(Pass(eng, ITERS - 1), True)


def run_skewed(eng, front, back, passes, **values):
    def both(it):
        front(it, 1)
        back(it)
    front(Pass(eng, 0), 0)
    both(Pass(eng, 0))
    with eng.Fori(1, passes - 1) as q:
        both(Pass(eng, q, **values))
    back(Pass(eng, passes - 1))


def run_woven(eng, early, front, late, passes, **values):
    def both(it):
        early(it)
        front(it, 1)
        late(it)
    front(Pass(eng, 0), 0)
    both(Pass(eng, 0))
    with eng.Fori(1, passes - 1) as q:
        both(Pass(eng, q, **values))
    early(Pass(eng, passes - 1))
    late(Pass(eng, passes - 1))


def load_steps(nc, eng, table, it, first, each, most):
    t = it.q * U + first
    at = slice(t, t + QUAD) if isinstance(it.q, int) else bass.ds(t, QUAD)
    _, values = nc.values_load_multi_w_load_instructions(
        table[0:1, at, :].rearrange("o t a -> o (t a)"), engines=[eng.engine], min_val=0, max_val=most,
        skip_runtime_bounds_check_because="the table is made in range, whatever the edges")
    return [values[i * each:(i + 1) * each] for i in range(QUAD)]


def load_windows(nc, eng, sh, it, first):
    return load_steps(nc, eng, sh.window, it, first, 2, BLOCKS - 1)


def load_places(nc, eng, sh, it, first):
    return load_steps(nc, eng, sh.place, it, first, 1, TILES - 1)


def prepare(eng, stage, lead):
    for k in range(lead):
        stage(Pass(eng, 0), 0, k)


def advance(it, last, k, stages):
    for stage, lead in stages:
        d, kk = ahead(k, lead)
        if not (last and d):
            stage(it, d, kk)


def dram(nc, name, shape, dt=F32):
    return nc.dram_tensor(name, shape, dt, kind="Internal").ap()


class Scope(ExitStack):

    def __init__(self, nc, tag):
        super().__init__()
        self.nc, self.tag = nc, tag
        self.sems = []

    def __exit__(self, *exc):
        super().__exit__(*exc)
        if self.sems:
            self.nc.clear_and_free_semaphores(self.sems)
            self.nc.all_engine_barrier()

    def sb(self, name, shape, dt=F32):
        return self.enter_context(self.nc.sbuf_tensor(self.tag + name, shape, dt))

    def ps(self, name, shape=(P, 512)):
        return self.enter_context(self.nc.psum_tensor(self.tag + name, list(shape), F32))

    def sem(self, name):
        self.sems.append(self.nc.alloc_semaphore(self.tag + name))
        return self.sems[-1]

    def sem_each(self, name, n=U):
        return [self.sem(f"{name}{i}") for i in range(n)]


class Shared:

    def __init__(self, nc, scope):
        self.sum_tabs = [dram(nc, f"sum_tab{i}", (TAB_ROWS, ROW)) for i in range(TABS)]
        self.msg_tabs = [dram(nc, f"msg_tab{i}", (TAB_ROWS, D)) for i in range(TABS)]
        self.q_tab = dram(nc, "q_tab", (NODES_PAD, D))
        self.kvy = dram(nc, "kvy", (P, BLOCKS, 3, D))
        self.curv_dram = dram(nc, "curv_dram", (P, TILES, HEADS))
        self.ident = scope.sb("ident", [P, P])
        self.iota = scope.sb("iota", [P, P])
        self.src_cols = scope.sb("src_cols", [P, TILES])
        self.rel_cols = scope.sb("rel_cols", [P, TILES])
        self.scat_cols = scope.sb("scat_cols", [P, TILES], I32)
        self.window = scope.sb("window", [1, TILES + U, 2], I16)
        self.place = scope.sb("place", [1, TILES + U, 1], I16)
        self.regular = scope.sb("regular", [1, 1], I32)
        self.in_tab = dram(nc, "in_tab", (NODES_PAD, ROW))
        self.max_tab = dram(nc, "max_tab", (NODES_PAD, HEADS))
        self.weight_tab = dram(nc, "weight_tab", (NODES_PAD, HEADS))
        self.trash = scope.sb("trash", [P, 1])


def load_regular(nc, sh):
    return nc.values_load(sh.regular[0:1, 0:1], min_val=0, max_val=1,
                          skip_runtime_bounds_check_because="stage_tables makes it 0 or 1")


def build(nc, x, src, dst, edge_attr, w, out):
    with Scope(nc, "") as whole:
        sh = Shared(nc, whole)
        stage_tables(nc, sh, src, dst)
        with Scope(nc, "a_") as sc:
            x_tab = sc.sb("x_tab", [P, BLOCKS, ROW])
            in_sum = sc.sb("in_sum", [P, BLOCKS, ROW])
            with nc.If(load_regular(nc, sh) > 0):
                stage_aggregate(nc, sh, x, edge_attr, w, x_tab, in_sum)
            with nc.Else():
                general_aggregate(nc, sh, src, dst, x, edge_attr, w, x_tab, in_sum)
            stage_first_nodes(nc, sh, w, x_tab, in_sum)
        with Scope(nc, "s_") as sc:
            scores = sc.sb("scores", [P, TILES, HEADS])
            with nc.If(load_regular(nc, sh) > 0):
                stage_scores(nc, sh, scores)
                stage_softmax(nc, sh, dst, scores)
                stage_messages(nc, sh, scores)
            with nc.Else():
                general_scores(nc, sh, src, dst, scores)
                general_sums(nc, sh, src, dst, scores)
                general_messages(nc, sh, src, dst, scores)
        stage_last_nodes(nc, sh, w, out)


def stage_tables(nc, sh, src, dst):
    groups = TILES // P
    with Scope(nc, "t_") as sc:
        src_rows = sc.sb("src_rows", [P, groups, P], I32)
        dst_rows = sc.sb("dst_rows", [P, groups, P], I32)
        dst_before = sc.sb("dst_before", [P, groups, P], I32)
        unsorted = sc.sb("unsorted", [P, groups, P])
        span = sc.sb("span", [P, 2, groups], I32)
        wide = sc.sb("wide", [P, groups])
        faults = sc.sb("faults", [P, 2])
        fault = sc.sb("fault", [P, 1])
        worst = sc.sb("worst", [1, 1])
        src_f = sc.sb("src_f", [P, groups, P])
        rel_i = sc.sb("rel_i", [P, groups, P], I32)
        rel_f = sc.sb("rel_f", [P, groups, P])
        first = sc.sb("first", [1, TILES], I32)
        half = sc.sb("half", [1, TILES], I32)
        half1 = sc.sb("half1", [1, TILES], I32)
        low = sc.sb("low", [1, TILES], I32)
        high = sc.sb("high", [1, TILES], I32)
        place = sc.sb("place", [1, TILES], I32)
        iota_i = sc.sb("iota_i", [P, P], I32)
        trash_i = sc.sb("trash_i", [P, 1], I32)
        zeros = sc.sb("zeros", [P, 9 * ROW])
        ps = [sc.ps(f"turn{i}", (P, 4, P)) for i in range(4)]
        loaded, made, cast, turned, copied, bits, zero_set, zeroed, checks, fault_turned = (sc.sem(n) for n in (
            "loaded", "made", "cast", "turned", "copied", "bits", "zero_set", "zeroed", "checks", "fault_turned"))
        block = sc.enter_context(nc.Block())
        quads = [(a, g0) for a in range(2) for g0 in range(0, groups, 4)]

        @block.sync
        def _(sp):
            sp.dma_start(src_rows[:], src.rearrange("(g p) e -> p g e", p=P)).then_inc(loaded, 16)
            sp.dma_start(dst_rows[:], dst[1:1 + EDGES_PAD].rearrange("(g p e) -> p g e", p=P, e=P)).then_inc(loaded, 16)
            sp.dma_start(dst_before[:], dst[0:EDGES_PAD].rearrange("(g p e) -> p g e", p=P, e=P)).then_inc(loaded, 16)
            with nc.allow_non_contiguous_dma(reason="one number of each tile"):
                sp.dma_start(first[:], dst[1:1 + EDGES_PAD].rearrange("(o t e) -> o t e", o=1, e=P)[:, :, 0])\
                    .then_inc(loaded, 16)
            sp.wait_ge(zero_set, 1)
            for tab in sh.sum_tabs + sh.msg_tabs:
                width = tab.shape[1] * 9
                sp.dma_start(tab.rearrange("(p a r) c -> p a (r c)", p=P, r=9),
                             zeros[:, None, 0:width].to_broadcast([P, TAB_ROWS // P // 9, width])).then_inc(zeroed, 16)
            sp.wait_ge(zeroed, 16 * 2 * TABS)

        @block.gpsimd
        def _(pool):
            pool.memset(sh.ident[:], 0.0).then_inc(made, 1)
            pool.iota(iota_i[:], [[1, P]], base=0, channel_multiplier=0).then_inc(made, 1)
            pool.iota(trash_i[:], [[0, 1]], base=NODES_PAD, channel_multiplier=1).then_inc(made, 1)
            pool.iota(place[:].rearrange("o (c j) -> o c j", c=CHUNKS), [[1, CHUNKS], [CHUNKS, CHUNK_TILES]], base=0,
                      channel_multiplier=0).then_inc(made, 1)
            pool.wait_ge(made, 1)
            pool.affine_select(out=sh.ident[:], in_=sh.ident[:], compare_op=ALU.not_equal, fill=1.0, base=0,
                               pattern=[[-1, P]], channel_multiplier=1).then_inc(made, 1)

        @block.vector
        def _(dve):
            dve.memset(zeros[:], 0.0).then_inc(zero_set, 1)
            dve.wait_ge(loaded, 64)
            dve.tensor_copy(src_f[:], src_rows[:]).then_inc(cast, 1)
            dve.tensor_scalar(rel_i[:], dst_rows[:], P - 1, None, ALU.bitwise_and).then_inc(bits, 1)
            dve.tensor_scalar(half[:], first[:], 6, None, ALU.arith_shift_right).then_inc(bits, 1)
            dve.wait_ge(bits, 1)
            dve.tensor_copy(rel_f[:], rel_i[:]).then_inc(cast, 1)
            dve.wait_ge(bits, 2)

            dve.tensor_scalar(half1[:], half[:], 1, None, ALU.add).then_inc(bits, 1)
            dve.tensor_scalar(high[:], half[:], 1, None, ALU.arith_shift_right).then_inc(bits, 1)
            dve.wait_ge(bits, 3)
            dve.tensor_scalar(low[:], half1[:], 1, None, ALU.arith_shift_right).then_inc(bits, 1)
            dve.wait_ge(bits, 5)
            dve.tensor_scalar(sh.window[:, 0:TILES, 0], low[:], BLOCKS - 1, None, ALU.min)
            dve.tensor_scalar(sh.window[:, 0:TILES, 1], high[:], BLOCKS - 1, None, ALU.min)
            dve.memset(sh.window[:, TILES:, :], 0)
            dve.memset(sh.place[:, TILES:, :], 0)
            dve.wait_ge(made, 5)
            dve.tensor_copy(sh.iota[:], iota_i[:]).then_inc(cast, 1)
            dve.tensor_copy(sh.trash[:], trash_i[:]).then_inc(cast, 1)
            dve.tensor_copy(sh.place[:, 0:TILES, 0], place[:]).then_inc(cast, 1)
            for n, (a, g0) in enumerate(quads):
                m = min(4, groups - g0)
                to = (sh.src_cols, sh.rel_cols)[a]
                dve.wait_ge(turned, n + 1)
                dve.tensor_copy(to[:, g0 * P:(g0 + m) * P].rearrange("p (g t) -> p g t", t=P),
                                ps[n % 4][:, 0:m, :]).then_inc(copied, 1)

            dve.tensor_tensor(unsorted[:], dst_rows[:], dst_before[:], ALU.is_lt).then_inc(checks, 1)
            dve.tensor_scalar(span[:], dst_rows[:, :, 0:P:P - 1].rearrange("p g i -> p i g"), 6, None,
                              ALU.arith_shift_right).then_inc(checks, 1)
            dve.wait_ge(checks, 2)
            dve.tensor_reduce(faults[:, 0:1], unsorted[:], AX.XY, ALU.max).then_inc(checks, 1)
            dve.scalar_tensor_tensor(out=wide[:], in0=span[:, 1, :], scalar=-1.0, in1=span[:, 0, :], op0=ALU.add,
                                     op1=ALU.is_gt).then_inc(checks, 1)
            dve.wait_ge(checks, 4)
            dve.tensor_reduce(faults[:, 1:2], wide[:], AX.X, ALU.max).then_inc(checks, 1)
            dve.wait_ge(checks, 5)
            dve.tensor_tensor(fault[:], faults[:, 0:1], faults[:, 1:2], ALU.max).then_inc(checks, 1)
            dve.wait_ge(fault_turned, 1)
            dve.tensor_reduce(worst[:], ps[0][0:1, 0, :], AX.X, ALU.max).then_inc(checks, 1)
            dve.wait_ge(checks, 7)
            dve.tensor_scalar(sh.regular[:], worst[:], -1.0, 1.0, ALU.mult, ALU.add).then_inc(checks, 1)

        @block.tensor
        def _(pe):
            pe.wait_ge(cast, 2)
            pe.wait_ge(made, 5)
            for n, (a, g0) in enumerate(quads):
                m = min(4, groups - g0)
                if n >= 4:
                    pe.wait_ge(copied, n - 3)
                for j in range(m):
                    ins = pe.transpose(ps[n % 4][:, j, :], (src_f, rel_f)[a][:, g0 + j, :], sh.ident[:])
                ins.then_inc(turned, 1)
            pe.wait_ge(copied, len(quads))
            pe.wait_ge(checks, 6)
            pe.transpose(ps[0][0:1, 0, :], fault[:], sh.ident[:]).then_inc(fault_turned, 1)


def stage_aggregate(nc, sh, x, edge_attr, w, x_tab, in_sum):
    with Scope(nc, "a_") as sc:
        xs = sc.sb("xs", [P, U, ROW])
        onehot = sc.sb("onehot", [P, U, P])
        same = sc.sb("same", [P, 4, P])
        below = sc.sb("below", [P, P])
        junk = sc.sb("junk", [P, 2, P])
        dups = sc.sb("dups", [P, U])
        trash_row = sc.sb("trash_row", [P, U])
        pick = sc.sb("pick", [P, 4, 2, P])
        comb = sc.sb("comb", [P, U, ROW])
        gat_idx = sc.sb("gat_idx", [P, U], I32)
        scat_idx = sc.sb("scat_idx", [P, U], I32)
        src_slot = sc.sb("src_slot", [P, U])
        curv = sc.sb("curv", [P, 2, QUAD, D])
        curv_t = sc.sb("curv_t", [P, QUAD, P])
        curv_s = sc.sb("curv_s", [P, 2, QUAD, HEADS])
        wc = sc.sb("wc", [P, HEADS])
        bc = sc.sb("bc", [P, QUAD, HEADS])

        src_ps = [sc.ps(f"src_ps{i}") for i in range(2)]
        pick_ps = [sc.ps(f"pick_ps{i}") for i in range(2)]
        comb_ps = [sc.ps(f"comb_ps{i}") for i in range(2)]
        sum_ps = sc.ps("sum_ps")
        curv_ps = sc.ps("curv_ps", (P, QUAD, P))

        laid, ready, loaded, issued = (sc.sem(n) for n in ("laid", "ready", "loaded", "issued"))
        (idx_set, slot_set, onehot_set, src_spread, same_set, dup_set, trash_set, scat_set, scat_kept, picked,
         pick_out, combined, comb_out, summed, sum_added, gathered, scattered) = (sc.sem_each(n) for n in (
             "idx_set", "slot_set", "onehot_set", "src_spread", "same_set", "dup_set", "trash_set", "scat_set",
             "scat_kept", "picked", "pick_out", "combined", "comb_out", "summed", "sum_added", "gathered",
             "scattered"))
        curv_in, curv_turned, curv_copied, curv_scored, curv_biased, curv_stored = (sc.sem_each(n, 2) for n in (
            "curv_in", "curv_turned", "curv_copied", "curv_scored", "curv_biased", "curv_stored"))
        block = sc.enter_context(nc.Block())

        @block.sync
        def _(sp):
            sp.dma_start(wc[:], w["L1_gnn_Wc"]).then_inc(loaded, 16)
            sp.dma_start(bc[:], w["L1_gnn_bc"].rearrange("(o r h) -> o r h", o=1, r=1).to_broadcast([P, QUAD, HEADS]))\
                .then_inc(loaded, 16)
            for b in range(0, BLOCKS, LOAD_BLOCKS):
                sp.dma_start(x_tab[:, b:b + LOAD_BLOCKS, 0:D], x[b * P:(b + LOAD_BLOCKS) * P]
                             .rearrange("(b p) c -> p b c", p=P)).then_inc(loaded, 16)
            sp.wait_ge(loaded, 16 * (2 + BLOCKS // LOAD_BLOCKS))

            def load(it, d, j):
                wait(sp, curv_turned[j], it.before(d))
                t = it.q * U + (d * U + j * QUAD)
                full = not isinstance(it.q, int) or t + QUAD <= FULL_TILES
                if full:
                    rows = slice(t * P, (t + QUAD) * P) if isinstance(it.q, int) else bass.ds(t * P, QUAD * P)
                    sp.dma_start(curv[:, j], edge_attr[rows, :].rearrange("(u p) c -> p u c", p=P))\
                        .then_inc(curv_in[j], 16)
                else:
                    sp.dma_start(curv[0:LAST_EDGES, j, 0, :], edge_attr[FULL_TILES * P:N_EDGES, :])\
                        .then_inc(curv_in[j], 16)

            def passes(it, last=False):
                for j in range(2):
                    if not last:
                        load(it, 1, j)
                    wait(sp, curv_biased[j], it.after())
                    t = it.q * U + j * QUAD
                    at = slice(t, t + QUAD) if isinstance(it.q, int) else bass.ds(t, QUAD)
                    sp.dma_start(sh.curv_dram[:, at, :], curv_s[:, j]).then_inc(curv_stored[j], 16)
            for j in range(2):
                load(Pass(sp, 0), 0, j)
            passes(Pass(sp, 0))
            with sp.Fori(1, ITERS - 2) as q:
                passes(Pass(sp, q))
            passes(Pass(sp, ITERS - 2))
            passes(Pass(sp, ITERS - 1), True)
            for j in range(2):
                sp.wait_ge(curv_stored[j], 16 * ITERS)

        @block.gpsimd
        def _(pool):
            pool.memset(below[:], 0.0).then_inc(laid, 1)
            pool.wait_ge(laid, 1)
            pool.affine_select(out=below[:], in_=below[:], compare_op=ALU.is_ge, fill=1.0, base=0,
                               pattern=[[1, P]], channel_multiplier=-1).then_inc(ready, 1)

            def gather(it, d, k):
                wait(pool, idx_set[k], it.after(d))
                wait(pool, summed[k], it.before(d))
                settle(pool, issued)
                pool.indirect_dma_start(xs[:, k, 0:D], None, x, bass.IndirectOffsetOnAxis(
                    ap=gat_idx[:, k:k + 1], axis=0)).then_inc(gathered[k], 16)

            def scatter(it, d, k):
                wait(pool, scat_set[k], it.after())
                wait(pool, comb_out[k], it.after())
                wait(pool, *freed(scattered, k, TABS, it, 0, 16))
                settle(pool, issued)
                pool.indirect_dma_start(sh.sum_tabs[k % TABS], bass.IndirectOffsetOnAxis(ap=scat_idx[:, k:k + 1], axis=0),
                                        comb[:, k, :], None, compute_op=ALU.add).then_inc(scattered[k], 16)

            def passes(it, last=False):
                for k in range(U):
                    advance(it, last, k, ((gather, 3), (scatter, 0)))
            pool.wait_ge(ready, 7)
            prepare(pool, gather, 3)
            run_passes(pool, passes, dmas=(0, 1))
            for k in range(U):
                pool.wait_ge(scattered[k], 16 * ITERS)

        @block.tensor
        def _(pe):
            pe.wait_ge(loaded, 16 * (2 + BLOCKS // LOAD_BLOCKS))
            pe.wait_ge(ready, 7)

            def spread(it, d, k):
                wait(pe, slot_set[k], it.after(d))
                wait(pe, *freed(dup_set, k, 2, it, d))
                pe.transpose(src_ps[k % 2][:, 0:P], src_slot[:, k:k + 1].to_broadcast([P, P]), sh.ident[:])\
                    .then_inc(src_spread[k], 1)

            def picks(it, d, k):
                wait(pe, same_set[k], it.after(d))
                wait(pe, onehot_set[k], it.after(d))
                wait(pe, *freed(pick_out, k, 2, it, d))
                pe.matmul(pick_ps[k % 2][:, 0:P], onehot[:, k, :], same[:, k % 4, :], start=True, stop=True)\
                    .then_inc(picked[k], 1)

            def combine(it, k, low, high):
                wait(pe, pick_out[k], it.after())
                wait(pe, *freed(comb_out, k, 2, it))
                pe.matmul(comb_ps[k % 2][:, 0:ROW], pick[:, k % 4, 0, :], x_tab[:, bass.ds(low, 1), :],
                          start=True, stop=False)
                pe.matmul(comb_ps[k % 2][:, 0:ROW], pick[:, k % 4, 1, :], x_tab[:, bass.ds(high, 1), :],
                          start=False, stop=True).then_inc(combined[k], 1)

            def sums(it, k):
                wait(pe, gathered[k], it.after(0, 16))
                wait(pe, *freed(sum_added, k, 1, it))
                pe.matmul(sum_ps[:, 0:ROW], onehot[:, k, :], xs[:, k, :], start=True, stop=True)\
                    .then_inc(summed[k], 1)

            def turn_curvature(it, j):
                wait(pe, curv_in[j], it.after(0, 16))
                wait(pe, *freed(curv_biased, j, 1, it))
                for u in range(QUAD):
                    ins = pe.transpose(curv_ps[:, u, :], curv[:, j, u, :], sh.ident[:])
                ins.then_inc(curv_turned[j], 1)

            def score_curvature(it, j):
                wait(pe, curv_copied[j], it.after())
                for u in range(QUAD):
                    ins = pe.matmul(curv_ps[:, 0, u * HEADS:(u + 1) * HEADS], curv_t[:, u, :], wc[:], start=True,
                                    stop=True)
                ins.then_inc(curv_scored[j], 1)

            def passes(it, last=False):
                for k in range(U):
                    if k % QUAD == 0:
                        windows = load_windows(nc, pe, sh, it, k)
                    combine(it, k, *windows[k % QUAD])
                    sums(it, k)
                    advance(it, last, k, ((picks, 2), (spread, 5)))
                    if k % QUAD == 0:
                        turn_curvature(it, k // QUAD)
                    if k % QUAD == 2:
                        score_curvature(it, k // QUAD)
            prepare(pe, spread, 5)
            prepare(pe, picks, 2)
            run_passes(pe, passes, dmas=(1,))

        @block.scalar
        def _(act):
            def pick_evac(it, d, k):
                wait(act, picked[k], it.after(d))
                wait(act, *freed(combined, k, 4, it, d))
                act.activation(pick[0:HALF, k % 4, 0, :], pick_ps[k % 2][0:HALF, 0:P], ACT.Copy)
                act.activation(pick[HALF:P, k % 4, 1, :], pick_ps[k % 2][HALF:P, 0:P], ACT.Copy).then_inc(pick_out[k], 1)

            def comb_evac(it, d, k):
                wait(act, combined[k], it.after())
                wait(act, scattered[k], it.before(0, 16))
                act.activation(comb[:, k, :], comb_ps[k % 2][:, 0:ROW], ACT.Copy).then_inc(comb_out[k], 1)

            def keep_rows(it, d, k):
                wait(act, scat_set[k], it.after())
                act.activation(col(sh.scat_cols, it, 0, k), scat_idx[:, k:k + 1], ACT.Copy).then_inc(scat_kept[k], 1)

            def curv_evac(it, j):
                wait(act, curv_turned[j], it.after())
                wait(act, *freed(curv_scored, j, 1, it))
                act.activation(curv_t[:], curv_ps[:], ACT.Copy).then_inc(curv_copied[j], 1)

            def passes(it, last=False):
                for k in range(U):
                    advance(it, last, k, ((pick_evac, 1), (comb_evac, 0), (keep_rows, 0)))
                    if k % QUAD == 1:
                        curv_evac(it, k // QUAD)
            act.wait_ge(ready, 7)
            prepare(act, pick_evac, 1)
            run_passes(act, passes, dmas=(0,))

        @block.vector
        def _(dve):
            dve.memset(x_tab[:, :, D:D + 1], 1.0).then_inc(ready, 1)
            dve.memset(x_tab[:, :, D + 1:ROW], 0.0).then_inc(ready, 1)
            dve.memset(xs[:, :, D:D + 1], 1.0).then_inc(ready, 1)
            dve.memset(xs[:, :, D + 1:ROW], 0.0).then_inc(ready, 1)
            dve.memset(pick[:], 0.0).then_inc(ready, 1)
            dve.memset(in_sum[:], 0.0).then_inc(ready, 1)
            dve.wait_ge(ready, 7)
            dve.wait_ge(loaded, 16 * (2 + BLOCKS // LOAD_BLOCKS))

            def index(it, d, k):
                wait(dve, gathered[k], it.before(d, 16))
                dve.tensor_scalar(gat_idx[:, k:k + 1], col(sh.src_cols, it, d, k), 0.0, None, ALU.max).then_inc(idx_set[k], 1)
                wait(dve, src_spread[k], it.before(d))
                dve.tensor_scalar(src_slot[:, k:k + 1], col(sh.src_cols, it, d, k), 0.0, None, ALU.max).then_inc(slot_set[k], 1)

            def hot(it, d, k):
                wait(dve, summed[k], it.before(d))
                wait(dve, picked[k], it.before(d))
                dve.tensor_scalar(onehot[:, k, :], sh.iota[:], col(sh.rel_cols, it, d, k), None, ALU.is_equal)\
                    .then_inc(onehot_set[k], 1)

            def match(it, d, k):
                wait(dve, src_spread[k], it.after(d))
                wait(dve, *freed(picked, k, 4, it, d))
                dve.tensor_scalar(same[:, k % 4, :], src_ps[k % 2][:, 0:P], col(sh.src_cols, it, d, k), None,
                                  ALU.is_equal).then_inc(same_set[k], 1)
                wait(dve, trash_set[k], it.before(d))
                wait(dve, *freed(dup_set, k, 2, it, d))
                dve.scalar_tensor_tensor(out=junk[:, k % 2, :], in0=src_ps[k % 2][:, 0:P],
                                         scalar=col(sh.src_cols, it, d, k), in1=below[:], op0=ALU.is_equal,
                                         op1=ALU.mult, accum_out=dups[:, k:k + 1]).then_inc(dup_set[k], 1)

            def rows(it, d, k):
                wait(dve, dup_set[k], it.after(d))
                wait(dve, scat_set[k], it.before(d))
                dve.tensor_scalar(trash_row[:, k:k + 1], dups[:, k:k + 1], 1.0, sh.trash[:], ALU.min, ALU.mult)\
                    .then_inc(trash_set[k], 1)
                wait(dve, trash_set[k], it.after(d))
                wait(dve, scattered[k], it.before(d, 16))
                wait(dve, scat_kept[k], it.before(d))
                dve.tensor_scalar(scat_idx[:, k:k + 1], trash_row[:, k:k + 1], col(sh.src_cols, it, d, k), None,
                                  ALU.max).then_inc(scat_set[k], 1)

            def add(it, k, low, high):
                wait(dve, summed[k], it.after())
                wait(dve, *freed(sum_added, k, 1, it))
                to = in_sum[0:HALF, bass.ds(low, 1), :].rearrange("p o c -> p (o c)")
                dve.tensor_tensor(to, to, sum_ps[0:HALF, 0:ROW], ALU.add)
                to = in_sum[HALF:P, bass.ds(high, 1), :].rearrange("p o c -> p (o c)")
                dve.tensor_tensor(to, to, sum_ps[HALF:P, 0:ROW], ALU.add).then_inc(sum_added[k], 1)

            def bias(it, j):
                wait(dve, curv_scored[j], it.after())
                wait(dve, curv_stored[j], it.before(0, 16))
                dve.tensor_tensor(curv_s[:, j], curv_ps[:, 0, 0:QUAD * HEADS].rearrange("p (u h) -> p u h", h=HEADS),
                                  bc[:], ALU.add).then_inc(curv_biased[j], 1)

            def passes(it, last=False):
                for k in range(U):
                    if k % QUAD == 0:
                        windows = load_windows(nc, dve, sh, it, k)
                    advance(it, last, k, ((index, 6), (hot, 4), (match, 4), (rows, 2)))
                    add(it, k, *windows[k % QUAD])
                    if k % QUAD == 3:
                        bias(it, k // QUAD)
            for stage, lead in ((index, 6), (hot, 4), (match, 4), (rows, 2)):
                prepare(dve, stage, lead)
            run_passes(dve, passes, dmas=(0, 1))


NODE_PASSES = BLOCKS // 2


def stage_first_nodes(nc, sh, w, x_tab, in_sum):
    with Scope(nc, "n_") as sc:
        out_parts = sc.sb("out_parts", [P, 2, TABS, ROW])
        pair_sum = sc.sb("pair_sum", [P, 2, 2, ROW])
        out_sum = sc.sb("out_sum", [P, 2, ROW])
        count = sc.sb("count", [P, 2, 2])
        inv = sc.sb("inv", [P, 2, 2])
        terms = sc.sb("terms", [P, 2, 3, D])
        turned = sc.sb("turned", [P, 2, 3, P])
        stats = sc.sb("stats", [P, 2, 2, 6])
        mean_var = sc.sb("mean_var", [P, 2, 2, 2])
        std = sc.sb("std", [P, 2, 2])
        rstd = sc.sb("rstd", [P, 2, 2])
        eps = sc.sb("eps", [P, 1])
        normed = sc.sb("normed", [P, 2, D])
        normed_t = sc.sb("normed_t", [P, 2, P])
        q_out = sc.sb("q_out", [P, 2, D])
        kvy_out = sc.sb("kvy_out", [P, 2, 3, D])
        w_first = sc.sb("w_first", [P, 3, D])
        b_first = sc.sb("b_first", [1, 3, D])
        b_part = sc.sb("b_part", [1, D])
        b_all = sc.sb("b_all", [1, D])
        w_qkv = sc.sb("w_qkv", [P, 3, D])
        w_qkv_g = sc.sb("w_qkv_g", [P, 3, D])
        b_qkv = sc.sb("b_qkv", [1, 3, D])
        b_qkv_g = sc.sb("b_qkv_g", [1, 3, D])
        g1 = sc.sb("g1", [P, 1])
        be1 = sc.sb("be1", [P, 1])
        ones = sc.sb("ones", [1, P])
        turn_ps = [sc.ps(f"turn_ps{i}", (P, 4, P)) for i in range(2)]
        out_ps = [sc.ps(f"out_ps{i}") for i in range(2)]
        norm_ps = [sc.ps(f"norm_ps{i}") for i in range(2)]
        qkv_ps = [sc.ps(f"qkv_ps{i}") for i in range(2)]

        weights, ready, bias_made, bias_kept, bias_half, aggregated = (sc.sem(n) for n in (
            "weights", "ready", "bias_made", "bias_kept", "bias_half", "aggregated"))
        (parts_in, paired, summed, x_copied, in_count, counted, inverted, in_mean, out_mean, turned_ps, turned_sb,
         first_out, stat1, agg1, std1, rstd1, y_out, stat2, agg2, std2, rstd2, norm_out, norm_turned, norm_t_out, qkv_out,
         q_copied, kv_copied, q_stored, kvy_stored) = (sc.sem_each(n, 2) for n in (
             "parts_in", "paired", "summed", "x_copied", "in_count", "counted", "inverted", "in_mean", "out_mean",
             "turned_ps", "turned_sb", "first_out", "stat1", "agg1", "std1", "rstd1", "y_out", "stat2", "agg2", "std2", "rstd2",
             "norm_out", "norm_turned", "norm_t_out", "qkv_out", "q_copied", "kv_copied", "q_stored", "kvy_stored"))
        block = sc.enter_context(nc.Block())
        n_weights = 16 * 14
        n_ready = 4

        def row(name):
            return w[name].rearrange("(o c) -> o c", o=1)

        def column(name):
            return w[name].rearrange("(c o) -> c o", o=1)

        @block.sync
        def _(sp):
            for i, n in enumerate(("s2d", "d2s", "self")):
                sp.dma_start(w_first[:, i, :], w["L0_gnn_W_" + n]).then_inc(weights, 16)
                sp.dma_start(b_first[:, i, :], row("L0_gnn_b_" + n)).then_inc(weights, 16)
            for i, n in enumerate("qkv"):
                sp.dma_start(w_qkv[:, i, :], w["L1_gnn_W" + n]).then_inc(weights, 16)
                sp.dma_start(b_qkv[:, i, :], row("L1_gnn_b" + n)).then_inc(weights, 16)
            sp.dma_start(g1[:], column("L1_gnn_g1")).then_inc(weights, 16)
            sp.dma_start(be1[:], column("L1_gnn_be1")).then_inc(weights, 16)

            def front(it, d):
                for s in range(2):
                    wait(sp, summed[s], it.before(d))
                    for t in range(TABS):
                        sp.dma_start(out_parts[:, s, t, :], sh.sum_tabs[t][block_at(it, s, d, P), :])\
                            .then_inc(parts_in[s], 16)

            def back(it):
                for s in range(2):
                    wait(sp, q_copied[s], it.after())
                    sp.dma_start(sh.q_tab[block_at(it, s, 0, P), :], q_out[:, s, :]).then_inc(q_stored[s], 16)
                    wait(sp, kv_copied[s], it.after())
                    wait(sp, y_out[s], it.after())
                    at = block_at(it, s)
                    sp.dma_start(sh.kvy[:, at].rearrange("p o i c -> p (o i c)"),
                                 kvy_out[:, s].rearrange("p i c -> p (i c)")).then_inc(kvy_stored[s], 16)
            run_skewed(sp, front, back, NODE_PASSES)
            for s in range(2):
                sp.wait_ge(q_stored[s], 16 * NODE_PASSES)
                sp.wait_ge(kvy_stored[s], 16 * NODE_PASSES)

        @block.gpsimd
        def _(pool):
            def front(it, d):
                for s in range(2):
                    wait(pool, parts_in[s], it.after(d, 16 * TABS))
                    wait(pool, summed[s], it.before(d))
                    pool.tensor_tensor(pair_sum[:, s], out_parts[:, s, 0:2, :], out_parts[:, s, 2:4, :], ALU.add)\
                        .then_inc(paired[s], 1)
                    wait(pool, turned_ps[s], it.before(d))
                    wait(pool, first_out[s], it.before(d))
                    pool.tensor_copy(terms[:, s, 2, :], x_tab[:, block_at(it, s, d), 0:D]
                                     .rearrange("p o c -> p (o c)")).then_inc(x_copied[s], 1)
                    wait(pool, paired[s], it.after(d))
                    wait(pool, out_mean[s], it.before(d))
                    pool.tensor_tensor(out_sum[:, s], pair_sum[:, s, 0, :], pair_sum[:, s, 1, :], ALU.add)\
                        .then_inc(summed[s], 1)

            run_skewed(pool, front, lambda it: None, NODE_PASSES, several=((16 * TABS, 2),))

        @block.tensor
        def _(pe):
            pe.wait_ge(weights, n_weights)
            pe.wait_ge(ready, n_ready)
            pe.matmul(qkv_ps[0][0:1, 0:3 * D], be1[:], w_qkv[:], start=True, stop=False)
            pe.matmul(qkv_ps[0][0:1, 0:3 * D], ones[0:1, 0:1], b_qkv[:], start=False, stop=True)\
                .then_inc(bias_made, 1)
            pe.wait_ge(bias_kept, 1)

            def front(it, d):
                for s in range(2):
                    wait(pe, x_copied[s], it.after(d))
                    wait(pe, in_mean[s], it.after(d))
                    wait(pe, out_mean[s], it.after(d))
                    wait(pe, turned_sb[s], it.before(d))
                    for i in range(3):
                        ins = pe.transpose(turn_ps[s][:, i, :], terms[:, s, i, :], sh.ident[:])
                    ins.then_inc(turned_ps[s], 1)
                for s in range(2):
                    wait(pe, turned_sb[s], it.after(d))
                    wait(pe, y_out[s], it.before(d))
                    for i in range(3):
                        pe.matmul(out_ps[s][:, 0:D], turned[:, s, i, :], w_first[:, i, :], start=(i == 0), stop=False)
                    pe.matmul(out_ps[s][:, 0:D], ones[:], b_all[:], start=False, stop=False)
                    pe.matmul(out_ps[s][:, 0:D], sh.ident[:], terms[:, s, 2, :], start=False, stop=True)\
                        .then_inc(first_out[s], 1)

            def back(it):
                for s in range(2):
                    wait(pe, norm_out[s], it.after())
                    wait(pe, norm_t_out[s], it.before())
                    pe.transpose(norm_ps[s][:, 0:P], normed[:, s, :], sh.ident[:]).then_inc(norm_turned[s], 1)
                for s in range(2):
                    wait(pe, norm_t_out[s], it.after())
                    wait(pe, q_copied[s], it.before())
                    wait(pe, kv_copied[s], it.before())
                    pe.matmul(qkv_ps[s][:, 0:3 * D], normed_t[:, s, :], w_qkv_g[:], start=True, stop=False)
                    pe.matmul(qkv_ps[s][:, 0:3 * D], ones[:], b_qkv_g[:], start=False, stop=True)\
                        .then_inc(qkv_out[s], 1)
            run_skewed(pe, front, back, NODE_PASSES)

        @block.scalar
        def _(act):
            act.wait_ge(ready, n_ready)
            act.wait_ge(bias_made, 1)
            act.activation(b_qkv_g[:].rearrange("o i c -> o (i c)"), qkv_ps[0][0:1, 0:3 * D], ACT.Copy)\
                .then_inc(bias_kept, 1)

            def front(it, d):
                for s in range(2):
                    wait(act, inverted[s], it.after(d))
                    wait(act, turned_ps[s], it.before(d))
                    act.activation(terms[:, s, 0, :], in_sum[:, block_at(it, s, d), 0:D]
                                   .rearrange("p o c -> p (o c)"), ACT.Copy, scale=inv[:, s, 0:1])\
                        .then_inc(in_mean[s], 1)
                    act.activation(terms[:, s, 1, :], out_sum[:, s, 0:D], ACT.Copy, scale=inv[:, s, 1:2])\
                        .then_inc(out_mean[s], 1)
                for s in range(2):
                    wait(act, turned_ps[s], it.after(d))
                    wait(act, first_out[s], it.before(d))
                    act.activation(turned[:, s], turn_ps[s][:, 0:3, :], ACT.Copy).then_inc(turned_sb[s], 1)

            def back(it):
                for i, (agg, root, inverse) in enumerate(((agg1, std1, rstd1), (agg2, std2, rstd2))):
                    for s in range(2):
                        wait(act, agg[s], it.after())
                        wait(act, inverse[s], it.before())
                        act.activation(std[:, s, i:i + 1], mean_var[:, s, i, 1:2], ACT.Sqrt, bias=eps[:])\
                            .then_inc(root[s], 1)
                for s in range(2):
                    wait(act, norm_turned[s], it.after())
                    wait(act, qkv_out[s], it.before())
                    act.activation(normed_t[:, s, :], norm_ps[s][:, 0:P], ACT.Copy).then_inc(norm_t_out[s], 1)
                for s in range(2):
                    wait(act, qkv_out[s], it.after())
                    wait(act, q_stored[s], it.before(0, 16))
                    act.activation(q_out[:, s, :], qkv_ps[s][:, 0:D], ACT.Copy, scale=HEAD_D ** -0.5)\
                        .then_inc(q_copied[s], 1)
                    wait(act, kvy_stored[s], it.before(0, 16))
                    act.activation(kvy_out[:, s, 0:2, :], qkv_ps[s][:, D:3 * D].rearrange("p (i c) -> p i c", c=D),
                                   ACT.Copy).then_inc(kv_copied[s], 1)
            run_skewed(act, front, back, NODE_PASSES, dmas=(0,))

        @block.vector
        def _(dve):
            dve.wait_ge(weights, n_weights)
            dve.memset(ones[:], 1.0).then_inc(ready, 1)
            dve.memset(eps[:], EPS).then_inc(ready, 1)
            dve.tensor_scalar(w_qkv_g[:], w_qkv[:], g1[:], None, ALU.mult).then_inc(ready, 1)
            dve.scalar_tensor_tensor(out=b_part[:], in0=b_first[:, 0, :], scalar=0.5, in1=b_first[:, 2, :],
                                     op0=ALU.mult, op1=ALU.add).then_inc(bias_half, 1)
            dve.wait_ge(bias_half, 1)
            dve.scalar_tensor_tensor(out=b_all[:], in0=b_first[:, 1, :], scalar=0.5, in1=b_part[:],
                                     op0=ALU.mult, op1=ALU.add).then_inc(ready, 1)

            def front(it, d):
                for s in range(2):
                    wait(dve, inverted[s], it.before(d))
                    dve.tensor_scalar(count[:, s, 0:1], in_sum[:, block_at(it, s, d), D:D + 1]
                                      .rearrange("p o c -> p (o c)"), 1.0, 2.0, ALU.max, ALU.mult)\
                        .then_inc(in_count[s], 1)
                    wait(dve, summed[s], it.after(d))
                    dve.tensor_scalar(count[:, s, 1:2], out_sum[:, s, D:D + 1], 1.0, 2.0, ALU.max, ALU.mult)\
                        .then_inc(counted[s], 1)
                for s in range(2):
                    wait(dve, counted[s], it.after(d))
                    wait(dve, out_mean[s], it.before(d))
                    dve.reciprocal(inv[:, s, :], count[:, s, :]).then_inc(inverted[s], 1)

            def back(it):
                for s in range(2):
                    wait(dve, first_out[s], it.after())
                    wait(dve, agg1[s], it.before())
                    dve.bn_stats(stats[:, s, 0, :], out_ps[s][:, 0:D]).then_inc(stat1[s], 1)
                for s in range(2):
                    wait(dve, stat1[s], it.after())
                    wait(dve, y_out[s], it.before())
                    settle(dve, aggregated)
                    dve.bn_aggr(mean_var[:, s, 0, :], stats[:, s, 0, :]).then_inc(agg1[s], 1)
                for s in range(2):
                    wait(dve, std1[s], it.after())
                    wait(dve, y_out[s], it.before())
                    dve.reciprocal(rstd[:, s, 0:1], std[:, s, 0:1]).then_inc(rstd1[s], 1)
                for s in range(2):
                    wait(dve, rstd1[s], it.after())
                    wait(dve, kvy_stored[s], it.before(0, 16))
                    wait(dve, norm_out[s], it.before())
                    dve.tensor_scalar(kvy_out[:, s, 2, :], out_ps[s][:, 0:D], mean_var[:, s, 0, 0:1],
                                      rstd[:, s, 0:1], ALU.subtract, ALU.mult).then_inc(y_out[s], 1)
                for s in range(2):
                    wait(dve, y_out[s], it.after())
                    wait(dve, agg2[s], it.before())
                    dve.bn_stats(stats[:, s, 1, :], kvy_out[:, s, 2, :]).then_inc(stat2[s], 1)
                for s in range(2):
                    wait(dve, stat2[s], it.after())
                    wait(dve, norm_out[s], it.before())
                    settle(dve, aggregated)
                    dve.bn_aggr(mean_var[:, s, 1, :], stats[:, s, 1, :]).then_inc(agg2[s], 1)
                for s in range(2):
                    wait(dve, std2[s], it.after())
                    wait(dve, norm_out[s], it.before())
                    dve.reciprocal(rstd[:, s, 1:2], std[:, s, 1:2]).then_inc(rstd2[s], 1)
                for s in range(2):
                    wait(dve, rstd2[s], it.after())
                    wait(dve, norm_turned[s], it.before())
                    dve.tensor_scalar(normed[:, s, :], kvy_out[:, s, 2, :], mean_var[:, s, 1, 0:1],
                                      rstd[:, s, 1:2], ALU.subtract, ALU.mult).then_inc(norm_out[s], 1)
            run_skewed(dve, front, back, NODE_PASSES, dmas=(0,))


def stage_scores(nc, sh, scores):
    with Scope(nc, "b_") as sc:
        k_tab = sc.sb("k_tab", [P, BLOCKS, D])
        qs = sc.sb("qs", [P, U, D])
        onehot = sc.sb("onehot", [P, U, P])
        onehot_t = sc.sb("onehot_t", [P, 4, 2, P])
        prod = sc.sb("prod", [P, U, D])
        dots = sc.sb("dots", [P, U, HEADS])
        gat_idx = sc.sb("gat_idx", [P, U], I32)
        curv = sc.sb("curv", [P, 2, CHUNK_TILES, HEADS])
        turn_ps = [sc.ps(f"turn_ps{i}") for i in range(2)]
        kd_ps = [sc.ps(f"kd_ps{i}") for i in range(4)]

        loaded, ready, placed, issued = (sc.sem(n) for n in ("loaded", "ready", "placed", "issued"))
        curv_in = sc.sem_each("curv_in", 2)
        (idx_set, gathered, onehot_set, turned, turn_out, expanded, prod_set, dot_set, scored) = (
            sc.sem_each(n) for n in ("idx_set", "gathered", "onehot_set", "turned", "turn_out", "expanded",
                                     "prod_set", "dot_set", "scored"))
        block = sc.enter_context(nc.Block())
        n_loaded = 16 * (BLOCKS // LOAD_BLOCKS)

        @block.sync
        def _(sp):
            for b in range(0, BLOCKS, LOAD_BLOCKS):
                sp.dma_start(k_tab[:, b:b + LOAD_BLOCKS, :], sh.kvy[:, b:b + LOAD_BLOCKS, 0, :]).then_inc(loaded, 16)
            for c in range(CHUNKS):
                if c >= 2:
                    sp.wait_ge(placed, c - 1)
                sp.dma_start(curv[:, c % 2], sh.curv_dram[:, c * CHUNK_TILES:(c + 1) * CHUNK_TILES, :])\
                    .then_inc(curv_in[c % 2], 16)
            sp.wait_ge(loaded, n_loaded)

        @block.gpsimd
        def _(pool):
            def gather(it, d, k):
                wait(pool, idx_set[k], it.after(d))
                wait(pool, prod_set[k], it.before(d))
                settle(pool, issued)
                pool.indirect_dma_start(qs[:, k, :], None, sh.q_tab, bass.IndirectOffsetOnAxis(
                    ap=gat_idx[:, k:k + 1], axis=0)).then_inc(gathered[k], 16)

            def passes(it, last=False):
                for k in range(U):
                    advance(it, last, k, ((gather, 5),))
            prepare(pool, gather, 5)
            run_passes(pool, passes)

        @block.tensor
        def _(pe):
            pe.wait_ge(loaded, n_loaded)

            def turn(it, d, k):
                wait(pe, onehot_set[k], it.after(d))
                wait(pe, *freed(turn_out, k, 2, it, d))
                pe.transpose(turn_ps[k % 2][:, 0:P], onehot[:, k, :], sh.ident[:]).then_inc(turned[k], 1)

            def expand(it, d, k, low, high):
                wait(pe, turn_out[k], it.after(d))
                wait(pe, *freed(prod_set, k, 4, it, d))
                pe.matmul(kd_ps[k % 4][:, 0:D], onehot_t[:, k % 4, 0, :], k_tab[:, bass.ds(low, 1), :], start=True,
                          stop=False)
                pe.matmul(kd_ps[k % 4][:, 0:D], onehot_t[:, k % 4, 1, :], k_tab[:, bass.ds(high, 1), :], start=False,
                          stop=True).then_inc(expanded[k], 1)

            def passes(it, last=False):
                for k in range(U):
                    if k % QUAD == 0:
                        windows = load_windows(nc, pe, sh, it, k + 1)
                    advance(it, last, k, ((turn, 4),
                                          (lambda it, d, kk: expand(it, d, kk, *windows[k % QUAD]), 1)))
            prepare(pe, turn, 4)
            expand(Pass(pe, 0), 0, 0, *load_windows(nc, pe, sh, Pass(pe, 0), 0)[0])
            run_passes(pe, passes)

        @block.scalar
        def _(act):
            for c in range(CHUNKS):
                act.wait_ge(curv_in[c % 2], 16 * (c // 2 + 1))
                act.activation(scores[:].rearrange("p (j c) h -> p j c h", c=CHUNKS)[:, :, c, :], curv[:, c % 2],
                               ACT.Copy).then_inc(placed, 1)
            act.wait_ge(ready, 1)

            def turn_evac(it, d, k):
                wait(act, turned[k], it.after(d))
                wait(act, *freed(expanded, k, 4, it, d))
                act.activation(onehot_t[0:HALF, k % 4, 0, :], turn_ps[k % 2][0:HALF, 0:P], ACT.Copy)
                act.activation(onehot_t[HALF:P, k % 4, 1, :], turn_ps[k % 2][HALF:P, 0:P], ACT.Copy)\
                    .then_inc(turn_out[k], 1)

            def passes(it, last=False):
                for k in range(U):
                    advance(it, last, k, ((turn_evac, 3),))
            prepare(act, turn_evac, 3)
            run_passes(act, passes)

        @block.vector
        def _(dve):
            dve.memset(onehot_t[:], 0.0).then_inc(ready, 1)
            dve.wait_ge(placed, CHUNKS)

            def index(it, d, k):
                wait(dve, gathered[k], it.before(d, 16))
                dve.tensor_scalar(gat_idx[:, k:k + 1], col(sh.src_cols, it, d, k), 0.0, None, ALU.max).then_inc(idx_set[k], 1)

            def hot(it, d, k):
                wait(dve, turned[k], it.before(d))
                dve.tensor_scalar(onehot[:, k, :], sh.iota[:], col(sh.rel_cols, it, d, k), None, ALU.is_equal)\
                    .then_inc(onehot_set[k], 1)

            def product(it, d, k):
                wait(dve, expanded[k], it.after(d))
                wait(dve, gathered[k], it.after(d, 16))
                wait(dve, dot_set[k], it.before(d))
                dve.tensor_tensor(prod[:, k, :], kd_ps[k % 4][:, 0:D], qs[:, k, :], ALU.mult).then_inc(prod_set[k], 1)

            def dot(it, d, k):
                wait(dve, prod_set[k], it.after())
                wait(dve, scored[k], it.before())
                dve.tensor_reduce(dots[:, k, :], prod[:, k, :].rearrange("p (h c) -> p h c", c=HEAD_D), AX.X,
                                  ALU.add).then_inc(dot_set[k], 1)

            def score(it, k, place):
                wait(dve, dot_set[k], it.after())
                to = scores[:, bass.ds(place, 1), :].rearrange("p o h -> p (o h)")
                dve.tensor_tensor(to, to, dots[:, k, :], ALU.add).then_inc(scored[k], 1)

            def passes(it, last=False):
                for k in range(U):
                    if k % QUAD == 0:
                        places = load_places(nc, dve, sh, it, k)
                    advance(it, last, k, ((index, 6), (dot, 0), (hot, 5), (product, 1)))
                    score(it, k, *places[k % QUAD])
            for stage, lead in ((index, 6), (hot, 5), (product, 1)):
                prepare(dve, stage, lead)
            run_passes(dve, passes, dmas=(0, 1, 2))


def stage_softmax(nc, sh, dst, scores):
    with Scope(nc, "m_") as sc:
        PIECES = 4
        WIDTH = CHUNK_EDGES // PIECES
        rows = sc.sb("rows", [P, CHUNK_EDGES + 2])
        keep = sc.sb("keep", [P, CHUNK_EDGES + 1], BF16)
        drop = sc.sb("drop", [P, CHUNK_EDGES + 1], BF16)
        ends = sc.sb("ends", [1, 3, CHUNKS], I32)
        links = sc.sb("links", [1, CHUNKS + 1])
        single = sc.sb("single", [1, CHUNKS])
        go_on = sc.sb("go_on", [1, 2, CHUNKS])
        chain_keep = sc.sb("chain_keep", [1, 2, HEADS, CHUNKS])
        chain_drop = sc.sb("chain_drop", [1, 2, HEADS, CHUNKS])
        chain = sc.sb("chain", [1, HEADS, CHUNKS])
        start_row = sc.sb("start_row", [1, CHUNKS, HEADS])
        start_col = sc.sb("start_col", [P, 1])
        edge_col = sc.sb("edge_col", [P, 1])
        one = sc.sb("one", [1, 1])
        turn_ps = [sc.ps(f"turn_ps{i}", (P, 4, P)) for i in range(6)]
        row_ps, col_ps = sc.ps("row_ps"), sc.ps("col_ps")
        work = scores[:].rearrange("p t h -> p (t h)")

        loaded, ends_in, masks, vec, rows_turned, rows_by_act, rows_by_dve = (sc.sem(n) for n in (
            "loaded", "ends_in", "masks", "vec", "rows_turned", "rows_by_act", "rows_by_dve"))
        edge_turned, start_turned, shifted, exped, back_turned, back_by_act, back_by_dve, divided = (
            sc.sem(n) for n in ("edge_turned", "start_turned", "shifted", "exped", "back_turned", "back_by_act",
                                "back_by_dve", "divided"))
        block = sc.enter_context(nc.Block())
        GROUPS = CHUNK_TILES // 4
        CHAIN_AT = [10 + 8 * i for i in range(4)]
        dst_rows = rows[:].bitcast(I32)

        @block.sync
        def _(sp):
            cut = dst[0:EDGES_PAD].rearrange("(c i) -> c i", i=CHUNK_EDGES)
            cut2 = dst[2:2 + EDGES_PAD].rearrange("(c i) -> c i", i=CHUNK_EDGES)
            for h in range(HEADS):
                to = dst_rows[h::HEADS, :]
                sp.dma_start(to[:, 2:], cut2).then_inc(loaded, 16)
                sp.dma_start(to[:, 0:2], cut[:, 0:2]).then_inc(loaded, 16)
            with nc.allow_non_contiguous_dma(reason="one number of each chunk"):
                for i, (a, at) in enumerate(((cut, 0), (cut, 1), (cut2, CHUNK_EDGES - 2))):
                    sp.dma_start(ends[:, i, :], a[:, at:at + 1].rearrange("c o -> o c")).then_inc(ends_in, 16)
            sp.wait_ge(loaded, 16 * 2 * HEADS)
            sp.wait_ge(ends_in, 48)

        @block.tensor
        def _(pe):
            pe.wait_ge(masks, 2)
            by_column = scores[:].rearrange("p (j c) h -> p j (c h)", c=CHUNKS)
            for g in range(GROUPS):
                if g >= 6:
                    pe.wait_ge((rows_by_act, rows_by_dve)[g % 2], (g - 6) // 2 + 1)
                for u in range(4):
                    ins = pe.transpose(turn_ps[g % 6][:, u, :], by_column[:, 4 * g + u], sh.ident[:])
                ins.then_inc(rows_turned, 1)
            for n in range(4):
                pe.wait_ge(vec, CHAIN_AT[n])
                pe.transpose(row_ps[0:1, 0:P], edge_col[:], sh.ident[:]).then_inc(edge_turned, 1)
                pe.wait_ge(vec, CHAIN_AT[n] + 4)
                pe.matmul(col_ps[:, 0:1], start_row[:].rearrange("o c h -> o (c h)"), one[:], start=True, stop=True)\
                    .then_inc(start_turned, 1)
            for g in range(GROUPS):
                pe.wait_ge(divided, 4 * g // (CHUNK_TILES // PIECES) + 1)
                if (4 * g + 3) // (CHUNK_TILES // PIECES) != 4 * g // (CHUNK_TILES // PIECES):
                    pe.wait_ge(divided, (4 * g + 3) // (CHUNK_TILES // PIECES) + 1)
                if g >= 6:
                    pe.wait_ge((back_by_act, back_by_dve)[g % 2], (g - 6) // 2 + 1)
                for u in range(4):
                    at = (4 * g + u) * P
                    ins = pe.transpose(turn_ps[g % 6][:, u, :], rows[:, at:at + P], sh.ident[:])
                ins.then_inc(back_turned, 1)

        def rows_out(eng, copy, g, done):
            eng.wait_ge(rows_turned, g + 1)
            copy(rows[:, 4 * P * g:4 * P * (g + 1)], turn_ps[g % 6][:].rearrange("p u e -> p (u e)")).then_inc(done, 1)

        def back_out(eng, copy, g, done):
            eng.wait_ge(back_turned, g + 1)
            to = scores[:].rearrange("p (j c) h -> p j (c h)", c=CHUNKS)[:, 4 * g:4 * g + 4]
            copy(to, turn_ps[g % 6][:]).then_inc(done, 1)

        @block.scalar
        def _(act):
            def copy(to, frm):
                return act.activation(to, frm, ACT.Copy)
            for g in range(0, GROUPS, 2):
                rows_out(act, copy, g, rows_by_act)
            for i in range(PIECES):
                part = rows[:, i * WIDTH:(i + 1) * WIDTH]
                act.wait_ge(shifted, i + 1)
                act.activation(part, part, ACT.Exp).then_inc(exped, 1)
            act.wait_ge(divided, PIECES)
            for g in range(0, GROUPS, 2):
                back_out(act, copy, g, back_by_act)

        @block.vector
        def _(dve):
            n = [0]

            def then(ins):
                n[0] += 1
                ins.then_inc(vec, 1)
                dve.wait_ge(vec, n[0])

            dve.wait_ge(loaded, 16 * 2 * HEADS)
            a, b = dst_rows[:, 1:CHUNK_EDGES + 2], dst_rows[:, 0:CHUNK_EDGES + 1]
            dve.tensor_tensor(keep[:], a, b, ALU.is_equal).then_inc(masks, 1)
            dve.wait_ge(masks, 1)
            dve.tensor_scalar(drop[:], keep[:], 1.0, BIG, ALU.subtract, ALU.mult).then_inc(masks, 1)
            dve.wait_ge(ends_in, 48)
            dve.memset(one[:], 1.0)
            then(dve.memset(links[:], 0.0))
            then(dve.tensor_tensor(links[:, 0:CHUNKS], ends[:, 0, :], ends[:, 1, :], ALU.is_equal))
            then(dve.tensor_tensor(single[:], ends[:, 1, :], ends[:, 2, :], ALU.is_equal))
            then(dve.tensor_tensor(go_on[:, 0, :], single[:], links[:, 0:CHUNKS], ALU.mult))
            then(dve.tensor_tensor(go_on[:, 1, :], single[:], links[:, 1:CHUNKS + 1], ALU.mult))
            for i in range(2):
                then(dve.tensor_copy(chain_keep[:, i], go_on[:, i:i + 1, :].to_broadcast([1, HEADS, CHUNKS])))
            then(dve.tensor_scalar(chain_drop[:], chain_keep[:], 1.0, BIG, ALU.subtract, ALU.mult))
            assert n[0] == 8
            for g in range(1, GROUPS, 2):
                rows_out(dve, dve.tensor_copy, g, rows_by_dve)
            dve.wait_ge(rows_by_act, (GROUPS + 1) // 2)
            dve.wait_ge(rows_by_dve, GROUPS // 2)
            dve.wait_ge(masks, 2)
            r = rows[:, 0:CHUNK_EDGES]
            last = CHUNK_EDGES - 1

            def scan(to, frm, back, mask, start, op0, op1):
                if back:
                    return dve.tensor_tensor_scan(to[:, ::-1], mask[:, CHUNK_EDGES:0:-1], frm[:, ::-1], start, op0, op1)
                return dve.tensor_tensor_scan(to, mask[:, 0:CHUNK_EDGES], frm, start, op0, op1)

            def spread(i, frm, back, mask, chain_mask, rest, op0, op1):
                then(scan(work, frm, back, mask, rest, op0, op1))
                at = 0 if back else last
                then(dve.tensor_copy(edge_col[:], work[:, at:at + 1]))
                assert n[0] == CHAIN_AT[i], n[0]
                dve.wait_ge(edge_turned, i + 1)
                ordered = row_ps[0:1, 0:P].rearrange("o (c h) -> o h c", h=HEADS)
                then(dve.tensor_copy(chain[:], ordered))
                flat, m = chain[:].rearrange("o h c -> o (h c)"), chain_mask[:, int(back)].rearrange("o h c -> o (h c)")
                if back:
                    flat, m = flat[:, ::-1], m[:, ::-1]
                then(dve.tensor_tensor_scan(flat, m, flat, rest, op0, op1))
                then(dve.memset(start_row[:], rest))
                if back:
                    then(dve.tensor_copy(start_row[:, 0:CHUNKS - 1, :].rearrange("o c h -> o h c"), chain[:, :, 1:]))
                else:
                    then(dve.tensor_copy(start_row[:, 1:, :].rearrange("o c h -> o h c"), chain[:, :, 0:CHUNKS - 1]))
                dve.wait_ge(start_turned, i + 1)
                then(dve.tensor_copy(start_col[:], col_ps[:, 0:1]))
                then(scan(work, frm, back, mask, start_col[:], op0, op1))
            spread(0, r, False, drop, chain_drop, -BIG, ALU.add, ALU.max)
            spread(1, work, True, drop, chain_drop, -BIG, ALU.add, ALU.max)
            for i in range(PIECES):
                part = slice(i * WIDTH, (i + 1) * WIDTH)
                dve.tensor_tensor(rows[:, part], rows[:, part], work[:, part], ALU.subtract).then_inc(shifted, 1)
            dve.wait_ge(exped, PIECES)
            spread(2, r, False, keep, chain_keep, 0.0, ALU.mult, ALU.add)
            spread(3, work, True, keep, chain_keep, 0.0, ALU.mult, ALU.max)
            then(dve.reciprocal(work, work))
            for i in range(PIECES):
                part = slice(i * WIDTH, (i + 1) * WIDTH)
                dve.tensor_tensor(rows[:, part], rows[:, part], work[:, part], ALU.mult).then_inc(divided, 1)
            dve.wait_ge(divided, PIECES)
            for g in range(1, GROUPS, 2):
                back_out(dve, dve.tensor_copy, g, back_by_dve)


def stage_messages(nc, sh, probs):
    with Scope(nc, "c_") as sc:
        v_tab = sc.sb("v_tab", [P, BLOCKS, D])
        onehot = sc.sb("onehot", [P, U, P])
        onehot_t = sc.sb("onehot_t", [P, 4, 2, P])
        same = sc.sb("same", [P, U, P])
        message = sc.sb("message", [P, U, D])
        comb = sc.sb("comb", [P, U, D])
        scat_idx = sc.sb("scat_idx", [P, U], I32)
        src_slot = sc.sb("src_slot", [P, U])
        src_ps = [sc.ps(f"src_ps{i}") for i in range(2)]
        turn_ps = [sc.ps(f"turn_ps{i}") for i in range(2)]
        vd_ps = [sc.ps(f"vd_ps{i}") for i in range(2)]
        comb_ps = [sc.ps(f"comb_ps{i}") for i in range(2)]

        loaded, ready, issued = (sc.sem(n) for n in ("loaded", "ready", "issued"))
        (idx_set, slot_set, onehot_set, turned, turn_out, src_spread, same_set, expanded, message_set, combined,
         comb_out, scattered) = (sc.sem_each(n) for n in (
             "idx_set", "slot_set", "onehot_set", "turned", "turn_out", "src_spread", "same_set", "expanded",
             "message_set", "combined", "comb_out", "scattered"))
        block = sc.enter_context(nc.Block())
        n_loaded = 16 * (BLOCKS // LOAD_BLOCKS)

        @block.sync
        def _(sp):
            for b in range(0, BLOCKS, LOAD_BLOCKS):
                sp.dma_start(v_tab[:, b:b + LOAD_BLOCKS, :], sh.kvy[:, b:b + LOAD_BLOCKS, 1, :]).then_inc(loaded, 16)
            sp.wait_ge(loaded, n_loaded)

        @block.gpsimd
        def _(pool):
            def scatter(it, d, k):
                wait(pool, idx_set[k], it.after())
                wait(pool, comb_out[k], it.after())
                wait(pool, *freed(scattered, k, TABS, it, 0, 16))
                settle(pool, issued)
                pool.indirect_dma_start(sh.msg_tabs[k % TABS], bass.IndirectOffsetOnAxis(ap=scat_idx[:, k:k + 1], axis=0),
                                        comb[:, k, :], None, compute_op=ALU.add).then_inc(scattered[k], 16)

            def passes(it, last=False):
                for k in range(U):
                    scatter(it, 0, k)
            run_passes(pool, passes, dmas=(0, 1))
            for k in range(U):
                pool.wait_ge(scattered[k], 16 * ITERS)

        @block.tensor
        def _(pe):
            pe.wait_ge(loaded, n_loaded)

            def spread(it, d, k):
                wait(pe, slot_set[k], it.after(d))
                wait(pe, *freed(same_set, k, 2, it, d))
                pe.transpose(src_ps[k % 2][:, 0:P], src_slot[:, k:k + 1].to_broadcast([P, P]), sh.ident[:])\
                    .then_inc(src_spread[k], 1)

            def turn(it, d, k):
                wait(pe, onehot_set[k], it.after(d))
                wait(pe, *freed(turn_out, k, 2, it, d))
                pe.transpose(turn_ps[k % 2][:, 0:P], onehot[:, k, :], sh.ident[:]).then_inc(turned[k], 1)

            def expand(it, d, k, low, high):
                wait(pe, turn_out[k], it.after(d))
                wait(pe, *freed(message_set, k, 2, it, d))
                pe.matmul(vd_ps[k % 2][:, 0:D], onehot_t[:, k % 4, 0, :], v_tab[:, bass.ds(low, 1), :], start=True,
                          stop=False)
                pe.matmul(vd_ps[k % 2][:, 0:D], onehot_t[:, k % 4, 1, :], v_tab[:, bass.ds(high, 1), :],
                          start=False, stop=True).then_inc(expanded[k], 1)

            def combine(it, k):
                wait(pe, same_set[k], it.after())
                wait(pe, message_set[k], it.after())
                wait(pe, *freed(comb_out, k, 2, it))
                pe.matmul(comb_ps[k % 2][:, 0:D], same[:, k, :], message[:, k, :], start=True, stop=True)\
                    .then_inc(combined[k], 1)

            def passes(it, last=False):
                for k in range(U):
                    if k % QUAD == 0:
                        windows = load_windows(nc, pe, sh, it, k + 2)
                    advance(it, last, k, ((turn, 4), (spread, 5),
                                          (lambda it, d, kk: expand(it, d, kk, *windows[k % QUAD]), 2)))
                    combine(it, k)
            prepare(pe, turn, 4)
            prepare(pe, spread, 5)
            windows = load_windows(nc, pe, sh, Pass(pe, 0), 0)
            for k in range(2):
                expand(Pass(pe, 0), 0, k, *windows[k])
            run_passes(pe, passes)

        @block.scalar
        def _(act):
            act.wait_ge(ready, 1)

            def turn_evac(it, d, k):
                wait(act, turned[k], it.after(d))
                wait(act, *freed(expanded, k, 4, it, d))
                act.activation(onehot_t[0:HALF, k % 4, 0, :], turn_ps[k % 2][0:HALF, 0:P], ACT.Copy)
                act.activation(onehot_t[HALF:P, k % 4, 1, :], turn_ps[k % 2][HALF:P, 0:P], ACT.Copy)\
                    .then_inc(turn_out[k], 1)

            def comb_evac(it, d, k):
                wait(act, combined[k], it.after())
                wait(act, scattered[k], it.before(0, 16))
                act.activation(comb[:, k, :], comb_ps[k % 2][:, 0:D], ACT.Copy).then_inc(comb_out[k], 1)

            def passes(it, last=False):
                for k in range(U):
                    advance(it, last, k, ((turn_evac, 3), (comb_evac, 0)))
            prepare(act, turn_evac, 3)
            run_passes(act, passes, dmas=(0,))

        @block.vector
        def _(dve):
            dve.memset(onehot_t[:], 0.0).then_inc(ready, 1)

            def index(it, d, k):
                wait(dve, scattered[k], it.before(d, 16))
                dve.tensor_scalar(scat_idx[:, k:k + 1], col(sh.scat_cols, it, d, k), 0.0, None, ALU.max).then_inc(idx_set[k], 1)

            def slot(it, d, k):
                wait(dve, src_spread[k], it.before(d))
                dve.tensor_scalar(src_slot[:, k:k + 1], col(sh.src_cols, it, d, k), 0.0, None, ALU.max).then_inc(slot_set[k], 1)

            def hot(it, d, k):
                wait(dve, turned[k], it.before(d))
                dve.tensor_scalar(onehot[:, k, :], sh.iota[:], col(sh.rel_cols, it, d, k), None, ALU.is_equal)\
                    .then_inc(onehot_set[k], 1)

            def match(it, d, k):
                wait(dve, src_spread[k], it.after(d))
                wait(dve, combined[k], it.before(d))
                dve.tensor_scalar(same[:, k, :], src_ps[k % 2][:, 0:P], col(sh.src_cols, it, d, k), None,
                                  ALU.is_equal).then_inc(same_set[k], 1)

            def weigh(it, d, k, place):
                wait(dve, expanded[k], it.after(d))
                wait(dve, combined[k], it.before(d))
                p = probs[:, bass.ds(place, 1), :]
                dve.tensor_tensor(message[:, k, :].rearrange("p (h c) -> p h c", c=HEAD_D),
                                  vd_ps[k % 2][:, 0:D].rearrange("p (h c) -> p h c", c=HEAD_D),
                                  p.rearrange("p o h -> p h o").to_broadcast([P, HEADS, HEAD_D]), ALU.mult)\
                    .then_inc(message_set[k], 1)

            def passes(it, last=False):
                for k in range(U):
                    if k % QUAD == 0:
                        places = load_places(nc, dve, sh, it, k + 1)
                    advance(it, last, k, ((index, 3), (slot, 6), (hot, 6), (match, 4),
                                          (lambda it, d, kk: weigh(it, d, kk, *places[k % QUAD]), 1)))
            for stage, lead in ((index, 3), (slot, 6), (hot, 6), (match, 4)):
                prepare(dve, stage, lead)
            weigh(Pass(dve, 0), 0, 0, *load_places(nc, dve, sh, Pass(dve, 0), 0)[0])
            run_passes(dve, passes, dmas=(0, 1))


def stage_last_nodes(nc, sh, w, out):
    with Scope(nc, "f_") as sc:
        msg_parts = sc.sb("msg_parts", [P, 2, TABS, D])
        pair_sum = sc.sb("pair_sum", [P, 2, 2, D])
        msg = sc.sb("msg", [P, 2, D])
        y = sc.sb("y", [P, 2, D])
        msg_t = sc.sb("msg_t", [P, 2, P])
        xy = sc.sb("xy", [P, 2, D])
        stats = sc.sb("stats", [P, 2, 2, 6])
        mean_var = sc.sb("mean_var", [P, 2, 2, 2])
        std = sc.sb("std", [P, 2, 2])
        rstd = sc.sb("rstd", [P, 2, 2])
        eps = sc.sb("eps", [P, 1])
        normed = sc.sb("normed", [P, 2, D])
        normed_t = sc.sb("normed_t", [P, 2, P])
        hidden = sc.sb("hidden", [P, 2, FFC, P])
        result = sc.sb("result", [P, 2, D])
        wo = sc.sb("wo", [P, D])
        w1 = sc.sb("w1", [P, FF])
        w1_g = sc.sb("w1_g", [P, FF])
        w2 = sc.sb("w2", [P, FFC, D])
        bo = sc.sb("bo", [1, D])
        b2 = sc.sb("b2", [1, D])
        b1 = sc.sb("b1", [P, FFC])
        b1_g = sc.sb("b1_g", [P, FFC])
        g2 = sc.sb("g2", [P, 1])
        be2 = sc.sb("be2", [P, 1])
        ones = sc.sb("ones", [1, P])
        turn_ps = [sc.ps(f"turn_ps{i}") for i in range(2)]
        x1_ps = [sc.ps(f"x1_ps{i}") for i in range(2)]
        hid_ps = [sc.ps(f"hid_ps{i}", (P, FFC, P)) for i in range(2)]
        out_ps = [sc.ps(f"out_ps{i}") for i in range(2)]

        weights, ready, bias_made, aggregated = (sc.sem(n) for n in ("weights", "ready", "bias_made", "aggregated"))
        (parts_in, y_in, paired, summed, msg_turned, msg_t_out, attended, xy_out, stat1, agg1, std1, rstd1, norm_out,
         norm_turned, norm_t_out, hid_out, relu_out, final_out, stat2, agg2, std2, rstd2, result_out, stored) = (
             sc.sem_each(n, 2) for n in (
                 "parts_in", "y_in", "paired", "summed", "msg_turned", "msg_t_out", "attended", "xy_out", "stat1",
                 "agg1", "std1", "rstd1", "norm_out", "norm_turned", "norm_t_out", "hid_out", "relu_out", "final_out",
                 "stat2", "agg2", "std2", "rstd2", "result_out", "stored"))
        block = sc.enter_context(nc.Block())
        n_weights = 16 * 8
        n_ready = 4

        @block.sync
        def _(sp):
            sp.dma_start(wo[:], w["L1_gnn_Wo"]).then_inc(weights, 16)
            sp.dma_start(w1[:], w["L1_gnn_W1"]).then_inc(weights, 16)
            sp.dma_start(w2[:], w["L1_gnn_W2"].rearrange("(i f) c -> f i c", f=P)).then_inc(weights, 16)
            for to, n in ((bo, "bo"), (b2, "b2")):
                sp.dma_start(to[:], w["L1_gnn_" + n].rearrange("(o c) -> o c", o=1)).then_inc(weights, 16)
            for to, n in ((g2, "g2"), (be2, "be2")):
                sp.dma_start(to[:], w["L1_gnn_" + n].rearrange("(c o) -> c o", o=1)).then_inc(weights, 16)
            with nc.allow_non_contiguous_dma(reason="a column of each chunk"):
                sp.dma_start(b1[:], w["L1_gnn_b1"].rearrange("(i f) -> f i", f=P)).then_inc(weights, 16)

            def front(it, d):
                for s in range(2):
                    wait(sp, summed[s], it.before(d))
                    for t in range(TABS):
                        sp.dma_start(msg_parts[:, s, t, :], sh.msg_tabs[t][block_at(it, s, d, P), :])\
                            .then_inc(parts_in[s], 16)
                    wait(sp, xy_out[s], it.before(d))
                    sp.dma_start(y[:, s, :], sh.kvy[:, block_at(it, s, d), 2, :].rearrange("p o c -> p (o c)"))\
                        .then_inc(y_in[s], 16)

            def back(it):
                for s in range(2):
                    wait(sp, result_out[s], it.after())
                    last = isinstance(it.q, int) and it.q == NODE_PASSES - 1
                    n = LAST_ROWS if last and s else P
                    b = it.q * (2 * P) + s * P
                    rows = slice(b, b + n) if isinstance(it.q, int) else bass.ds(b, P)
                    sp.dma_start(out[rows, :], result[0:n, s, :]).then_inc(stored[s], 16)
            run_skewed(sp, front, back, NODE_PASSES)
            for s in range(2):
                sp.wait_ge(stored[s], 16 * NODE_PASSES)

        @block.gpsimd
        def _(pool):
            def front(it, d):
                for s in range(2):
                    wait(pool, parts_in[s], it.after(d, 16 * TABS))
                    wait(pool, summed[s], it.before(d))
                    pool.tensor_tensor(pair_sum[:, s], msg_parts[:, s, 0:2, :], msg_parts[:, s, 2:4, :], ALU.add)\
                        .then_inc(paired[s], 1)
                    wait(pool, paired[s], it.after(d))
                    wait(pool, msg_turned[s], it.before(d))
                    pool.tensor_tensor(msg[:, s, :], pair_sum[:, s, 0, :], pair_sum[:, s, 1, :], ALU.add)\
                        .then_inc(summed[s], 1)

            run_skewed(pool, front, lambda it: None, NODE_PASSES, several=((16 * TABS, 2),))

        @block.tensor
        def _(pe):
            pe.wait_ge(weights, n_weights)
            for i in range(FFC):
                ins = pe.matmul(out_ps[0][:, i:i + 1], w1[:, i * P:(i + 1) * P], be2[:], start=True, stop=True)
            ins.then_inc(bias_made, 1)
            pe.wait_ge(ready, n_ready)

            def front(it, d):
                for s in range(2):
                    wait(pe, summed[s], it.after(d))
                    wait(pe, norm_out[s], it.before(d))
                    wait(pe, xy_out[s], it.before(d))
                    pe.transpose(x1_ps[s][:, P:2 * P], msg[:, s, :], sh.ident[:]).then_inc(msg_turned[s], 1)
                for s in range(2):
                    wait(pe, msg_t_out[s], it.after(d))
                    wait(pe, y_in[s], it.after(d, 16))
                    pe.matmul(x1_ps[s][:, 0:D], msg_t[:, s, :], wo[:], start=True, stop=False)
                    pe.matmul(x1_ps[s][:, 0:D], ones[:], bo[:], start=False, stop=False)
                    pe.matmul(x1_ps[s][:, 0:D], sh.ident[:], y[:, s, :], start=False, stop=True)\
                        .then_inc(attended[s], 1)

            def early(it):
                for s in range(2):
                    wait(pe, norm_out[s], it.after())
                    wait(pe, norm_t_out[s], it.before())
                    pe.transpose(turn_ps[s][:, 0:P], normed[:, s, :], sh.ident[:]).then_inc(norm_turned[s], 1)

            def late(it):
                for s in range(2):
                    wait(pe, norm_t_out[s], it.after())
                    wait(pe, relu_out[s], it.before())
                    for i in range(FFC):
                        ins = pe.matmul(hid_ps[s][:, i, :], w1_g[:, i * P:(i + 1) * P], normed_t[:, s, :], start=True,
                                        stop=True)
                    ins.then_inc(hid_out[s], 1)
                for s in range(2):
                    wait(pe, relu_out[s], it.after())
                    wait(pe, result_out[s], it.before())
                    pe.matmul(out_ps[s][:, 0:D], ones[:], b2[:], start=True, stop=False)
                    pe.matmul(out_ps[s][:, 0:D], sh.ident[:], xy[:, s, :], start=False, stop=False)
                    for i in range(FFC):
                        ins = pe.matmul(out_ps[s][:, 0:D], hidden[:, s, i, :], w2[:, i, :], start=False,
                                        stop=(i == FFC - 1))
                    ins.then_inc(final_out[s], 1)
            run_woven(pe, early, front, late, NODE_PASSES, dmas=(2,))

        @block.scalar
        def _(act):
            act.wait_ge(ready, n_ready)

            def front(it, d):
                for s in range(2):
                    wait(act, msg_turned[s], it.after(d))
                    wait(act, attended[s], it.before(d))
                    act.activation(msg_t[:, s, :], x1_ps[s][:, P:2 * P], ACT.Copy).then_inc(msg_t_out[s], 1)

            def roots(it, i, agg, root, inverse):
                for s in range(2):
                    wait(act, agg[s], it.after())
                    wait(act, inverse[s], it.before())
                    act.activation(std[:, s, i:i + 1], mean_var[:, s, i, 1:2], ACT.Sqrt, bias=eps[:])\
                        .then_inc(root[s], 1)

            def early(it):
                roots(it, 0, agg1, std1, rstd1)
                for s in range(2):
                    wait(act, norm_turned[s], it.after())
                    wait(act, hid_out[s], it.before())
                    act.activation(normed_t[:, s, :], turn_ps[s][:, 0:P], ACT.Copy).then_inc(norm_t_out[s], 1)

            def late(it):
                for s in range(2):
                    wait(act, hid_out[s], it.after())
                    wait(act, final_out[s], it.before())
                    for i in range(FFC):
                        ins = act.activation(hidden[:, s, i, :], hid_ps[s][:, i, :], ACT.Relu, bias=b1_g[:, i:i + 1])
                    ins.then_inc(relu_out[s], 1)
                roots(it, 1, agg2, std2, rstd2)
            run_woven(act, early, front, late, NODE_PASSES)

        @block.vector
        def _(dve):
            dve.wait_ge(weights, n_weights)
            dve.memset(ones[:], 1.0).then_inc(ready, 1)
            dve.memset(eps[:], EPS).then_inc(ready, 1)
            dve.tensor_scalar(w1_g[:], w1[:], g2[:], None, ALU.mult).then_inc(ready, 1)
            dve.wait_ge(bias_made, 1)
            dve.tensor_tensor(b1_g[:], out_ps[0][:, 0:FFC], b1[:], ALU.add).then_inc(ready, 1)

            def normalise(it, z, i, stat, agg, root, rs, z_done, spent, to, done):
                for s in range(2):
                    wait(dve, z_done[s], it.after())
                    wait(dve, agg[s], it.before())
                    dve.bn_stats(stats[:, s, i, :], z(s)).then_inc(stat[s], 1)
                for s in range(2):
                    wait(dve, stat[s], it.after())
                    wait(dve, done[s], it.before())
                    settle(dve, aggregated)
                    dve.bn_aggr(mean_var[:, s, i, :], stats[:, s, i, :]).then_inc(agg[s], 1)
                for s in range(2):
                    wait(dve, root[s], it.after())
                    wait(dve, done[s], it.before())
                    dve.reciprocal(rstd[:, s, i:i + 1], std[:, s, i:i + 1]).then_inc(rs[s], 1)
                for s in range(2):
                    wait(dve, rs[s], it.after())
                    wait(dve, *spent(s))
                    dve.tensor_scalar(to(s), z(s), mean_var[:, s, i, 0:1], rstd[:, s, i:i + 1], ALU.subtract,
                                      ALU.mult).then_inc(done[s], 1)

            def back(it):
                for s in range(2):
                    wait(dve, attended[s], it.after())
                    wait(dve, final_out[s], it.before())
                    dve.tensor_tensor(xy[:, s, :], x1_ps[s][:, 0:D], y[:, s, :], ALU.add).then_inc(xy_out[s], 1)
                normalise(it, lambda s: x1_ps[s][:, 0:D], 0, stat1, agg1, std1, rstd1, attended,
                          lambda s: (norm_turned[s], it.before()), lambda s: normed[:, s, :], norm_out)
                normalise(it, lambda s: out_ps[s][:, 0:D], 1, stat2, agg2, std2, rstd2, final_out,
                          lambda s: (stored[s], it.before(0, 16)), lambda s: result[:, s, :], result_out)
            run_skewed(dve, lambda it, d: None, back, NODE_PASSES, dmas=(0,))


class General:

    def __init__(self, nc, sc, src, dst):
        self.nc = nc
        self.nodes = (src.rearrange("t e -> (t e)"), dst[1:1 + EDGES_PAD])
        self.index = sc.sb("index", [P, 2], I32)
        self.index_f = sc.sb("index_f", [P, 2])
        self.in_block = sc.sb("in_block", [P, 1], I32)
        self.block_no = sc.sb("block_no", [P, 1], I32)
        self.kvy_row = sc.sb("kvy_row", [P, 1], I32)
        self.same = sc.sb("same", [P, 2, P])
        self.index_in = sc.sem_each("index_in", 2)
        self.cast, self.split, self.row_set, self.same_set, self.spread_set, self.issued = (
            sc.sem(n) for n in ("cast", "split", "row_set", "same_set", "spread_set", "issued"))

    def load(self, sp, it):
        for i in range(2):
            at = it.q * P
            rows = self.nodes[i][slice(at, at + P) if isinstance(it.q, int) else bass.ds(at, P)]
            with self.nc.allow_non_contiguous_dma(reason="an index each partition"):
                sp.dma_start(self.index[:, i:i + 1], rows.rearrange("(p o) -> p o", o=1)).then_inc(self.index_in[i], 16)

    def wait_index(self, eng, it):
        for i in range(2):
            wait(eng, self.index_in[i], it.after(0, 16))

    def floats(self, dve, it):
        self.wait_index(dve, it)
        dve.tensor_scalar(self.index_f[:], self.index[:], 0.0, None, ALU.max).then_inc(self.cast, 1)

    def kvy_rows(self, dve, it):
        dve.tensor_scalar(self.in_block[:], self.index[:, 1:2], P - 1, None, ALU.bitwise_and).then_inc(self.split, 1)
        dve.tensor_scalar(self.block_no[:], self.index[:, 1:2], 7, None, ALU.arith_shift_right).then_inc(self.split, 1)
        wait(dve, self.split, it.after(0, 2))
        dve.scalar_tensor_tensor(out=self.kvy_row[:], in0=self.in_block[:], scalar=float(BLOCKS), in1=self.block_no[:],
                                 op0=ALU.mult, op1=ALU.add).then_inc(self.row_set, 1)

    def spread(self, pe, sh, it, ps):
        wait(pe, self.cast, it.after())
        for i in range(2):
            ins = pe.transpose(ps[:, i * P:(i + 1) * P], self.index_f[:, i:i + 1].to_broadcast([P, P]), sh.ident[:])
        ins.then_inc(self.spread_set, 1)

    def masks(self, dve, it, ps):
        wait(dve, self.spread_set, it.after())
        for i in range(2):
            ins = dve.tensor_scalar(self.same[:, i, :], ps[:, i * P:(i + 1) * P], self.index_f[:, i:i + 1], None,
                                    ALU.is_equal)
        ins.then_inc(self.same_set, 1)

    def gather(self, pool, to, table, i, done):
        at = self.kvy_row[:] if i == 2 else self.index[:, i:i + 1]
        pool.indirect_dma_start(to, None, table, bass.IndirectOffsetOnAxis(ap=at, axis=0)).then_inc(done, 16)

    def scatter(self, pool, table, i, rows, done):
        pool.indirect_dma_start(table, bass.IndirectOffsetOnAxis(ap=self.index[:, i:i + 1], axis=0), rows, None)\
            .then_inc(done, 16)


def run_tiles(eng, tile, until=TILES):
    tile(Pass(eng, 0))
    with eng.Fori(1, until) as q:
        tile(Pass(eng, q, counts=(1,), dmas=(0, 1), several=((2, 1),)))


def fill_table(sp, table, values, done):
    sp.dma_start(table.rearrange("(p b) c -> p b c", p=P),
                 values[:, None, :].to_broadcast([P, table.shape[0] // P, table.shape[1]])).then_inc(done, 16)


def general_aggregate(nc, sh, src, dst, x, edge_attr, w, x_tab, in_sum):
    with Scope(nc, "ga_") as sc:
        gen = General(nc, sc, src, dst)
        feats = sc.sb("feats", [P, 2, ROW])
        old = sc.sb("old", [P, 2, ROW])
        new = sc.sb("new", [P, 2, ROW])
        zeros = sc.sb("zeros", [P, ROW])
        attr = sc.sb("attr", [P, P])
        attr_t = sc.sb("attr_t", [P, P])
        curv = sc.sb("curv", [P, HEADS])
        wc = sc.sb("wc", [P, HEADS])
        bc = sc.sb("bc", [P, HEADS])
        spread_ps, comb_ps, turn_ps, score_ps = (sc.ps(n) for n in ("spread_ps", "comb_ps", "turn_ps", "score_ps"))
        loaded, ready, zeroed, tables_in, combined, new_set, attr_in, turned, turn_out, scored, curv_set, curv_stored = (
            sc.sem(n) for n in ("loaded", "ready", "zeroed", "tables_in", "combined", "new_set", "attr_in", "turned",
                                "turn_out", "scored", "curv_set", "curv_stored"))
        feats_in, old_in, stored = (sc.sem_each(n, 2) for n in ("feats_in", "old_in", "stored"))
        block = sc.enter_context(nc.Block())
        tables = (sh.sum_tabs[0], sh.in_tab)

        @block.sync
        def _(sp):
            sp.dma_start(wc[:], w["L1_gnn_Wc"]).then_inc(loaded, 16)
            sp.dma_start(bc[:], w["L1_gnn_bc"].rearrange("(o h) -> o h", o=1).to_broadcast([P, HEADS]))\
                .then_inc(loaded, 16)
            for b in range(0, BLOCKS, LOAD_BLOCKS):
                sp.dma_start(x_tab[:, b:b + LOAD_BLOCKS, 0:D], x[b * P:(b + LOAD_BLOCKS) * P]
                             .rearrange("(b p) c -> p b c", p=P)).then_inc(loaded, 16)
            sp.wait_ge(loaded, 16 * (2 + BLOCKS // LOAD_BLOCKS))
            sp.wait_ge(ready, 3)
            fill_table(sp, sh.in_tab, zeros, zeroed)
            sp.wait_ge(zeroed, 16)

            def tile(it):
                for i in range(2):
                    wait(sp, stored[i], it.before(0, 16))
                wait(sp, curv_stored, it.before(0, 16))
                gen.load(sp, it)
                at = it.q * P
                if not isinstance(it.q, int):
                    sp.dma_start(attr[:], edge_attr[bass.ds(at, P), :]).then_inc(attr_in, 16)
                elif it.q < FULL_TILES:
                    sp.dma_start(attr[:], edge_attr[at:at + P, :]).then_inc(attr_in, 16)
                else:
                    sp.dma_start(attr[0:LAST_EDGES, :], edge_attr[FULL_TILES * P:N_EDGES, :]).then_inc(attr_in, 16)
                wait(sp, curv_set, it.after())
                t = slice(it.q, it.q + 1) if isinstance(it.q, int) else bass.ds(it.q, 1)
                sp.dma_start(sh.curv_dram[:, t, :].rearrange("p o h -> p (o h)"), curv[:]).then_inc(curv_stored, 16)
            run_tiles(sp, tile, FULL_TILES)
            for q in range(FULL_TILES, TILES):
                tile(Pass(sp, q))
            for i in range(2):
                sp.wait_ge(stored[i], 16 * TILES)
            sp.wait_ge(curv_stored, 16 * TILES)
            for b in range(0, BLOCKS, LOAD_BLOCKS):
                sp.dma_start(in_sum[:, b:b + LOAD_BLOCKS, :], sh.in_tab[b * P:(b + LOAD_BLOCKS) * P, :]
                             .rearrange("(b p) c -> p b c", p=P)).then_inc(tables_in, 16)
            sp.wait_ge(tables_in, 16 * (BLOCKS // LOAD_BLOCKS))

        @block.gpsimd
        def _(pool):
            pool.wait_ge(ready, 3)

            def tile(it):
                gen.wait_index(pool, it)
                settle(pool, gen.issued)
                for i in range(2):
                    gen.gather(pool, feats[:, i, 0:D], x, 1 - i, feats_in[i])
                    gen.gather(pool, old[:, i, :], tables[i], i, old_in[i])
                wait(pool, new_set, it.after())
                settle(pool, gen.issued)
                for i in range(2):
                    gen.scatter(pool, tables[i], i, new[:, i, :], stored[i])
            run_tiles(pool, tile)

        @block.tensor
        def _(pe):
            pe.wait_ge(loaded, 16 * (2 + BLOCKS // LOAD_BLOCKS))

            def tile(it):
                gen.spread(pe, sh, it, spread_ps)
                wait(pe, gen.same_set, it.after())
                for i in range(2):
                    wait(pe, feats_in[i], it.after(0, 16))
                    ins = pe.matmul(comb_ps[:, i * ROW:(i + 1) * ROW], gen.same[:, i, :], feats[:, i, :], start=True,
                                    stop=True)
                ins.then_inc(combined, 1)
                wait(pe, attr_in, it.after(0, 16))
                pe.transpose(turn_ps[:, 0:P], attr[:], sh.ident[:]).then_inc(turned, 1)
                wait(pe, turn_out, it.after())
                pe.matmul(score_ps[:, 0:HEADS], attr_t[:], wc[:], start=True, stop=True).then_inc(scored, 1)
            run_tiles(pe, tile)

        @block.scalar
        def _(act):
            def tile(it):
                wait(act, turned, it.after())
                act.activation(attr_t[:], turn_ps[:, 0:P], ACT.Copy).then_inc(turn_out, 1)
            run_tiles(act, tile)

        @block.vector
        def _(dve):
            dve.memset(zeros[:], 0.0).then_inc(ready, 1)
            dve.memset(feats[:, :, D:D + 1], 1.0).then_inc(ready, 1)
            dve.memset(feats[:, :, D + 1:ROW], 0.0).then_inc(ready, 1)
            dve.wait_ge(loaded, 16 * (2 + BLOCKS // LOAD_BLOCKS))

            def tile(it):
                gen.floats(dve, it)
                gen.masks(dve, it, spread_ps)
                for i in range(2):
                    wait(dve, old_in[i], it.after(0, 16))
                wait(dve, combined, it.after())
                dve.tensor_tensor(new[:], old[:], comb_ps[:, 0:2 * ROW].rearrange("p (i c) -> p i c", c=ROW),
                                  ALU.add).then_inc(new_set, 1)
                wait(dve, scored, it.after())
                dve.tensor_tensor(curv[:], score_ps[:, 0:HEADS], bc[:], ALU.add).then_inc(curv_set, 1)
            run_tiles(dve, tile)


def general_scores(nc, sh, src, dst, scores):
    with Scope(nc, "gb_") as sc:
        gen = General(nc, sc, src, dst)
        curv = sc.sb("curv", [P, HEADS])
        q_row = sc.sb("q_row", [P, D])
        kvy = sc.sb("kvy", [P, 3 * D])
        prod = sc.sb("prod", [P, D])
        dots = sc.sb("dots", [P, HEADS])
        score = sc.sb("score", [P, HEADS])
        drop = sc.sb("drop", [P, P])
        masked = sc.sb("masked", [P, HEADS, P])
        tile_max = sc.sb("tile_max", [P, HEADS])
        old = sc.sb("old", [P, HEADS])
        new = sc.sb("new", [P, HEADS])
        low = sc.sb("low", [P, HEADS])
        spread_ps = sc.ps("spread_ps")
        row_ps = [sc.ps(f"row_ps{i}", (P, 4, P)) for i in range(2)]
        (ready, filled, curv_in, q_in, kvy_in, old_in, prod_set, dot_set, score_set, kept, rows_set, drop_set,
         masked_set, max_set, new_set, stored) = (sc.sem(n) for n in (
             "ready", "filled", "curv_in", "q_in", "kvy_in", "old_in", "prod_set", "dot_set", "score_set", "kept",
             "rows_set", "drop_set", "masked_set", "max_set", "new_set", "stored"))
        block = sc.enter_context(nc.Block())

        @block.sync
        def _(sp):
            sp.wait_ge(ready, 1)
            with nc.allow_non_contiguous_dma(reason="short rows"):
                fill_table(sp, sh.max_tab, low, filled)
            sp.wait_ge(filled, 16)

            def tile(it):
                wait(sp, stored, it.before(0, 16))
                wait(sp, kept, it.before())
                gen.load(sp, it)
                t = slice(it.q, it.q + 1) if isinstance(it.q, int) else bass.ds(it.q, 1)
                sp.dma_start(curv[:], sh.curv_dram[:, t, :].rearrange("p o h -> p (o h)")).then_inc(curv_in, 16)
            run_tiles(sp, tile)

        @block.gpsimd
        def _(pool):
            def tile(it):
                gen.wait_index(pool, it)
                settle(pool, gen.issued)
                gen.gather(pool, q_row[:], sh.q_tab, 0, q_in)
                gen.gather(pool, old[:], sh.max_tab, 1, old_in)
                wait(pool, gen.row_set, it.after())
                settle(pool, gen.issued)
                gen.gather(pool, kvy[:], sh.kvy.rearrange("p b i c -> (p b) (i c)"), 2, kvy_in)
                wait(pool, new_set, it.after())
                settle(pool, gen.issued)
                gen.scatter(pool, sh.max_tab, 1, new[:], stored)
            run_tiles(pool, tile)
            pool.wait_ge(stored, 16 * TILES)

        @block.tensor
        def _(pe):
            def tile(it):
                gen.spread(pe, sh, it, spread_ps)
                wait(pe, score_set, it.after())
                for h in range(HEADS):
                    ins = pe.transpose(row_ps[h // 4][:, h % 4, :], score[:, h:h + 1].to_broadcast([P, P]), sh.ident[:])
                ins.then_inc(rows_set, 1)
            run_tiles(pe, tile)

        @block.vector
        def _(dve):
            dve.memset(low[:], -2 * BIG).then_inc(ready, 1)

            def tile(it):
                gen.floats(dve, it)
                gen.kvy_rows(dve, it)
                gen.masks(dve, it, spread_ps)
                wait(dve, gen.same_set, it.after())
                dve.tensor_scalar(drop[:], gen.same[:, 1, :], 1.0, BIG, ALU.subtract, ALU.mult).then_inc(drop_set, 1)
                wait(dve, q_in, it.after(0, 16))
                wait(dve, kvy_in, it.after(0, 16))
                dve.tensor_tensor(prod[:], q_row[:], kvy[:, 0:D], ALU.mult).then_inc(prod_set, 1)
                wait(dve, prod_set, it.after())
                dve.tensor_reduce(dots[:], prod[:].rearrange("p (h c) -> p h c", c=HEAD_D), AX.X, ALU.add)\
                    .then_inc(dot_set, 1)
                wait(dve, dot_set, it.after())
                wait(dve, curv_in, it.after(0, 16))
                dve.tensor_tensor(score[:], dots[:], curv[:], ALU.add).then_inc(score_set, 1)
                wait(dve, score_set, it.after())
                t = slice(it.q, it.q + 1) if isinstance(it.q, int) else bass.ds(it.q, 1)
                dve.tensor_scalar(scores[:, t, :].rearrange("p o h -> p (o h)"), score[:], 1.0, None, ALU.mult)\
                    .then_inc(kept, 1)
                wait(dve, rows_set, it.after())
                wait(dve, drop_set, it.after())
                for i in range(2):
                    ins = dve.tensor_tensor(masked[:, 4 * i:4 * i + 4, :], row_ps[i][:],
                                            drop[:, None, :].to_broadcast([P, 4, P]), ALU.add)
                ins.then_inc(masked_set, 1)
                wait(dve, masked_set, it.after())
                dve.tensor_reduce(tile_max[:], masked[:], AX.X, ALU.max).then_inc(max_set, 1)
                wait(dve, max_set, it.after())
                wait(dve, old_in, it.after(0, 16))
                dve.tensor_tensor(new[:], old[:], tile_max[:], ALU.max).then_inc(new_set, 1)
            run_tiles(dve, tile)

        @block.scalar
        def _(act):
            act.wait_ge(ready, 1)


def general_sums(nc, sh, src, dst, scores):
    with Scope(nc, "gc_") as sc:
        gen = General(nc, sc, src, dst)
        peak = sc.sb("peak", [P, HEADS])
        shifted = sc.sb("shifted", [P, HEADS])
        weight = sc.sb("weight", [P, HEADS])
        old = sc.sb("old", [P, HEADS])
        new = sc.sb("new", [P, HEADS])
        zeros = sc.sb("zeros", [P, HEADS])
        spread_ps, comb_ps = sc.ps("spread_ps"), sc.ps("comb_ps")
        ready, filled, peak_in, old_in, shift_set, exp_set, kept, combined, new_set, stored = (sc.sem(n) for n in (
            "ready", "filled", "peak_in", "old_in", "shift_set", "exp_set", "kept", "combined", "new_set", "stored"))
        block = sc.enter_context(nc.Block())

        @block.sync
        def _(sp):
            sp.wait_ge(ready, 1)
            with nc.allow_non_contiguous_dma(reason="short rows"):
                fill_table(sp, sh.weight_tab, zeros, filled)
            sp.wait_ge(filled, 16)

            def tile(it):
                wait(sp, stored, it.before(0, 16))
                wait(sp, kept, it.before())
                gen.load(sp, it)
            run_tiles(sp, tile)

        @block.gpsimd
        def _(pool):
            def tile(it):
                gen.wait_index(pool, it)
                settle(pool, gen.issued)
                gen.gather(pool, peak[:], sh.max_tab, 1, peak_in)
                gen.gather(pool, old[:], sh.weight_tab, 1, old_in)
                wait(pool, new_set, it.after())
                settle(pool, gen.issued)
                gen.scatter(pool, sh.weight_tab, 1, new[:], stored)
            run_tiles(pool, tile)
            pool.wait_ge(stored, 16 * TILES)

        @block.tensor
        def _(pe):
            def tile(it):
                gen.spread(pe, sh, it, spread_ps)
                wait(pe, gen.same_set, it.after())
                wait(pe, exp_set, it.after())
                pe.matmul(comb_ps[:, 0:HEADS], gen.same[:, 1, :], weight[:], start=True, stop=True)\
                    .then_inc(combined, 1)
            run_tiles(pe, tile)

        @block.scalar
        def _(act):
            def tile(it):
                wait(act, shift_set, it.after())
                act.activation(weight[:], shifted[:], ACT.Exp).then_inc(exp_set, 1)
            run_tiles(act, tile)

        @block.vector
        def _(dve):
            dve.memset(zeros[:], 0.0).then_inc(ready, 1)

            def tile(it):
                gen.floats(dve, it)
                gen.masks(dve, it, spread_ps)
                t = slice(it.q, it.q + 1) if isinstance(it.q, int) else bass.ds(it.q, 1)
                mine = scores[:, t, :].rearrange("p o h -> p (o h)")
                wait(dve, peak_in, it.after(0, 16))
                dve.tensor_tensor(shifted[:], mine, peak[:], ALU.subtract).then_inc(shift_set, 1)
                wait(dve, exp_set, it.after())
                dve.tensor_scalar(mine, weight[:], 1.0, None, ALU.mult).then_inc(kept, 1)
                wait(dve, old_in, it.after(0, 16))
                wait(dve, combined, it.after())
                dve.tensor_tensor(new[:], old[:], comb_ps[:, 0:HEADS], ALU.add).then_inc(new_set, 1)
            run_tiles(dve, tile)


def general_messages(nc, sh, src, dst, scores):
    with Scope(nc, "gd_") as sc:
        gen = General(nc, sc, src, dst)
        total = sc.sb("total", [P, HEADS])
        inverse = sc.sb("inverse", [P, HEADS])
        prob = sc.sb("prob", [P, HEADS])
        kvy = sc.sb("kvy", [P, 3 * D])
        message = sc.sb("message", [P, D])
        old = sc.sb("old", [P, D])
        new = sc.sb("new", [P, D])
        spread_ps, comb_ps = sc.ps("spread_ps"), sc.ps("comb_ps")
        total_in, kvy_in, old_in, inverted, prob_set, message_set, combined, new_set, stored, done = (
            sc.sem(n) for n in ("total_in", "kvy_in", "old_in", "inverted", "prob_set", "message_set", "combined",
                                "new_set", "stored", "done"))
        block = sc.enter_context(nc.Block())

        @block.sync
        def _(sp):
            def tile(it):
                wait(sp, stored, it.before(0, 16))
                gen.load(sp, it)
            run_tiles(sp, tile)

        @block.gpsimd
        def _(pool):
            def tile(it):
                gen.wait_index(pool, it)
                settle(pool, gen.issued)
                gen.gather(pool, total[:], sh.weight_tab, 1, total_in)
                gen.gather(pool, old[:], sh.msg_tabs[0], 0, old_in)
                wait(pool, gen.row_set, it.after())
                settle(pool, gen.issued)
                gen.gather(pool, kvy[:], sh.kvy.rearrange("p b i c -> (p b) (i c)"), 2, kvy_in)
                wait(pool, new_set, it.after())
                settle(pool, gen.issued)
                gen.scatter(pool, sh.msg_tabs[0], 0, new[:], stored)
            run_tiles(pool, tile)
            pool.wait_ge(stored, 16 * TILES)

        @block.tensor
        def _(pe):
            def tile(it):
                gen.spread(pe, sh, it, spread_ps)
                wait(pe, gen.same_set, it.after())
                wait(pe, message_set, it.after())
                pe.matmul(comb_ps[:, 0:D], gen.same[:, 0, :], message[:], start=True, stop=True).then_inc(combined, 1)
            run_tiles(pe, tile)

        @block.vector
        def _(dve):
            def tile(it):
                gen.floats(dve, it)
                gen.kvy_rows(dve, it)
                gen.masks(dve, it, spread_ps)
                wait(dve, total_in, it.after(0, 16))
                dve.reciprocal(inverse[:], total[:]).then_inc(inverted, 1)
                wait(dve, inverted, it.after())
                t = slice(it.q, it.q + 1) if isinstance(it.q, int) else bass.ds(it.q, 1)
                dve.tensor_tensor(prob[:], scores[:, t, :].rearrange("p o h -> p (o h)"), inverse[:], ALU.mult)\
                    .then_inc(prob_set, 1)
                wait(dve, prob_set, it.after())
                wait(dve, kvy_in, it.after(0, 16))
                dve.tensor_tensor(message[:].rearrange("p (h c) -> p h c", c=HEAD_D),
                                  kvy[:, D:2 * D].rearrange("p (h c) -> p h c", c=HEAD_D),
                                  prob[:, :, None].to_broadcast([P, HEADS, HEAD_D]), ALU.mult)\
                    .then_inc(message_set, 1)
                wait(dve, old_in, it.after(0, 16))
                wait(dve, combined, it.after())
                dve.tensor_tensor(new[:], old[:], comb_ps[:, 0:D], ALU.add).then_inc(new_set, 1)
            run_tiles(dve, tile)

        @block.scalar
        def _(act):
            act.wait_ge(new_set, TILES)


_OUT_SHAPE = (N_NODES, D)


def kernel(**inputs):
    import concourse.bacc as bacc
    from concourse.bass_utils import run_bass_kernel_spmd

    nc = bacc.Bacc("TRN2", target_bir_lowering=False, num_devices=1)
    arrays, aps = {}, {}
    for name, a in inputs.items():
        a = np.ascontiguousarray(a)
        if name == "x":
            a = np.pad(a, ((0, NODES_PAD - N_NODES), (0, 0)))
        elif name == "src":
            a = np.pad(a, (0, EDGES_PAD - N_EDGES), constant_values=NODES_PAD - 1).reshape(TILES, P)
        elif name == "dst":
            a = np.pad(a, (1, EDGES_PAD - N_EDGES + 1), constant_values=(-1, NODES_PAD - 1))
            a[-1] = NODES_PAD
        arrays[name] = a
        aps[name] = nc.dram_tensor(f"{name}", a.shape, mybir.dt.from_np(a.dtype), kind="ExternalInput").ap()
    out = nc.dram_tensor("out", _OUT_SHAPE, F32, kind="ExternalOutput").ap()
    x, src, dst, edge_attr = (aps.pop(n) for n in ("x", "src", "dst", "edge_attr_128"))
    build(nc, x, src, dst, edge_attr, aps, out)
    return run_bass_kernel_spmd(nc, [arrays], core_ids=[0]).results[0]["out"]
```

```python
from contextlib import ExitStack

import numpy as np

import concourse.bass as bass
from concourse import mybir

ALU = mybir.AluOpType
ACT = mybir.ActivationFunctionType
AX = mybir.AxisListType
F32 = mybir.dt.float32
I32 = mybir.dt.int32
BF16 = mybir.dt.bfloat16
I16 = mybir.dt.int16

P = 128
HALF = P // 2
N_NODES = 12500
N_EDGES = 212500
D = 128
HEADS = 8
HEAD_D = D // HEADS
FF = 4 * D
FFC = FF // P
BLOCKS = -(-N_NODES // P)
LAST_ROWS = N_NODES - (BLOCKS - 1) * P
NODES_PAD = BLOCKS * P
CHUNKS = P // HEADS
TILES = 1664
EDGES_PAD = TILES * P
CHUNK_TILES = TILES // CHUNKS
CHUNK_EDGES = CHUNK_TILES * P
FULL_TILES = N_EDGES // P
LAST_EDGES = N_EDGES - FULL_TILES * P
U = 8
QUAD = 4
ITERS = TILES // U
ROW = D + 4
SUM_TABS = 2
MSG_TABS = 4
TAB_ROWS = NODES_PAD + P
LOAD_BLOCKS = 14
BIG = 1.5e38
EPS = 1e-5


class Pass:

    def __init__(self, eng, q, counts=(1, 2), dmas=(), several=()):
        self.eng, self.q = eng, q
        self.known = {(1, 0): q}
        if not isinstance(q, int):
            for d in counts:
                self.known[1, d] = eng.snap(q + d)
            for d in dmas:
                self.known[16, d] = eng.snap((q + d) * 16)
            for times, d in several:
                self.known[times, d] = eng.snap((q + d) * times)

    def before(self, d=0, times=1):
        if times == 1:
            return Uses(self, d)
        return (self.q + d) * times if isinstance(self.q, int) else self.known[times, d]

    def after(self, d=0, times=1):
        return self.before(d + 1, times)

    def counted(self, d, s, n):
        at = d * n + s + 1 - n
        if isinstance(self.q, int):
            return self.q * n + at
        if (n, at) not in self.known_counts():
            self.known_counts()[n, at] = self.eng.snap(self.q * n + at)
        return self.known_counts()[n, at]

    def known_counts(self):
        return self.known.setdefault("counts", {})


class Uses:

    def __init__(self, it, d):
        self.it, self.d = it, d

    def value(self, sem):
        if isinstance(sem, Counted):
            return self.it.counted(self.d, sem.s, sem.n)
        return self.it.q + self.d if isinstance(self.it.q, int) else self.it.known[1, self.d]


class Counted:

    def __init__(self, sem, s, n):
        self.sem, self.s, self.n = sem, s, n


def wait(eng, sem, value):
    if isinstance(value, Uses):
        value = value.value(sem)
    if isinstance(sem, Counted):
        sem = sem.sem
    if not (isinstance(value, int) and value <= 0):
        eng.wait_ge(sem, value)


def settle(eng, counter):
    eng.sem_inc(counter, 1)


def ahead(k, lead):
    return (k + lead) // U, (k + lead) % U


def freed(sems, k, back, it, d=0, times=1):
    n = len(sems)
    return (sems[k - back], it.after(d, times)) if k >= back else (sems[k - back + n], it.before(d, times))


def col(a, it, d, k):
    t = it.q * U + (d * U + k)
    return a[:, t:t + 1] if isinstance(it.q, int) else a[:, bass.ds(t, 1)]


def blocks_at(it, d=0, size=1, s=None):
    b = it.q * (NODE_S * size) + (d * NODE_S + (s or 0)) * size
    n = (NODE_S if s is None else 1) * size
    return slice(b, b + n) if isinstance(it.q, int) else bass.ds(b, n)


def bank_freed(sems, s, it, d=0):
    return (sems[s - 2], it.after(d)) if s >= 2 else (sems[-1], it.before(d))


class Layernorm:

    def __init__(self, sc, tag, n, z, z_done, to, done, spent, times=1):
        self.n, self.z, self.z_done, self.to, self.done = n, z, z_done, to, done
        self.spent, self.times = spent, times
        self.stats, self.mean_var = sc.sb(tag + "stats", [P, n, 6]), sc.sb(tag + "mean_var", [P, n, 2])
        self.std, self.rstd = sc.sb(tag + "std", [P, n]), sc.sb(tag + "rstd", [P, n])
        self.stat = sc.sem_counted(tag + "stat", n)
        self.agg, self.root, self.inverse, self.settled = (
            sc.sem(tag + name) for name in ("agg", "root", "inverse", "settled"))

    def roots(self, act, eps, it, d):
        wait(act, self.agg, it.after(d))
        wait(act, self.inverse, it.before(d))
        act.activation(self.std[:], self.mean_var[:, :, 1], ACT.Sqrt, bias=eps[:]).then_inc(self.root, 1)

    def moments(self, dve, it, d):
        wait(dve, self.agg, it.before(d))
        for s in range(self.n):
            wait(dve, self.z_done[s], it.after(d))
            dve.bn_stats(self.stats[:, s, :], self.z(s)).then_inc(self.stat[s].sem, 1)
        wait(dve, self.done[self.n - 1], it.before(d))
        for s in range(self.n):
            wait(dve, self.stat[s], it.after(d))
            settle(dve, self.settled)
            ins = dve.bn_aggr(self.mean_var[:, s, :], self.stats[:, s, :])
        ins.then_inc(self.agg, 1)

    def rescale(self, dve, it, d):
        wait(dve, self.root, it.after(d))
        dve.reciprocal(self.rstd[:], self.std[:]).then_inc(self.inverse, 1)
        wait(dve, self.inverse, it.after(d))
        wait(dve, self.spent, it.before(d, self.times))
        for s in range(self.n):
            dve.tensor_scalar(self.to(s), self.z(s), self.mean_var[:, s, 0:1], self.rstd[:, s:s + 1], ALU.subtract,
                              ALU.mult).then_inc(self.done[s].sem, 1)


def run_passes(eng, passes, **values):
    passes(Pass(eng, 0))
    with eng.Fori(1, ITERS - 1) as q:
        passes(Pass(eng, q, **values))
    passes(Pass(eng, ITERS - 1), True)


def run_parts(eng, passes, parts, **values):
    most = max(lead for _, lead in parts)

    def each(q, it):
        for part, lead in parts:
            if q is None or 0 <= q + lead < passes:
                part(it, lead if q is None or q >= 0 else lead + q)
    for q in range(-most, 1):
        each(q, Pass(eng, max(q, 0)))
    with eng.Fori(1, passes - most) as q:
        each(None, Pass(eng, q, **values))
    for q in range(passes - most, passes):
        each(q, Pass(eng, q))


def load_steps(nc, eng, table, it, first, each, most):
    t = it.q * U + first
    at = slice(t, t + QUAD) if isinstance(it.q, int) else bass.ds(t, QUAD)
    _, values = nc.values_load_multi_w_load_instructions(
        table[0:1, at, :].rearrange("o t a -> o (t a)"), engines=[eng.engine], min_val=0, max_val=most,
        skip_runtime_bounds_check_because="the table is made in range, whatever the edges")
    return [values[i * each:(i + 1) * each] for i in range(QUAD)]


def load_windows(nc, eng, sh, it, first):
    return load_steps(nc, eng, sh.window, it, first, 2, BLOCKS - 1)


def load_places(nc, eng, sh, it, first):
    return load_steps(nc, eng, sh.place, it, first, 1, TILES - 1)


def prepare(eng, stage, lead):
    for k in range(lead):
        stage(Pass(eng, 0), 0, k)


def advance(it, last, k, stages):
    for stage, lead in stages:
        d, kk = ahead(k, lead)
        if not (last and d):
            stage(it, d, kk)


def dram(nc, name, shape, dt=F32):
    return nc.dram_tensor(name, shape, dt, kind="Internal").ap()


class Scope(ExitStack):

    def __init__(self, nc, tag):
        super().__init__()
        self.nc, self.tag = nc, tag
        self.sems = []

    def __exit__(self, *exc):
        super().__exit__(*exc)
        if self.sems:
            self.nc.clear_and_free_semaphores(self.sems)
            self.nc.all_engine_barrier()

    def sb(self, name, shape, dt=F32):
        return self.enter_context(self.nc.sbuf_tensor(self.tag + name, shape, dt))

    def ps(self, name, shape=(P, 512)):
        return self.enter_context(self.nc.psum_tensor(self.tag + name, list(shape), F32))

    def sem(self, name):
        self.sems.append(self.nc.alloc_semaphore(self.tag + name))
        return self.sems[-1]

    def sem_counted(self, name, n):
        sem = self.sem(name)
        return [Counted(sem, s, n) for s in range(n)]

    def sem_each(self, name, n=U):
        return [self.sem(f"{name}{i}") for i in range(n)]


class Shared:

    def __init__(self, nc, scope):
        self.sum_tabs = [dram(nc, f"sum_tab{i}", (TAB_ROWS, ROW)) for i in range(SUM_TABS)]
        self.msg_tabs = [dram(nc, f"msg_tab{i}", (TAB_ROWS, D)) for i in range(MSG_TABS)]
        self.q_tab = dram(nc, "q_tab", (NODES_PAD, D))
        self.kvy = dram(nc, "kvy", (P, BLOCKS, 3, D))
        self.curv_dram = dram(nc, "curv_dram", (P, TILES, HEADS))
        self.ident = scope.sb("ident", [P, P])
        self.iota = scope.sb("iota", [P, P])
        self.src_cols = scope.sb("src_cols", [P, TILES])
        self.rel_cols = scope.sb("rel_cols", [P, TILES])
        self.scat_cols = scope.sb("scat_cols", [P, TILES], I32)
        self.window = scope.sb("window", [1, TILES + U, 2], I16)
        self.place = scope.sb("place", [1, TILES + U, 1], I16)
        self.regular = scope.sb("regular", [1, 1], I32)
        self.in_tab = dram(nc, "in_tab", (NODES_PAD, ROW))
        self.max_tab = dram(nc, "max_tab", (NODES_PAD, HEADS))
        self.weight_tab = dram(nc, "weight_tab", (NODES_PAD, HEADS))
        self.zeros = scope.sb("zeros", [P, 9 * ROW])
        self.trash = scope.sb("trash", [P, 1])


def zero_tables(sp, sh, tables, zeroed):
    for tab in tables:
        width = tab.shape[1] * 9
        sp.dma_start(tab.rearrange("(p a r) c -> p a (r c)", p=P, r=9),
                     sh.zeros[:, None, 0:width].to_broadcast([P, TAB_ROWS // P // 9, width])).then_inc(zeroed, 16)


def load_regular(nc, sh):
    return nc.values_load(sh.regular[0:1, 0:1], min_val=0, max_val=1,
                          skip_runtime_bounds_check_because="stage_tables makes it 0 or 1")


def build(nc, x, src, dst, edge_attr, w, out):
    with Scope(nc, "") as whole:
        sh = Shared(nc, whole)
        stage_tables(nc, sh, src, dst)
        with Scope(nc, "a_") as sc:
            x_tab = sc.sb("x_tab", [P, BLOCKS, ROW])
            in_sum = sc.sb("in_sum", [P, BLOCKS, ROW])
            with nc.If(load_regular(nc, sh) > 0):
                stage_aggregate(nc, sh, x, edge_attr, w, x_tab, in_sum)
            with nc.Else():
                general_aggregate(nc, sh, src, dst, x, edge_attr, w, x_tab, in_sum)
            stage_first_nodes(nc, sh, w, x_tab, in_sum)
        with Scope(nc, "s_") as sc:
            scores = sc.sb("scores", [P, TILES, HEADS])
            with nc.If(load_regular(nc, sh) > 0):
                stage_scores(nc, sh, scores)
                stage_softmax(nc, sh, dst, scores)
                stage_messages(nc, sh, scores)
            with nc.Else():
                general_scores(nc, sh, src, dst, scores)
                general_sums(nc, sh, src, dst, scores)
                general_messages(nc, sh, src, dst, scores)
        stage_last_nodes(nc, sh, w, out)


def stage_tables(nc, sh, src, dst):
    groups = TILES // P
    with Scope(nc, "t_") as sc:
        src_rows = sc.sb("src_rows", [P, groups, P], I32)
        dst_rows = sc.sb("dst_rows", [P, groups, P], I32)
        dst_before = sc.sb("dst_before", [P, groups, P], I32)
        unsorted = sc.sb("unsorted", [P, groups, P])
        span = sc.sb("span", [P, 2, groups], I32)
        wide = sc.sb("wide", [P, groups])
        faults = sc.sb("faults", [P, 2])
        fault = sc.sb("fault", [P, 1])
        worst = sc.sb("worst", [1, 1])
        src_f = sc.sb("src_f", [P, groups, P])
        rel_i = sc.sb("rel_i", [P, groups, P], I32)
        rel_f = sc.sb("rel_f", [P, groups, P])
        first = sc.sb("first", [1, TILES], I32)
        half = sc.sb("half", [1, TILES], I32)
        half1 = sc.sb("half1", [1, TILES], I32)
        low = sc.sb("low", [1, TILES], I32)
        high = sc.sb("high", [1, TILES], I32)
        place = sc.sb("place", [1, TILES], I32)
        iota_i = sc.sb("iota_i", [P, P], I32)
        trash_i = sc.sb("trash_i", [P, 1], I32)
        ps = [sc.ps(f"turn{i}", (P, 4, P)) for i in range(4)]
        loaded, made, cast, turned, copied, bits, zero_set, zeroed, checks, fault_turned = (sc.sem(n) for n in (
            "loaded", "made", "cast", "turned", "copied", "bits", "zero_set", "zeroed", "checks", "fault_turned"))
        block = sc.enter_context(nc.Block())
        quads = [(a, g0) for a in range(2) for g0 in range(0, groups, 4)]

        @block.sync
        def _(sp):
            sp.dma_start(src_rows[:], src.rearrange("(g p) e -> p g e", p=P)).then_inc(loaded, 16)
            sp.dma_start(dst_rows[:], dst[1:1 + EDGES_PAD].rearrange("(g p e) -> p g e", p=P, e=P)).then_inc(loaded, 16)
            sp.dma_start(dst_before[:], dst[0:EDGES_PAD].rearrange("(g p e) -> p g e", p=P, e=P)).then_inc(loaded, 16)
            with nc.allow_non_contiguous_dma(reason="one number of each tile"):
                sp.dma_start(first[:], dst[1:1 + EDGES_PAD].rearrange("(o t e) -> o t e", o=1, e=P)[:, :, 0])\
                    .then_inc(loaded, 16)
            sp.wait_ge(zero_set, 1)
            zero_tables(sp, sh, sh.sum_tabs, zeroed)
            sp.wait_ge(zeroed, 16 * SUM_TABS)

        @block.gpsimd
        def _(pool):
            pool.memset(sh.ident[:], 0.0).then_inc(made, 1)
            pool.iota(iota_i[:], [[1, P]], base=0, channel_multiplier=0).then_inc(made, 1)
            pool.iota(trash_i[:], [[0, 1]], base=NODES_PAD, channel_multiplier=1).then_inc(made, 1)
            pool.iota(place[:].rearrange("o (c j) -> o c j", c=CHUNKS), [[1, CHUNKS], [CHUNKS, CHUNK_TILES]], base=0,
                      channel_multiplier=0).then_inc(made, 1)
            pool.wait_ge(made, 1)
            pool.affine_select(out=sh.ident[:], in_=sh.ident[:], compare_op=ALU.not_equal, fill=1.0, base=0,
                               pattern=[[-1, P]], channel_multiplier=1).then_inc(made, 1)

        @block.vector
        def _(dve):
            dve.memset(sh.zeros[:], 0.0).then_inc(zero_set, 1)
            dve.wait_ge(loaded, 64)
            dve.tensor_copy(src_f[:], src_rows[:]).then_inc(cast, 1)
            dve.tensor_scalar(rel_i[:], dst_rows[:], P - 1, None, ALU.bitwise_and).then_inc(bits, 1)
            dve.tensor_scalar(half[:], first[:], 6, None, ALU.arith_shift_right).then_inc(bits, 1)
            dve.wait_ge(bits, 1)
            dve.tensor_copy(rel_f[:], rel_i[:]).then_inc(cast, 1)
            dve.wait_ge(bits, 2)

            dve.tensor_scalar(half1[:], half[:], 1, None, ALU.add).then_inc(bits, 1)
            dve.tensor_scalar(high[:], half[:], 1, None, ALU.arith_shift_right).then_inc(bits, 1)
            dve.wait_ge(bits, 3)
            dve.tensor_scalar(low[:], half1[:], 1, None, ALU.arith_shift_right).then_inc(bits, 1)
            dve.wait_ge(bits, 5)
            dve.tensor_scalar(sh.window[:, 0:TILES, 0], low[:], BLOCKS - 1, None, ALU.min)
            dve.tensor_scalar(sh.window[:, 0:TILES, 1], high[:], BLOCKS - 1, None, ALU.min)
            dve.memset(sh.window[:, TILES:, :], 0)
            dve.memset(sh.place[:, TILES:, :], 0)
            dve.wait_ge(made, 5)
            dve.tensor_copy(sh.iota[:], iota_i[:]).then_inc(cast, 1)
            dve.tensor_copy(sh.trash[:], trash_i[:]).then_inc(cast, 1)
            dve.tensor_copy(sh.place[:, 0:TILES, 0], place[:]).then_inc(cast, 1)
            for n, (a, g0) in enumerate(quads):
                m = min(4, groups - g0)
                to = (sh.src_cols, sh.rel_cols)[a]
                dve.wait_ge(turned, n + 1)
                dve.tensor_copy(to[:, g0 * P:(g0 + m) * P].rearrange("p (g t) -> p g t", t=P),
                                ps[n % 4][:, 0:m, :]).then_inc(copied, 1)

            dve.tensor_tensor(unsorted[:], dst_rows[:], dst_before[:], ALU.is_lt).then_inc(checks, 1)
            dve.tensor_scalar(span[:], dst_rows[:, :, 0:P:P - 1].rearrange("p g i -> p i g"), 6, None,
                              ALU.arith_shift_right).then_inc(checks, 1)
            dve.wait_ge(checks, 2)
            dve.tensor_reduce(faults[:, 0:1], unsorted[:], AX.XY, ALU.max).then_inc(checks, 1)
            dve.scalar_tensor_tensor(out=wide[:], in0=span[:, 1, :], scalar=-1.0, in1=span[:, 0, :], op0=ALU.add,
                                     op1=ALU.is_gt).then_inc(checks, 1)
            dve.wait_ge(checks, 4)
            dve.tensor_reduce(faults[:, 1:2], wide[:], AX.X, ALU.max).then_inc(checks, 1)
            dve.wait_ge(checks, 5)
            dve.tensor_tensor(fault[:], faults[:, 0:1], faults[:, 1:2], ALU.max).then_inc(checks, 1)
            dve.wait_ge(fault_turned, 1)
            dve.tensor_reduce(worst[:], ps[0][0:1, 0, :], AX.X, ALU.max).then_inc(checks, 1)
            dve.wait_ge(checks, 7)
            dve.tensor_scalar(sh.regular[:], worst[:], -1.0, 1.0, ALU.mult, ALU.add).then_inc(checks, 1)

        @block.tensor
        def _(pe):
            pe.wait_ge(cast, 2)
            pe.wait_ge(made, 5)
            for n, (a, g0) in enumerate(quads):
                m = min(4, groups - g0)
                if n >= 4:
                    pe.wait_ge(copied, n - 3)
                for j in range(m):
                    ins = pe.transpose(ps[n % 4][:, j, :], (src_f, rel_f)[a][:, g0 + j, :], sh.ident[:])
                ins.then_inc(turned, 1)
            pe.wait_ge(copied, len(quads))
            pe.wait_ge(checks, 6)
            pe.transpose(ps[0][0:1, 0, :], fault[:], sh.ident[:]).then_inc(fault_turned, 1)


def stage_aggregate(nc, sh, x, edge_attr, w, x_tab, in_sum):
    with Scope(nc, "a_") as sc:
        xs = sc.sb("xs", [P, U, ROW])
        onehot = sc.sb("onehot", [P, U, P])
        same = sc.sb("same", [P, 4, P])
        below = sc.sb("below", [P, P])
        junk = sc.sb("junk", [P, 2, P])
        dups = sc.sb("dups", [P, U])
        trash_row = sc.sb("trash_row", [P, U])
        pick = sc.sb("pick", [P, 4, 2, P])
        comb = sc.sb("comb", [P, U, ROW])
        gat_idx = sc.sb("gat_idx", [P, U], I32)
        scat_idx = sc.sb("scat_idx", [P, U], I32)
        src_slot = sc.sb("src_slot", [P, U])
        curv = sc.sb("curv", [P, 2, QUAD, D])
        curv_t = sc.sb("curv_t", [P, QUAD, P])
        curv_s = sc.sb("curv_s", [P, 2, QUAD, HEADS])
        wc = sc.sb("wc", [P, HEADS])
        bc = sc.sb("bc", [P, QUAD, HEADS])

        src_ps = [sc.ps(f"src_ps{i}") for i in range(2)]
        pick_ps = [sc.ps(f"pick_ps{i}") for i in range(2)]
        comb_ps = [sc.ps(f"comb_ps{i}") for i in range(2)]
        sum_ps = sc.ps("sum_ps")
        curv_ps = sc.ps("curv_ps", (P, QUAD, P))

        laid, ready, loaded, issued, zeroed = (sc.sem(n) for n in ("laid", "ready", "loaded", "issued", "zeroed"))
        (idx_set, slot_set, onehot_set, src_spread, same_set, dup_set, trash_set, scat_set, scat_kept, picked,
         pick_out, combined, comb_out, summed, sum_added, gathered, scattered) = (sc.sem_each(n) for n in (
             "idx_set", "slot_set", "onehot_set", "src_spread", "same_set", "dup_set", "trash_set", "scat_set",
             "scat_kept", "picked", "pick_out", "combined", "comb_out", "summed", "sum_added", "gathered",
             "scattered"))
        curv_in, curv_turned, curv_copied, curv_scored, curv_biased, curv_stored = (sc.sem_each(n, 2) for n in (
            "curv_in", "curv_turned", "curv_copied", "curv_scored", "curv_biased", "curv_stored"))
        block = sc.enter_context(nc.Block())

        @block.sync
        def _(sp):
            sp.dma_start(wc[:], w["L1_gnn_Wc"]).then_inc(loaded, 16)
            sp.dma_start(bc[:], w["L1_gnn_bc"].rearrange("(o r h) -> o r h", o=1, r=1).to_broadcast([P, QUAD, HEADS]))\
                .then_inc(loaded, 16)
            for b in range(0, BLOCKS, LOAD_BLOCKS):
                sp.dma_start(x_tab[:, b:b + LOAD_BLOCKS, 0:D], x[b * P:(b + LOAD_BLOCKS) * P]
                             .rearrange("(b p) c -> p b c", p=P)).then_inc(loaded, 16)
            sp.wait_ge(loaded, 16 * (2 + BLOCKS // LOAD_BLOCKS))

            def load(it, d, j):
                wait(sp, curv_turned[j], it.before(d))
                t = it.q * U + (d * U + j * QUAD)
                full = not isinstance(it.q, int) or t + QUAD <= FULL_TILES
                if full:
                    rows = slice(t * P, (t + QUAD) * P) if isinstance(it.q, int) else bass.ds(t * P, QUAD * P)
                    sp.dma_start(curv[:, j], edge_attr[rows, :].rearrange("(u p) c -> p u c", p=P))\
                        .then_inc(curv_in[j], 16)
                else:
                    sp.dma_start(curv[0:LAST_EDGES, j, 0, :], edge_attr[FULL_TILES * P:N_EDGES, :])\
                        .then_inc(curv_in[j], 16)

            def passes(it, last=False):
                for j in range(2):
                    if not last:
                        load(it, 1, j)
                    wait(sp, curv_biased[j], it.after())
                    t = it.q * U + j * QUAD
                    at = slice(t, t + QUAD) if isinstance(it.q, int) else bass.ds(t, QUAD)
                    sp.dma_start(sh.curv_dram[:, at, :], curv_s[:, j]).then_inc(curv_stored[j], 16)
            for j in range(2):
                load(Pass(sp, 0), 0, j)
            zero_tables(sp, sh, sh.msg_tabs, zeroed)
            passes(Pass(sp, 0))
            with sp.Fori(1, ITERS - 2) as q:
                passes(Pass(sp, q))
            passes(Pass(sp, ITERS - 2))
            passes(Pass(sp, ITERS - 1), True)
            for j in range(2):
                sp.wait_ge(curv_stored[j], 16 * ITERS)
            sp.wait_ge(zeroed, 16 * MSG_TABS)

        @block.gpsimd
        def _(pool):
            pool.memset(below[:], 0.0).then_inc(laid, 1)
            pool.wait_ge(laid, 1)
            pool.affine_select(out=below[:], in_=below[:], compare_op=ALU.is_ge, fill=1.0, base=0,
                               pattern=[[1, P]], channel_multiplier=-1).then_inc(ready, 1)

            def gather(it, d, k):
                wait(pool, idx_set[k], it.after(d))
                wait(pool, summed[k], it.before(d))
                settle(pool, issued)
                pool.indirect_dma_start(xs[:, k, 0:D], None, x, bass.IndirectOffsetOnAxis(
                    ap=gat_idx[:, k:k + 1], axis=0)).then_inc(gathered[k], 16)

            def scatter(it, d, k):
                wait(pool, scat_set[k], it.after())
                wait(pool, comb_out[k], it.after())
                wait(pool, *freed(scattered, k, SUM_TABS, it, 0, 16))
                settle(pool, issued)
                pool.indirect_dma_start(sh.sum_tabs[k % SUM_TABS], bass.IndirectOffsetOnAxis(ap=scat_idx[:, k:k + 1], axis=0),
                                        comb[:, k, :], None, compute_op=ALU.add).then_inc(scattered[k], 16)

            def passes(it, last=False):
                for k in range(U):
                    advance(it, last, k, ((gather, 3), (scatter, 0)))
            pool.wait_ge(ready, 7)
            prepare(pool, gather, 3)
            run_passes(pool, passes, dmas=(0, 1))
            for k in range(U):
                pool.wait_ge(scattered[k], 16 * ITERS)

        @block.tensor
        def _(pe):
            pe.wait_ge(loaded, 16 * (2 + BLOCKS // LOAD_BLOCKS))
            pe.wait_ge(ready, 7)

            def spread(it, d, k):
                wait(pe, slot_set[k], it.after(d))
                wait(pe, *freed(dup_set, k, 2, it, d))
                pe.transpose(src_ps[k % 2][:, 0:P], src_slot[:, k:k + 1].to_broadcast([P, P]), sh.ident[:])\
                    .then_inc(src_spread[k], 1)

            def picks(it, d, k):
                wait(pe, same_set[k], it.after(d))
                wait(pe, onehot_set[k], it.after(d))
                wait(pe, *freed(pick_out, k, 2, it, d))
                pe.matmul(pick_ps[k % 2][:, 0:P], onehot[:, k, :], same[:, k % 4, :], start=True, stop=True)\
                    .then_inc(picked[k], 1)

            def combine(it, k, low, high):
                wait(pe, pick_out[k], it.after())
                wait(pe, *freed(comb_out, k, 2, it))
                pe.matmul(comb_ps[k % 2][:, 0:ROW], pick[:, k % 4, 0, :], x_tab[:, bass.ds(low, 1), :],
                          start=True, stop=False)
                pe.matmul(comb_ps[k % 2][:, 0:ROW], pick[:, k % 4, 1, :], x_tab[:, bass.ds(high, 1), :],
                          start=False, stop=True).then_inc(combined[k], 1)

            def sums(it, k):
                wait(pe, gathered[k], it.after(0, 16))
                wait(pe, *freed(sum_added, k, 1, it))
                pe.matmul(sum_ps[:, 0:ROW], onehot[:, k, :], xs[:, k, :], start=True, stop=True)\
                    .then_inc(summed[k], 1)

            def turn_curvature(it, j):
                wait(pe, curv_in[j], it.after(0, 16))
                wait(pe, *freed(curv_biased, j, 1, it))
                for u in range(QUAD):
                    ins = pe.transpose(curv_ps[:, u, :], curv[:, j, u, :], sh.ident[:])
                ins.then_inc(curv_turned[j], 1)

            def score_curvature(it, j):
                wait(pe, curv_copied[j], it.after())
                for u in range(QUAD):
                    ins = pe.matmul(curv_ps[:, 0, u * HEADS:(u + 1) * HEADS], curv_t[:, u, :], wc[:], start=True,
                                    stop=True)
                ins.then_inc(curv_scored[j], 1)

            def passes(it, last=False):
                for k in range(U):
                    if k % QUAD == 0:
                        windows = load_windows(nc, pe, sh, it, k)
                    combine(it, k, *windows[k % QUAD])
                    sums(it, k)
                    advance(it, last, k, ((picks, 2), (spread, 5)))
                    if k % QUAD == 0:
                        turn_curvature(it, k // QUAD)
                    if k % QUAD == 2:
                        score_curvature(it, k // QUAD)
            prepare(pe, spread, 5)
            prepare(pe, picks, 2)
            run_passes(pe, passes, dmas=(1,))

        @block.scalar
        def _(act):
            def pick_evac(it, d, k):
                wait(act, picked[k], it.after(d))
                wait(act, *freed(combined, k, 4, it, d))
                act.activation(pick[0:HALF, k % 4, 0, :], pick_ps[k % 2][0:HALF, 0:P], ACT.Copy)
                act.activation(pick[HALF:P, k % 4, 1, :], pick_ps[k % 2][HALF:P, 0:P], ACT.Copy)\
                    .then_inc(pick_out[k], 1)

            def comb_evac(it, d, k):
                wait(act, combined[k], it.after())
                wait(act, scattered[k], it.before(0, 16))
                act.activation(comb[:, k, :], comb_ps[k % 2][:, 0:ROW], ACT.Copy).then_inc(comb_out[k], 1)

            def keep_rows(it, d, k):
                wait(act, scat_set[k], it.after())
                act.activation(col(sh.scat_cols, it, 0, k), scat_idx[:, k:k + 1], ACT.Copy).then_inc(scat_kept[k], 1)

            def curv_evac(it, j):
                wait(act, curv_turned[j], it.after())
                wait(act, *freed(curv_scored, j, 1, it))
                act.activation(curv_t[:], curv_ps[:], ACT.Copy).then_inc(curv_copied[j], 1)

            def passes(it, last=False):
                for k in range(U):
                    advance(it, last, k, ((pick_evac, 1), (comb_evac, 0), (keep_rows, 0)))
                    if k % QUAD == 1:
                        curv_evac(it, k // QUAD)
            act.wait_ge(ready, 7)
            prepare(act, pick_evac, 1)
            run_passes(act, passes, dmas=(0,))

        @block.vector
        def _(dve):
            dve.memset(x_tab[:, :, D:D + 1], 1.0).then_inc(ready, 1)
            dve.memset(x_tab[:, :, D + 1:ROW], 0.0).then_inc(ready, 1)
            dve.memset(xs[:, :, D:D + 1], 1.0).then_inc(ready, 1)
            dve.memset(xs[:, :, D + 1:ROW], 0.0).then_inc(ready, 1)
            dve.memset(pick[:], 0.0).then_inc(ready, 1)
            dve.memset(in_sum[:], 0.0).then_inc(ready, 1)
            dve.wait_ge(ready, 7)
            dve.wait_ge(loaded, 16 * (2 + BLOCKS // LOAD_BLOCKS))

            def index(it, d, k):
                wait(dve, gathered[k], it.before(d, 16))
                dve.tensor_scalar(gat_idx[:, k:k + 1], col(sh.src_cols, it, d, k), 0.0, None, ALU.max)\
                    .then_inc(idx_set[k], 1)
                wait(dve, src_spread[k], it.before(d))
                dve.tensor_scalar(src_slot[:, k:k + 1], col(sh.src_cols, it, d, k), 0.0, None, ALU.max)\
                    .then_inc(slot_set[k], 1)

            def hot(it, d, k):
                wait(dve, summed[k], it.before(d))
                wait(dve, picked[k], it.before(d))
                dve.tensor_scalar(onehot[:, k, :], sh.iota[:], col(sh.rel_cols, it, d, k), None, ALU.is_equal)\
                    .then_inc(onehot_set[k], 1)

            def match(it, d, k):
                wait(dve, src_spread[k], it.after(d))
                wait(dve, *freed(picked, k, 4, it, d))
                dve.tensor_scalar(same[:, k % 4, :], src_ps[k % 2][:, 0:P], col(sh.src_cols, it, d, k), None,
                                  ALU.is_equal).then_inc(same_set[k], 1)
                wait(dve, trash_set[k], it.before(d))
                wait(dve, *freed(dup_set, k, 2, it, d))
                dve.scalar_tensor_tensor(out=junk[:, k % 2, :], in0=src_ps[k % 2][:, 0:P],
                                         scalar=col(sh.src_cols, it, d, k), in1=below[:], op0=ALU.is_equal,
                                         op1=ALU.mult, accum_out=dups[:, k:k + 1]).then_inc(dup_set[k], 1)

            def rows(it, d, k):
                wait(dve, dup_set[k], it.after(d))
                wait(dve, scat_set[k], it.before(d))
                dve.tensor_scalar(trash_row[:, k:k + 1], dups[:, k:k + 1], 1.0, sh.trash[:], ALU.min, ALU.mult)\
                    .then_inc(trash_set[k], 1)
                wait(dve, trash_set[k], it.after(d))
                wait(dve, scattered[k], it.before(d, 16))
                wait(dve, scat_kept[k], it.before(d))
                dve.tensor_scalar(scat_idx[:, k:k + 1], trash_row[:, k:k + 1], col(sh.src_cols, it, d, k), None,
                                  ALU.max).then_inc(scat_set[k], 1)

            def add(it, k, low, high):
                wait(dve, summed[k], it.after())
                wait(dve, *freed(sum_added, k, 1, it))
                to = in_sum[0:HALF, bass.ds(low, 1), :].rearrange("p o c -> p (o c)")
                dve.tensor_tensor(to, to, sum_ps[0:HALF, 0:ROW], ALU.add)
                to = in_sum[HALF:P, bass.ds(high, 1), :].rearrange("p o c -> p (o c)")
                dve.tensor_tensor(to, to, sum_ps[HALF:P, 0:ROW], ALU.add).then_inc(sum_added[k], 1)

            def bias(it, j):
                wait(dve, curv_scored[j], it.after())
                wait(dve, curv_stored[j], it.before(0, 16))
                dve.tensor_tensor(curv_s[:, j], curv_ps[:, 0, 0:QUAD * HEADS].rearrange("p (u h) -> p u h", h=HEADS),
                                  bc[:], ALU.add).then_inc(curv_biased[j], 1)

            def passes(it, last=False):
                for k in range(U):
                    if k % QUAD == 0:
                        windows = load_windows(nc, dve, sh, it, k)
                    advance(it, last, k, ((index, 6), (hot, 4), (match, 4), (rows, 2)))
                    add(it, k, *windows[k % QUAD])
                    if k % QUAD == 3:
                        bias(it, k // QUAD)
            for stage, lead in ((index, 6), (hot, 4), (match, 4), (rows, 2)):
                prepare(dve, stage, lead)
            run_passes(dve, passes, dmas=(0, 1))


NODE_S = 7
NODE_PASSES = BLOCKS // NODE_S


def stage_first_nodes(nc, sh, w, x_tab, in_sum):
    with Scope(nc, "n_") as sc:
        S = NODE_S
        out_parts = sc.sb("out_parts", [P, SUM_TABS, S, ROW])
        out_sum = sc.sb("out_sum", [P, S, ROW])
        count = sc.sb("count", [P, 2, S])
        inv = sc.sb("inv", [P, 2, S])
        terms = sc.sb("terms", [P, S, 3, D])
        turned = sc.sb("turned", [P, S, 3, P])
        first = sc.sb("first", [P, S, D])
        eps = sc.sb("eps", [P, 1])
        normed = sc.sb("normed", [P, S, D])
        normed_t = sc.sb("normed_t", [P, S, P])
        y_out = sc.sb("y_out", [P, S, D])
        qkv_out = sc.sb("qkv_out", [P, S, 3, D])
        w_first = sc.sb("w_first", [P, 3, D])
        w_res = sc.sb("w_res", [P, D])
        b_first = sc.sb("b_first", [P, 3, D])
        b_part = sc.sb("b_part", [P, D])
        b_all = sc.sb("b_all", [P, D])
        w_qkv = sc.sb("w_qkv", [P, 3, D])
        w_qkv_g = sc.sb("w_qkv_g", [P, 3, D])
        b_qkv = sc.sb("b_qkv", [P, 3, D])
        b_qkv_g = sc.sb("b_qkv_g", [P, 3, D])
        g1 = sc.sb("g1", [P, 1])
        be1 = sc.sb("be1", [P, 1])
        turn_ps = [sc.ps(f"turn_ps{i}", (P, 4, P)) for i in range(2)]
        out_ps = [sc.ps(f"out_ps{i}") for i in range(2)]
        norm_ps = [sc.ps(f"norm_ps{i}") for i in range(2)]
        qkv_ps = [sc.ps(f"qkv_ps{i}") for i in range(2)]

        weights, ready, bias_made, halved = (sc.sem(n) for n in ("weights", "ready", "bias_made", "halved"))
        (parts_in, summed, x_copied, in_count, counted, inverted, biased, q_stored, kv_stored, y_stored) = (
            sc.sem(n) for n in ("parts_in", "summed", "x_copied", "in_count", "counted", "inverted", "biased",
                                "q_stored", "kv_stored", "y_stored"))
        (in_mean, out_mean, turned_ps, turned_sb, first_ps, first_out, y_set, norm_out, norm_turned, norm_t_out,
         qkv_made, qkv_copied) = (sc.sem_counted(n, S) for n in (
             "in_mean", "out_mean", "turned_ps", "turned_sb", "first_ps", "first_out", "y_set", "norm_out",
             "norm_turned", "norm_t_out", "qkv_made", "qkv_copied"))
        norm1 = Layernorm(sc, "norm1_", S, lambda s: first[:, s, :], first_out, lambda s: y_out[:, s, :], y_set,
                          y_stored, 16)
        norm2 = Layernorm(sc, "norm2_", S, lambda s: y_out[:, s, :], y_set, lambda s: normed[:, s, :], norm_out,
                          norm_turned[S - 1])
        block = sc.enter_context(nc.Block())
        n_weights = 16 * 14
        n_ready = 5

        def row(name):
            return w[name].rearrange("(o c) -> o c", o=1).to_broadcast([P, D])

        def column(name):
            return w[name].rearrange("(c o) -> c o", o=1)

        @block.sync
        def _(sp):
            for i, n in enumerate(("s2d", "d2s", "self")):
                sp.dma_start(w_first[:, i, :], w["L0_gnn_W_" + n]).then_inc(weights, 16)
                sp.dma_start(b_first[:, i, :], row("L0_gnn_b_" + n)).then_inc(weights, 16)
            for i, n in enumerate("qkv"):
                sp.dma_start(w_qkv[:, i, :], w["L1_gnn_W" + n]).then_inc(weights, 16)
                sp.dma_start(b_qkv[:, i, :], row("L1_gnn_b" + n)).then_inc(weights, 16)
            sp.dma_start(g1[:], column("L1_gnn_g1")).then_inc(weights, 16)
            sp.dma_start(be1[:], column("L1_gnn_be1")).then_inc(weights, 16)

            def load(it, d):
                wait(sp, summed, it.before(d))
                for t in range(SUM_TABS):
                    sp.dma_start(out_parts[:, t], sh.sum_tabs[t][blocks_at(it, d, P), :]
                                 .rearrange("(s p) c -> p s c", p=P)).then_inc(parts_in, 16)

            def store_y(it, d):
                wait(sp, y_set[S - 1], it.after(d))
                sp.dma_start(sh.kvy[:, blocks_at(it, d), 2, :], y_out[:]).then_inc(y_stored, 16)

            def store_qkv(it, d):
                wait(sp, biased, it.after(d))
                sp.dma_start(sh.q_tab[blocks_at(it, d, P), :].rearrange("(s p) c -> p s c", p=P), qkv_out[:, :, 0, :])\
                    .then_inc(q_stored, 16)
                sp.dma_start(sh.kvy[:, blocks_at(it, d), 0:2, :].rearrange("p s i c -> p s (i c)"),
                             qkv_out[:, :, 1:3, :].rearrange("p s i c -> p s (i c)")).then_inc(kv_stored, 16)
            run_parts(sp, NODE_PASSES, ((load, 4), (store_y, 1), (store_qkv, 0)), counts=(1, 2, 3, 4))
            for stored in (q_stored, kv_stored, y_stored):
                sp.wait_ge(stored, 16 * NODE_PASSES)

        @block.gpsimd
        def _(pool):
            pool.wait_ge(ready, n_ready)

            def add_parts(it, d):
                wait(pool, parts_in, it.after(d, 16 * SUM_TABS))
                wait(pool, out_mean[S - 1], it.before(d))
                wait(pool, counted, it.before(d))
                pool.tensor_tensor(out_sum[:], out_parts[:, 0], out_parts[:, 1], ALU.add).then_inc(summed, 1)

            def copy_x(it, d):
                wait(pool, turned_ps[S - 1], it.before(d))
                pool.tensor_copy(terms[:, :, 2, :], x_tab[:, blocks_at(it, d), 0:D]).then_inc(x_copied, 1)

            def bias(it, d):
                wait(pool, qkv_copied[S - 1], it.after(d))
                rows = qkv_out[:].rearrange("p s i c -> p s (i c)")
                pool.tensor_tensor(rows, rows, b_qkv_g[:, None].rearrange("p o i c -> p o (i c)")
                                   .to_broadcast([P, S, 3 * D]), ALU.add).then_inc(biased, 1)
            run_parts(pool, NODE_PASSES, ((add_parts, 3), (copy_x, 3), (bias, 0)), counts=(1, 2, 3, 4),
                      several=((16 * SUM_TABS, 4),))

        @block.tensor
        def _(pe):
            pe.wait_ge(weights, n_weights)
            pe.matmul(qkv_ps[0][:, 0:3 * D], be1[:].to_broadcast([P, P]), w_qkv[:], start=True, stop=True)\
                .then_inc(bias_made, 1)
            pe.wait_ge(ready, n_ready)

            def turn_terms(it, d):
                wait(pe, x_copied, it.after(d))
                for s in range(S):
                    wait(pe, in_mean[s], it.after(d))
                    wait(pe, out_mean[s], it.after(d))
                    wait(pe, *bank_freed(turned_sb, s, it, d))
                    for i in range(3):
                        ins = pe.transpose(turn_ps[s % 2][:, i, :], terms[:, s, i, :], sh.ident[:])
                    ins.then_inc(turned_ps[s].sem, 1)

            def first_layer(it, d):
                for s in range(S):
                    wait(pe, turned_sb[s], it.after(d))
                    wait(pe, *bank_freed(first_out, s, it, d))
                    for i in range(3):
                        ins = pe.matmul(out_ps[s % 2][:, 0:D], turned[:, s, i, :],
                                        w_first[:, i, :] if i < 2 else w_res[:], start=(i == 0), stop=(i == 2))
                    ins.then_inc(first_ps[s].sem, 1)

            def turn_normed(it, d):
                for s in range(S):
                    wait(pe, norm_out[s], it.after(d))
                    wait(pe, *bank_freed(norm_t_out, s, it, d))
                    pe.transpose(norm_ps[s % 2][:, 0:P], normed[:, s, :], sh.ident[:]).then_inc(norm_turned[s].sem, 1)

            def qkv(it, d):
                for s in range(S):
                    wait(pe, norm_t_out[s], it.after(d))
                    wait(pe, *bank_freed(qkv_copied, s, it, d))
                    pe.matmul(qkv_ps[s % 2][:, 0:3 * D], normed_t[:, s, :], w_qkv_g[:], start=True, stop=True)\
                        .then_inc(qkv_made[s].sem, 1)
            run_parts(pe, NODE_PASSES, ((first_layer, 1), (turn_terms, 2), (qkv, 0), (turn_normed, 1)),
                      counts=(1, 2, 3))

        @block.scalar
        def _(act):
            act.wait_ge(ready, n_ready)

            def means(it, d):
                wait(act, inverted, it.after(d))
                for s in range(S):
                    wait(act, turned_ps[s], it.before(d))
                    act.activation(terms[:, s, 0, :], in_sum[:, blocks_at(it, d, 1, s), 0:D]
                                   .rearrange("p o c -> p (o c)"), ACT.Copy, scale=inv[:, 0, s:s + 1])\
                        .then_inc(in_mean[s].sem, 1)
                    act.activation(terms[:, s, 1, :], out_sum[:, s, 0:D], ACT.Copy, scale=inv[:, 1, s:s + 1])\
                        .then_inc(out_mean[s].sem, 1)

            def terms_out(it, d):
                for s in range(S):
                    wait(act, turned_ps[s], it.after(d))
                    wait(act, first_ps[s], it.before(d))
                    act.activation(turned[:, s], turn_ps[s % 2][:, 0:3, :], ACT.Copy).then_inc(turned_sb[s].sem, 1)

            def qkv_copy(it, d):
                wait(act, q_stored, it.before(d, 16))
                wait(act, kv_stored, it.before(d, 16))
                for s in range(S):
                    wait(act, qkv_made[s], it.after(d))
                    act.activation(qkv_out[:, s].rearrange("p i c -> p (i c)"), qkv_ps[s % 2][:, 0:3 * D], ACT.Copy)\
                        .then_inc(qkv_copied[s].sem, 1)

            def normed_out(it, d):
                for s in range(S):
                    wait(act, norm_turned[s], it.after(d))
                    wait(act, qkv_made[s], it.before(d))
                    act.activation(normed_t[:, s, :], norm_ps[s % 2][:, 0:P], ACT.Copy).then_inc(norm_t_out[s].sem, 1)
            run_parts(act, NODE_PASSES, ((means, 2), (terms_out, 2), (lambda it, d: norm1.roots(act, eps, it, d), 1),
                                         (qkv_copy, 0), (lambda it, d: norm2.roots(act, eps, it, d), 1),
                                         (normed_out, 1)), counts=(1, 2, 3), dmas=(0,))

        @block.vector
        def _(dve):
            dve.wait_ge(weights, n_weights)
            dve.memset(eps[:], EPS).then_inc(ready, 1)
            dve.tensor_tensor(w_res[:], w_first[:, 2, :], sh.ident[:], ALU.add).then_inc(ready, 1)
            dve.scalar_tensor_tensor(out=b_part[:], in0=b_first[:, 0, :], scalar=0.5, in1=b_first[:, 2, :],
                                     op0=ALU.mult, op1=ALU.add).then_inc(halved, 1)
            dve.wait_ge(halved, 1)
            dve.scalar_tensor_tensor(out=b_all[:], in0=b_first[:, 1, :], scalar=0.5, in1=b_part[:],
                                     op0=ALU.mult, op1=ALU.add).then_inc(ready, 1)
            dve.tensor_scalar(w_qkv_g[:, 0, :], w_qkv[:, 0, :], g1[:], HEAD_D ** -0.5, ALU.mult, ALU.mult)
            dve.tensor_scalar(w_qkv_g[:, 1:3, :], w_qkv[:, 1:3, :], g1[:], None, ALU.mult).then_inc(ready, 1)
            dve.wait_ge(bias_made, 1)
            dve.tensor_tensor(b_qkv_g[:].rearrange("p i c -> p (i c)"), qkv_ps[0][:, 0:3 * D],
                              b_qkv[:].rearrange("p i c -> p (i c)"), ALU.add).then_inc(halved, 1)
            dve.wait_ge(halved, 2)
            dve.tensor_scalar(b_qkv_g[:, 0, :], b_qkv_g[:, 0, :], HEAD_D ** -0.5, None, ALU.mult).then_inc(ready, 1)
            dve.wait_ge(ready, n_ready)

            def first_copy(it, d):
                for s in range(S):
                    wait(dve, first_ps[s], it.after(d))
                    wait(dve, y_set[s], it.before(d))
                    dve.tensor_tensor(first[:, s, :], out_ps[s % 2][:, 0:D], b_all[:], ALU.add)\
                        .then_inc(first_out[s].sem, 1)

            def counts(it, d):
                wait(dve, inverted, it.before(d))
                dve.tensor_scalar(count[:, 0], in_sum[:, blocks_at(it, d), D], 1.0, 2.0, ALU.max, ALU.mult)\
                    .then_inc(in_count, 1)
                wait(dve, summed, it.after(d))
                dve.tensor_scalar(count[:, 1], out_sum[:, :, D], 1.0, 2.0, ALU.max, ALU.mult).then_inc(counted, 1)
                wait(dve, in_count, it.after(d))
                wait(dve, counted, it.after(d))
                wait(dve, out_mean[S - 1], it.before(d))
                dve.reciprocal(inv[:], count[:]).then_inc(inverted, 1)

            def norms(it, d):
                norm1.moments(dve, it, d)
                norm1.rescale(dve, it, d)
                wait(dve, norm_out[S - 1], it.before(d))
                norm2.moments(dve, it, d)
                norm2.rescale(dve, it, d)
            run_parts(dve, NODE_PASSES, ((counts, 2), (first_copy, 1), (norms, 1)), counts=(1, 2, 3), dmas=(1,))


def stage_scores(nc, sh, scores):
    with Scope(nc, "b_") as sc:
        k_tab = sc.sb("k_tab", [P, BLOCKS, D])
        qs = sc.sb("qs", [P, U, D])
        onehot = sc.sb("onehot", [P, U, P])
        onehot_t = sc.sb("onehot_t", [P, 4, 2, P])
        prod = sc.sb("prod", [P, U, D])
        gat_idx = sc.sb("gat_idx", [P, U], I32)
        curv = sc.sb("curv", [P, 2, CHUNK_TILES, HEADS])
        turn_ps = [sc.ps(f"turn_ps{i}") for i in range(2)]
        kd_ps = [sc.ps(f"kd_ps{i}") for i in range(4)]

        loaded, ready, placed, issued, settled = (sc.sem(n) for n in (
            "loaded", "ready", "placed", "issued", "settled"))
        curv_in = sc.sem_each("curv_in", 2)
        (idx_set, gathered, onehot_set, turned, turn_out, expanded, prod_set, dot_set) = (
            sc.sem_each(n) for n in ("idx_set", "gathered", "onehot_set", "turned", "turn_out", "expanded",
                                     "prod_set", "dot_set"))
        block = sc.enter_context(nc.Block())
        n_loaded = 16 * (BLOCKS // LOAD_BLOCKS)

        @block.sync
        def _(sp):
            for b in range(0, BLOCKS, LOAD_BLOCKS):
                sp.dma_start(k_tab[:, b:b + LOAD_BLOCKS, :], sh.kvy[:, b:b + LOAD_BLOCKS, 0, :]).then_inc(loaded, 16)
            for c in range(CHUNKS):
                if c >= 2:
                    sp.wait_ge(placed, c - 1)
                sp.dma_start(curv[:, c % 2], sh.curv_dram[:, c * CHUNK_TILES:(c + 1) * CHUNK_TILES, :])\
                    .then_inc(curv_in[c % 2], 16)
            sp.wait_ge(loaded, n_loaded)

        @block.gpsimd
        def _(pool):
            def gather(it, d, k):
                wait(pool, idx_set[k], it.after(d))
                wait(pool, prod_set[k], it.before(d))
                settle(pool, issued)
                pool.indirect_dma_start(qs[:, k, :], None, sh.q_tab, bass.IndirectOffsetOnAxis(
                    ap=gat_idx[:, k:k + 1], axis=0)).then_inc(gathered[k], 16)

            def passes(it, last=False):
                for k in range(U):
                    advance(it, last, k, ((gather, 5),))
            prepare(pool, gather, 5)
            run_passes(pool, passes)

        @block.tensor
        def _(pe):
            pe.wait_ge(loaded, n_loaded)

            def turn(it, d, k):
                wait(pe, onehot_set[k], it.after(d))
                wait(pe, *freed(turn_out, k, 2, it, d))
                pe.transpose(turn_ps[k % 2][:, 0:P], onehot[:, k, :], sh.ident[:]).then_inc(turned[k], 1)

            def expand(it, d, k, low, high):
                wait(pe, turn_out[k], it.after(d))
                wait(pe, *freed(prod_set, k, 4, it, d))
                pe.matmul(kd_ps[k % 4][:, 0:D], onehot_t[:, k % 4, 0, :], k_tab[:, bass.ds(low, 1), :], start=True,
                          stop=False)
                pe.matmul(kd_ps[k % 4][:, 0:D], onehot_t[:, k % 4, 1, :], k_tab[:, bass.ds(high, 1), :], start=False,
                          stop=True).then_inc(expanded[k], 1)

            def passes(it, last=False):
                for k in range(U):
                    if k % QUAD == 0:
                        windows = load_windows(nc, pe, sh, it, k + 2)
                    advance(it, last, k, ((turn, 4),
                                          (lambda it, d, kk: expand(it, d, kk, *windows[k % QUAD]), 2)))
            prepare(pe, turn, 4)
            windows = load_windows(nc, pe, sh, Pass(pe, 0), 0)
            for k in range(2):
                expand(Pass(pe, 0), 0, k, *windows[k])
            run_passes(pe, passes)

        @block.scalar
        def _(act):
            act.wait_ge(ready, 1)

            def turn_evac(it, d, k):
                wait(act, turned[k], it.after(d))
                wait(act, *freed(expanded, k, 4, it, d))
                act.activation(onehot_t[0:HALF, k % 4, 0, :], turn_ps[k % 2][0:HALF, 0:P], ACT.Copy)
                act.activation(onehot_t[HALF:P, k % 4, 1, :], turn_ps[k % 2][HALF:P, 0:P], ACT.Copy)\
                    .then_inc(turn_out[k], 1)

            def passes(it, last=False):
                for k in range(U):
                    advance(it, last, k, ((turn_evac, 3),))
            prepare(act, turn_evac, 3)
            run_passes(act, passes)

        @block.vector
        def _(dve):
            dve.memset(onehot_t[:], 0.0).then_inc(ready, 1)

            def index(it, d, k):
                wait(dve, gathered[k], it.before(d, 16))
                dve.tensor_scalar(gat_idx[:, k:k + 1], col(sh.src_cols, it, d, k), 0.0, None, ALU.max)\
                    .then_inc(idx_set[k], 1)

            def hot(it, d, k):
                wait(dve, turned[k], it.before(d))
                dve.tensor_scalar(onehot[:, k, :], sh.iota[:], col(sh.rel_cols, it, d, k), None, ALU.is_equal)\
                    .then_inc(onehot_set[k], 1)

            def product(it, d, k):
                wait(dve, expanded[k], it.after(d))
                wait(dve, gathered[k], it.after(d, 16))
                wait(dve, dot_set[k], it.before(d))
                dve.tensor_tensor(prod[:, k, :], kd_ps[k % 4][:, 0:D], qs[:, k, :], ALU.mult).then_inc(prod_set[k], 1)

            def dot(it, k, place):
                wait(dve, prod_set[k], it.after())
                settle(dve, settled)
                dve.tensor_reduce(scores[:, bass.ds(place, 1), :].rearrange("p o h -> p (o h)"),
                                  prod[:, k, :].rearrange("p (h c) -> p h c", c=HEAD_D), AX.X,
                                  ALU.add).then_inc(dot_set[k], 1)

            def passes(it, last=False):
                for k in range(U):
                    if k % QUAD == 0:
                        places = load_places(nc, dve, sh, it, k)
                    advance(it, last, k, ((index, 6), (hot, 5)))
                    dot(it, k, *places[k % QUAD])
                    advance(it, last, k, ((product, 2),))
            for stage, lead in ((index, 6), (hot, 5), (product, 2)):
                prepare(dve, stage, lead)
            run_passes(dve, passes, dmas=(0, 1, 2))
            for k in range(U):
                dve.wait_ge(dot_set[k], ITERS)
            for c in range(CHUNKS):
                dve.wait_ge(curv_in[c % 2], 16 * (c // 2 + 1))
                to = scores[:].rearrange("p (j c) h -> p j c h", c=CHUNKS)[:, :, c, :]
                dve.tensor_tensor(to, to, curv[:, c % 2], ALU.add).then_inc(placed, 1)


def stage_softmax(nc, sh, dst, scores):
    with Scope(nc, "m_") as sc:
        PIECES = 4
        WIDTH = CHUNK_EDGES // PIECES
        rows = sc.sb("rows", [P, CHUNK_EDGES + 2])
        keep = sc.sb("keep", [P, CHUNK_EDGES + 1], BF16)
        drop = sc.sb("drop", [P, CHUNK_EDGES + 1], BF16)
        ends = sc.sb("ends", [1, 3, CHUNKS], I32)
        links = sc.sb("links", [1, CHUNKS + 1])
        single = sc.sb("single", [1, CHUNKS])
        go_on = sc.sb("go_on", [1, 2, CHUNKS])
        chain_keep = sc.sb("chain_keep", [1, 2, HEADS, CHUNKS])
        chain_drop = sc.sb("chain_drop", [1, 2, HEADS, CHUNKS])
        chain = sc.sb("chain", [1, HEADS, CHUNKS])
        start_row = sc.sb("start_row", [1, CHUNKS, HEADS])
        start_col = sc.sb("start_col", [P, 1])
        edge_col = sc.sb("edge_col", [P, 1])
        one = sc.sb("one", [1, 1])
        turn_ps = [sc.ps(f"turn_ps{i}", (P, 4, P)) for i in range(6)]
        row_ps, col_ps = sc.ps("row_ps"), sc.ps("col_ps")
        work = scores[:].rearrange("p t h -> p (t h)")

        loaded, ends_in, masks, vec, rows_turned, rows_by_act, rows_by_dve = (sc.sem(n) for n in (
            "loaded", "ends_in", "masks", "vec", "rows_turned", "rows_by_act", "rows_by_dve"))
        edge_turned, start_turned, shifted, exped, back_turned, back_by_act, back_by_dve, divided = (
            sc.sem(n) for n in ("edge_turned", "start_turned", "shifted", "exped", "back_turned", "back_by_act",
                                "back_by_dve", "divided"))
        block = sc.enter_context(nc.Block())
        GROUPS = CHUNK_TILES // 4
        CHAIN_AT = [10 + 8 * i for i in range(4)]
        dst_rows = rows[:].bitcast(I32)

        @block.sync
        def _(sp):
            cut = dst[0:EDGES_PAD].rearrange("(c i) -> c i", i=CHUNK_EDGES)
            cut2 = dst[2:2 + EDGES_PAD].rearrange("(c i) -> c i", i=CHUNK_EDGES)
            for h in range(HEADS):
                to = dst_rows[h::HEADS, :]
                sp.dma_start(to[:, 2:], cut2).then_inc(loaded, 16)
                sp.dma_start(to[:, 0:2], cut[:, 0:2]).then_inc(loaded, 16)
            with nc.allow_non_contiguous_dma(reason="one number of each chunk"):
                for i, (a, at) in enumerate(((cut, 0), (cut, 1), (cut2, CHUNK_EDGES - 2))):
                    sp.dma_start(ends[:, i, :], a[:, at:at + 1].rearrange("c o -> o c")).then_inc(ends_in, 16)
            sp.wait_ge(loaded, 16 * 2 * HEADS)
            sp.wait_ge(ends_in, 48)

        @block.tensor
        def _(pe):
            pe.wait_ge(masks, 2)
            by_column = scores[:].rearrange("p (j c) h -> p j (c h)", c=CHUNKS)
            for g in range(GROUPS):
                if g >= 6:
                    pe.wait_ge((rows_by_act, rows_by_dve)[g % 2], (g - 6) // 2 + 1)
                for u in range(4):
                    ins = pe.transpose(turn_ps[g % 6][:, u, :], by_column[:, 4 * g + u], sh.ident[:])
                ins.then_inc(rows_turned, 1)
            for n in range(4):
                pe.wait_ge(vec, CHAIN_AT[n])
                pe.transpose(row_ps[0:1, 0:P], edge_col[:], sh.ident[:]).then_inc(edge_turned, 1)
                pe.wait_ge(vec, CHAIN_AT[n] + 4)
                pe.matmul(col_ps[:, 0:1], start_row[:].rearrange("o c h -> o (c h)"), one[:], start=True, stop=True)\
                    .then_inc(start_turned, 1)
            for g in range(GROUPS):
                pe.wait_ge(divided, 4 * g // (CHUNK_TILES // PIECES) + 1)
                if (4 * g + 3) // (CHUNK_TILES // PIECES) != 4 * g // (CHUNK_TILES // PIECES):
                    pe.wait_ge(divided, (4 * g + 3) // (CHUNK_TILES // PIECES) + 1)
                if g >= 6:
                    pe.wait_ge((back_by_act, back_by_dve)[g % 2], (g - 6) // 2 + 1)
                for u in range(4):
                    at = (4 * g + u) * P
                    ins = pe.transpose(turn_ps[g % 6][:, u, :], rows[:, at:at + P], sh.ident[:])
                ins.then_inc(back_turned, 1)

        def rows_out(eng, copy, g, done):
            eng.wait_ge(rows_turned, g + 1)
            copy(rows[:, 4 * P * g:4 * P * (g + 1)], turn_ps[g % 6][:].rearrange("p u e -> p (u e)")).then_inc(done, 1)

        def back_out(eng, copy, g, done):
            eng.wait_ge(back_turned, g + 1)
            to = scores[:].rearrange("p (j c) h -> p j (c h)", c=CHUNKS)[:, 4 * g:4 * g + 4]
            copy(to, turn_ps[g % 6][:]).then_inc(done, 1)

        @block.scalar
        def _(act):
            def copy(to, frm):
                return act.activation(to, frm, ACT.Copy)
            for g in range(0, GROUPS, 2):
                rows_out(act, copy, g, rows_by_act)
            for i in range(PIECES):
                part = rows[:, i * WIDTH:(i + 1) * WIDTH]
                act.wait_ge(shifted, i + 1)
                act.activation(part, part, ACT.Exp).then_inc(exped, 1)
            act.wait_ge(divided, PIECES)
            for g in range(0, GROUPS, 2):
                back_out(act, copy, g, back_by_act)

        @block.vector
        def _(dve):
            n = [0]

            def then(ins):
                n[0] += 1
                ins.then_inc(vec, 1)
                dve.wait_ge(vec, n[0])

            dve.wait_ge(loaded, 16 * 2 * HEADS)
            a, b = dst_rows[:, 1:CHUNK_EDGES + 2], dst_rows[:, 0:CHUNK_EDGES + 1]
            dve.tensor_tensor(keep[:], a, b, ALU.is_equal).then_inc(masks, 1)
            dve.wait_ge(masks, 1)
            dve.tensor_scalar(drop[:], keep[:], 1.0, BIG, ALU.subtract, ALU.mult).then_inc(masks, 1)
            dve.wait_ge(ends_in, 48)
            dve.memset(one[:], 1.0)
            then(dve.memset(links[:], 0.0))
            then(dve.tensor_tensor(links[:, 0:CHUNKS], ends[:, 0, :], ends[:, 1, :], ALU.is_equal))
            then(dve.tensor_tensor(single[:], ends[:, 1, :], ends[:, 2, :], ALU.is_equal))
            then(dve.tensor_tensor(go_on[:, 0, :], single[:], links[:, 0:CHUNKS], ALU.mult))
            then(dve.tensor_tensor(go_on[:, 1, :], single[:], links[:, 1:CHUNKS + 1], ALU.mult))
            for i in range(2):
                then(dve.tensor_copy(chain_keep[:, i], go_on[:, i:i + 1, :].to_broadcast([1, HEADS, CHUNKS])))
            then(dve.tensor_scalar(chain_drop[:], chain_keep[:], 1.0, BIG, ALU.subtract, ALU.mult))
            assert n[0] == 8
            for g in range(1, GROUPS, 2):
                rows_out(dve, dve.tensor_copy, g, rows_by_dve)
            dve.wait_ge(rows_by_act, (GROUPS + 1) // 2)
            dve.wait_ge(rows_by_dve, GROUPS // 2)
            dve.wait_ge(masks, 2)
            r = rows[:, 0:CHUNK_EDGES]
            last = CHUNK_EDGES - 1

            def scan(to, frm, back, mask, start, op0, op1):
                if back:
                    return dve.tensor_tensor_scan(to[:, ::-1], mask[:, CHUNK_EDGES:0:-1], frm[:, ::-1], start, op0, op1)
                return dve.tensor_tensor_scan(to, mask[:, 0:CHUNK_EDGES], frm, start, op0, op1)

            def spread(i, frm, back, mask, chain_mask, rest, op0, op1):
                then(scan(work, frm, back, mask, rest, op0, op1))
                at = 0 if back else last
                then(dve.tensor_copy(edge_col[:], work[:, at:at + 1]))
                assert n[0] == CHAIN_AT[i], n[0]
                dve.wait_ge(edge_turned, i + 1)
                ordered = row_ps[0:1, 0:P].rearrange("o (c h) -> o h c", h=HEADS)
                then(dve.tensor_copy(chain[:], ordered))
                flat, m = chain[:].rearrange("o h c -> o (h c)"), chain_mask[:, int(back)].rearrange("o h c -> o (h c)")
                if back:
                    flat, m = flat[:, ::-1], m[:, ::-1]
                then(dve.tensor_tensor_scan(flat, m, flat, rest, op0, op1))
                then(dve.memset(start_row[:], rest))
                if back:
                    then(dve.tensor_copy(start_row[:, 0:CHUNKS - 1, :].rearrange("o c h -> o h c"), chain[:, :, 1:]))
                else:
                    then(dve.tensor_copy(start_row[:, 1:, :].rearrange("o c h -> o h c"), chain[:, :, 0:CHUNKS - 1]))
                dve.wait_ge(start_turned, i + 1)
                then(dve.tensor_copy(start_col[:], col_ps[:, 0:1]))
                then(scan(work, frm, back, mask, start_col[:], op0, op1))
            spread(0, r, False, drop, chain_drop, -BIG, ALU.add, ALU.max)
            spread(1, work, True, drop, chain_drop, -BIG, ALU.add, ALU.max)
            for i in range(PIECES):
                part = slice(i * WIDTH, (i + 1) * WIDTH)
                dve.tensor_tensor(rows[:, part], rows[:, part], work[:, part], ALU.subtract).then_inc(shifted, 1)
            dve.wait_ge(exped, PIECES)
            spread(2, r, False, keep, chain_keep, 0.0, ALU.mult, ALU.add)
            spread(3, work, True, keep, chain_keep, 0.0, ALU.mult, ALU.max)
            then(dve.reciprocal(work, work))
            for i in range(PIECES):
                part = slice(i * WIDTH, (i + 1) * WIDTH)
                dve.tensor_tensor(rows[:, part], rows[:, part], work[:, part], ALU.mult).then_inc(divided, 1)
            dve.wait_ge(divided, PIECES)
            for g in range(1, GROUPS, 2):
                back_out(dve, dve.tensor_copy, g, back_by_dve)


def stage_messages(nc, sh, probs):
    with Scope(nc, "c_") as sc:
        v_tab = sc.sb("v_tab", [P, BLOCKS, D])
        onehot = sc.sb("onehot", [P, U, P])
        onehot_t = sc.sb("onehot_t", [P, 4, 2, P])
        same = sc.sb("same", [P, U, P])
        message = sc.sb("message", [P, U, D])
        comb = sc.sb("comb", [P, U, D])
        scat_idx = sc.sb("scat_idx", [P, U], I32)
        src_slot = sc.sb("src_slot", [P, U])
        src_ps = [sc.ps(f"src_ps{i}") for i in range(2)]
        turn_ps = [sc.ps(f"turn_ps{i}") for i in range(2)]
        vd_ps = [sc.ps(f"vd_ps{i}") for i in range(2)]
        comb_ps = [sc.ps(f"comb_ps{i}") for i in range(2)]

        loaded, ready, issued = (sc.sem(n) for n in ("loaded", "ready", "issued"))
        (idx_set, slot_set, onehot_set, turned, turn_out, src_spread, same_set, expanded, message_set, combined,
         comb_out, scattered) = (sc.sem_each(n) for n in (
             "idx_set", "slot_set", "onehot_set", "turned", "turn_out", "src_spread", "same_set", "expanded",
             "message_set", "combined", "comb_out", "scattered"))
        block = sc.enter_context(nc.Block())
        n_loaded = 16 * (BLOCKS // LOAD_BLOCKS)

        @block.sync
        def _(sp):
            for b in range(0, BLOCKS, LOAD_BLOCKS):
                sp.dma_start(v_tab[:, b:b + LOAD_BLOCKS, :], sh.kvy[:, b:b + LOAD_BLOCKS, 1, :]).then_inc(loaded, 16)
            sp.wait_ge(loaded, n_loaded)

        @block.gpsimd
        def _(pool):
            def scatter(it, d, k):
                wait(pool, idx_set[k], it.after())
                wait(pool, comb_out[k], it.after())
                wait(pool, *freed(scattered, k, MSG_TABS, it, 0, 16))
                settle(pool, issued)
                pool.indirect_dma_start(sh.msg_tabs[k % MSG_TABS], bass.IndirectOffsetOnAxis(ap=scat_idx[:, k:k + 1], axis=0),
                                        comb[:, k, :], None, compute_op=ALU.add).then_inc(scattered[k], 16)

            def passes(it, last=False):
                for k in range(U):
                    scatter(it, 0, k)
            run_passes(pool, passes, dmas=(0, 1))
            for k in range(U):
                pool.wait_ge(scattered[k], 16 * ITERS)

        @block.tensor
        def _(pe):
            pe.wait_ge(loaded, n_loaded)

            def spread(it, d, k):
                wait(pe, slot_set[k], it.after(d))
                wait(pe, *freed(same_set, k, 2, it, d))
                pe.transpose(src_ps[k % 2][:, 0:P], src_slot[:, k:k + 1].to_broadcast([P, P]), sh.ident[:])\
                    .then_inc(src_spread[k], 1)

            def turn(it, d, k):
                wait(pe, onehot_set[k], it.after(d))
                wait(pe, *freed(turn_out, k, 2, it, d))
                pe.transpose(turn_ps[k % 2][:, 0:P], onehot[:, k, :], sh.ident[:]).then_inc(turned[k], 1)

            def expand(it, d, k, low, high):
                wait(pe, turn_out[k], it.after(d))
                wait(pe, *freed(message_set, k, 2, it, d))
                pe.matmul(vd_ps[k % 2][:, 0:D], onehot_t[:, k % 4, 0, :], v_tab[:, bass.ds(low, 1), :], start=True,
                          stop=False)
                pe.matmul(vd_ps[k % 2][:, 0:D], onehot_t[:, k % 4, 1, :], v_tab[:, bass.ds(high, 1), :],
                          start=False, stop=True).then_inc(expanded[k], 1)

            def combine(it, k):
                wait(pe, same_set[k], it.after())
                wait(pe, message_set[k], it.after())
                wait(pe, *freed(comb_out, k, 2, it))
                pe.matmul(comb_ps[k % 2][:, 0:D], same[:, k, :], message[:, k, :], start=True, stop=True)\
                    .then_inc(combined[k], 1)

            def passes(it, last=False):
                for k in range(U):
                    if k % QUAD == 0:
                        windows = load_windows(nc, pe, sh, it, k + 3)
                    advance(it, last, k, ((turn, 5), (spread, 5),
                                          (lambda it, d, kk: expand(it, d, kk, *windows[k % QUAD]), 3)))
                    combine(it, k)
            prepare(pe, turn, 5)
            prepare(pe, spread, 5)
            windows = load_windows(nc, pe, sh, Pass(pe, 0), 0)
            for k in range(3):
                expand(Pass(pe, 0), 0, k, *windows[k])
            run_passes(pe, passes)

        @block.scalar
        def _(act):
            act.wait_ge(ready, 1)

            def turn_evac(it, d, k):
                wait(act, turned[k], it.after(d))
                wait(act, *freed(expanded, k, 4, it, d))
                act.activation(onehot_t[0:HALF, k % 4, 0, :], turn_ps[k % 2][0:HALF, 0:P], ACT.Copy)
                act.activation(onehot_t[HALF:P, k % 4, 1, :], turn_ps[k % 2][HALF:P, 0:P], ACT.Copy)\
                    .then_inc(turn_out[k], 1)

            def comb_evac(it, d, k):
                wait(act, combined[k], it.after())
                wait(act, scattered[k], it.before(0, 16))
                act.activation(comb[:, k, :], comb_ps[k % 2][:, 0:D], ACT.Copy).then_inc(comb_out[k], 1)

            def passes(it, last=False):
                for k in range(U):
                    advance(it, last, k, ((turn_evac, 4), (comb_evac, 0)))
            prepare(act, turn_evac, 4)
            run_passes(act, passes, dmas=(0,))

        @block.vector
        def _(dve):
            dve.memset(onehot_t[:], 0.0).then_inc(ready, 1)

            def index(it, d, k):
                wait(dve, scattered[k], it.before(d, 16))
                dve.tensor_scalar(scat_idx[:, k:k + 1], col(sh.scat_cols, it, d, k), 0.0, None, ALU.max)\
                    .then_inc(idx_set[k], 1)

            def slot(it, d, k):
                wait(dve, src_spread[k], it.before(d))
                dve.tensor_scalar(src_slot[:, k:k + 1], col(sh.src_cols, it, d, k), 0.0, None, ALU.max)\
                    .then_inc(slot_set[k], 1)

            def hot(it, d, k):
                wait(dve, turned[k], it.before(d))
                dve.tensor_scalar(onehot[:, k, :], sh.iota[:], col(sh.rel_cols, it, d, k), None, ALU.is_equal)\
                    .then_inc(onehot_set[k], 1)

            def match(it, d, k):
                wait(dve, src_spread[k], it.after(d))
                wait(dve, combined[k], it.before(d))
                dve.tensor_scalar(same[:, k, :], src_ps[k % 2][:, 0:P], col(sh.src_cols, it, d, k), None,
                                  ALU.is_equal).then_inc(same_set[k], 1)

            def weigh(it, d, k, place):
                wait(dve, expanded[k], it.after(d))
                wait(dve, combined[k], it.before(d))
                p = probs[:, bass.ds(place, 1), :]
                dve.tensor_tensor(message[:, k, :].rearrange("p (h c) -> p h c", c=HEAD_D),
                                  vd_ps[k % 2][:, 0:D].rearrange("p (h c) -> p h c", c=HEAD_D),
                                  p.rearrange("p o h -> p h o").to_broadcast([P, HEADS, HEAD_D]), ALU.mult)\
                    .then_inc(message_set[k], 1)

            def passes(it, last=False):
                for k in range(U):
                    if k % QUAD == 0:
                        places = load_places(nc, dve, sh, it, k + 2)
                    advance(it, last, k, ((index, 1), (slot, 6), (hot, 6), (match, 4),
                                          (lambda it, d, kk: weigh(it, d, kk, *places[k % QUAD]), 2)))
            for stage, lead in ((index, 1), (slot, 6), (hot, 6), (match, 4)):
                prepare(dve, stage, lead)
            places = load_places(nc, dve, sh, Pass(dve, 0), 0)
            for k in range(2):
                weigh(Pass(dve, 0), 0, k, *places[k])
            run_passes(dve, passes, dmas=(0, 1))


def stage_last_nodes(nc, sh, w, out):
    with Scope(nc, "f_") as sc:
        S = NODE_S
        msg_parts = sc.sb("msg_parts", [P, MSG_TABS, S, D])
        msg = sc.sb("msg", [P, S, D])
        y = sc.sb("y", [P, S, D])
        y_bo = sc.sb("y_bo", [P, S, D])
        y_b2 = sc.sb("y_b2", [P, S, D])
        msg_t = sc.sb("msg_t", [P, S, P])
        x1 = sc.sb("x1", [P, S, D])
        xy = sc.sb("xy", [P, S, D])
        eps = sc.sb("eps", [P, 1])
        normed = sc.sb("normed", [P, S, D])
        normed_t = sc.sb("normed_t", [P, S, P])
        hidden = sc.sb("hidden", [P, S, FFC, P])
        x2 = sc.sb("x2", [P, S, D])
        result = sc.sb("result", [P, S, D])
        wo = sc.sb("wo", [P, D])
        w1 = sc.sb("w1", [P, FF])
        w1_g = sc.sb("w1_g", [P, FF])
        w2 = sc.sb("w2", [P, FFC, D])
        bo = sc.sb("bo", [P, D])
        b2 = sc.sb("b2", [P, D])
        b1 = sc.sb("b1", [P, FFC])
        b1_g = sc.sb("b1_g", [P, FFC])
        g2 = sc.sb("g2", [P, 1])
        be2 = sc.sb("be2", [P, 1])
        turn_ps = [sc.ps(f"turn_ps{i}") for i in range(2)]
        x1_ps = [sc.ps(f"x1_ps{i}") for i in range(2)]
        hid_ps = [sc.ps(f"hid_ps{i}", (P, FFC, P)) for i in range(2)]
        out_ps = [sc.ps(f"out_ps{i}") for i in range(2)]

        weights, ready, bias_made = (sc.sem(n) for n in ("weights", "ready", "bias_made"))
        parts_in, y_in, paired, summed, y_bo_set, y_b2_set, xy_out, stored = (sc.sem(n) for n in (
            "parts_in", "y_in", "paired", "summed", "y_bo_set", "y_b2_set", "xy_out", "stored"))
        (msg_turned, msg_t_out, attended, x1_out, norm_out, norm_turned, norm_t_out, hid_out, relu_out, final_ps,
         final_out, result_out) = (sc.sem_counted(n, S) for n in (
             "msg_turned", "msg_t_out", "attended", "x1_out", "norm_out", "norm_turned", "norm_t_out", "hid_out",
             "relu_out", "final_ps", "final_out", "result_out"))
        norm1 = Layernorm(sc, "norm1_", S, lambda s: x1[:, s, :], x1_out, lambda s: normed[:, s, :], norm_out,
                          norm_turned[S - 1])
        norm2 = Layernorm(sc, "norm2_", S, lambda s: x2[:, s, :], final_out, lambda s: result[:, s, :], result_out,
                          stored, 16)
        block = sc.enter_context(nc.Block())
        n_weights = 16 * 8
        n_ready = 3

        @block.sync
        def _(sp):
            sp.dma_start(wo[:], w["L1_gnn_Wo"]).then_inc(weights, 16)
            sp.dma_start(w1[:], w["L1_gnn_W1"]).then_inc(weights, 16)
            sp.dma_start(w2[:], w["L1_gnn_W2"].rearrange("(i f) c -> f i c", f=P)).then_inc(weights, 16)
            for to, n in ((bo, "bo"), (b2, "b2")):
                sp.dma_start(to[:], w["L1_gnn_" + n].rearrange("(o c) -> o c", o=1).to_broadcast([P, D]))\
                    .then_inc(weights, 16)
            for to, n in ((g2, "g2"), (be2, "be2")):
                sp.dma_start(to[:], w["L1_gnn_" + n].rearrange("(c o) -> c o", o=1)).then_inc(weights, 16)
            with nc.allow_non_contiguous_dma(reason="a column of each chunk"):
                sp.dma_start(b1[:], w["L1_gnn_b1"].rearrange("(i f) -> f i", f=P)).then_inc(weights, 16)

            def load_y(it, d):
                wait(sp, y_b2_set, it.before(d))
                sp.dma_start(y[:], sh.kvy[:, blocks_at(it, d), 2, :]).then_inc(y_in, 16)

            def load_parts(it, d):
                wait(sp, summed, it.before(d))
                for t in range(MSG_TABS):
                    sp.dma_start(msg_parts[:, t], sh.msg_tabs[t][blocks_at(it, d, P), :]
                                 .rearrange("(s p) c -> p s c", p=P)).then_inc(parts_in, 16)

            def store(it, d):
                wait(sp, result_out[S - 1], it.after(d))
                if isinstance(it.q, int) and it.q == NODE_PASSES - 1:
                    b = it.q * NODE_S * P
                    sp.dma_start(out[b:b + (S - 1) * P, :].rearrange("(s p) c -> p s c", p=P), result[:, 0:S - 1])\
                        .then_inc(stored, 16)
                    sp.dma_start(out[b + (S - 1) * P:N_NODES, :], result[0:LAST_ROWS, S - 1, :]).then_inc(stored, 16)
                else:
                    sp.dma_start(out[blocks_at(it, d, P), :].rearrange("(s p) c -> p s c", p=P), result[:])\
                        .then_inc(stored, 16)
            run_parts(sp, NODE_PASSES, ((load_y, 2), (load_parts, 3), (store, 0)), counts=(1, 2, 3))
            sp.wait_ge(stored, 16 * (NODE_PASSES + 1))

        @block.gpsimd
        def _(pool):
            pool.wait_ge(weights, n_weights)

            def add_b2(it, d):
                wait(pool, y_in, it.after(d, 16))
                wait(pool, xy_out, it.before(d))
                pool.tensor_tensor(y_b2[:], y[:], b2[:, None, :].to_broadcast([P, S, D]), ALU.add).then_inc(y_b2_set, 1)

            def add_bo(it, d):
                wait(pool, y_in, it.after(d, 16))
                wait(pool, x1_out[S - 1], it.before(d))
                pool.tensor_tensor(y_bo[:], y[:], bo[:, None, :].to_broadcast([P, S, D]), ALU.add).then_inc(y_bo_set, 1)

            def add_parts(it, d):
                wait(pool, parts_in, it.after(d, 16 * MSG_TABS))
                pool.tensor_tensor(msg_parts[:, 0:2], msg_parts[:, 0:2], msg_parts[:, 2:4], ALU.add)\
                    .then_inc(paired, 1)
                wait(pool, paired, it.after(d))
                wait(pool, msg_turned[S - 1], it.before(d))
                pool.tensor_tensor(msg[:], msg_parts[:, 0], msg_parts[:, 1], ALU.add).then_inc(summed, 1)
            run_parts(pool, NODE_PASSES, ((add_parts, 2), (add_b2, 1), (add_bo, 2)), counts=(1, 2, 3), dmas=(2, 3),
                      several=((16 * MSG_TABS, 3),))

        @block.tensor
        def _(pe):
            pe.wait_ge(weights, n_weights)
            for i in range(FFC):
                ins = pe.matmul(out_ps[0][:, i:i + 1], w1[:, i * P:(i + 1) * P], be2[:], start=True, stop=True)
            ins.then_inc(bias_made, 1)
            pe.wait_ge(ready, n_ready)

            def attend(it, d):
                for s in range(S):
                    wait(pe, msg_t_out[s], it.after(d))
                    wait(pe, *bank_freed(x1_out, s, it, d))
                    pe.matmul(x1_ps[s % 2][:, 0:D], msg_t[:, s, :], wo[:], start=True, stop=True)\
                        .then_inc(attended[s].sem, 1)

            def turn_messages(it, d):
                wait(pe, summed, it.after(d))
                wait(pe, norm_t_out[S - 1], it.before(d - 1))
                for s in range(S):
                    if s >= 2:
                        wait(pe, msg_t_out[s - 2], it.after(d))
                    pe.transpose(turn_ps[s % 2][:, 0:P], msg[:, s, :], sh.ident[:]).then_inc(msg_turned[s].sem, 1)

            def turn_normed(it, d):
                none = isinstance(it.q, int) and it.q + d == NODE_PASSES - 1
                wait(pe, msg_t_out[S - 1], it.after(d + (not none)))
                for s in range(S):
                    wait(pe, norm_out[s], it.after(d))
                    if s >= 2:
                        wait(pe, norm_t_out[s - 2], it.after(d))
                    pe.transpose(turn_ps[s % 2][:, 0:P], normed[:, s, :], sh.ident[:]).then_inc(norm_turned[s].sem, 1)

            def feed(it, d):
                for s in range(S + 1):
                    if s < S:
                        wait(pe, norm_t_out[s], it.after(d))
                        wait(pe, *bank_freed(relu_out, s, it, d))
                        for i in range(FFC):
                            ins = pe.matmul(hid_ps[s % 2][:, i, :], w1_g[:, i * P:(i + 1) * P], normed_t[:, s, :],
                                            start=True, stop=True)
                        ins.then_inc(hid_out[s].sem, 1)
                    if s:
                        wait(pe, relu_out[s - 1], it.after(d))
                        wait(pe, *bank_freed(final_out, s - 1, it, d))
                        for i in range(FFC):
                            ins = pe.matmul(out_ps[(s - 1) % 2][:, 0:D], hidden[:, s - 1, i, :], w2[:, i, :],
                                            start=(i == 0), stop=(i == FFC - 1))
                        ins.then_inc(final_ps[s - 1].sem, 1)
            run_parts(pe, NODE_PASSES, ((attend, 1), (turn_messages, 2), (feed, 0), (turn_normed, 1)),
                      counts=(1, 2, 3))

        @block.scalar
        def _(act):
            act.wait_ge(ready, n_ready)

            def messages_out(it, d):
                for s in range(S):
                    wait(act, msg_turned[s], it.after(d))
                    wait(act, attended[s], it.before(d))
                    act.activation(msg_t[:, s, :], turn_ps[s % 2][:, 0:P], ACT.Copy).then_inc(msg_t_out[s].sem, 1)

            def normed_out(it, d):
                for s in range(S):
                    wait(act, norm_turned[s], it.after(d))
                    wait(act, hid_out[s], it.before(d))
                    act.activation(normed_t[:, s, :], turn_ps[s % 2][:, 0:P], ACT.Copy).then_inc(norm_t_out[s].sem, 1)

            def relu(it, d):
                for s in range(S):
                    wait(act, hid_out[s], it.after(d))
                    wait(act, final_ps[s], it.before(d))
                    for i in range(FFC):
                        ins = act.activation(hidden[:, s, i, :], hid_ps[s % 2][:, i, :], ACT.Relu,
                                             bias=b1_g[:, i:i + 1])
                    ins.then_inc(relu_out[s].sem, 1)
            run_parts(act, NODE_PASSES, ((messages_out, 2), (lambda it, d: norm1.roots(act, eps, it, d), 1), (relu, 0),
                                         (normed_out, 1), (lambda it, d: norm2.roots(act, eps, it, d), 0)),
                      counts=(1, 2, 3))

        @block.vector
        def _(dve):
            dve.wait_ge(weights, n_weights)
            dve.memset(eps[:], EPS).then_inc(ready, 1)
            dve.tensor_scalar(w1_g[:], w1[:], g2[:], None, ALU.mult).then_inc(ready, 1)
            dve.wait_ge(bias_made, 1)
            dve.tensor_tensor(b1_g[:], out_ps[0][:, 0:FFC], b1[:], ALU.add).then_inc(ready, 1)

            def head(it, d):
                wait(dve, y_bo_set, it.after(d))
                wait(dve, norm_out[S - 1], it.before(d))
                wait(dve, xy_out, it.before(d))
                for s in range(S):
                    wait(dve, attended[s], it.after(d))
                    dve.tensor_tensor(x1[:, s, :], x1_ps[s % 2][:, 0:D], y_bo[:, s, :], ALU.add)\
                        .then_inc(x1_out[s].sem, 1)
                norm1.moments(dve, it, d)
                norm1.rescale(dve, it, d)

            def tail(it, d):
                wait(dve, xy_out, it.after(d))
                wait(dve, result_out[S - 1], it.before(d))
                for s in range(S):
                    wait(dve, final_ps[s], it.after(d))
                    dve.tensor_tensor(x2[:, s, :], out_ps[s % 2][:, 0:D], xy[:, s, :], ALU.add)\
                        .then_inc(final_out[s].sem, 1)
                norm2.moments(dve, it, d)
                norm2.rescale(dve, it, d)

            def residual(it, d):
                wait(dve, x1_out[S - 1], it.after(d))
                wait(dve, y_b2_set, it.after(d))
                wait(dve, final_out[S - 1], it.before(d))
                dve.tensor_tensor(xy[:], x1[:], y_b2[:], ALU.add).then_inc(xy_out, 1)
            run_parts(dve, NODE_PASSES, ((head, 1), (tail, 0), (residual, 1)), dmas=(0, 1))


class General:

    def __init__(self, nc, sc, src, dst):
        self.nc = nc
        self.nodes = (src.rearrange("t e -> (t e)"), dst[1:1 + EDGES_PAD])
        self.index = sc.sb("index", [P, 2], I32)
        self.index_f = sc.sb("index_f", [P, 2])
        self.in_block = sc.sb("in_block", [P, 1], I32)
        self.block_no = sc.sb("block_no", [P, 1], I32)
        self.kvy_row = sc.sb("kvy_row", [P, 1], I32)
        self.same = sc.sb("same", [P, 2, P])
        self.index_in = sc.sem_each("index_in", 2)
        self.cast, self.split, self.row_set, self.same_set, self.spread_set, self.issued = (
            sc.sem(n) for n in ("cast", "split", "row_set", "same_set", "spread_set", "issued"))

    def load(self, sp, it):
        for i in range(2):
            at = it.q * P
            rows = self.nodes[i][slice(at, at + P) if isinstance(it.q, int) else bass.ds(at, P)]
            with self.nc.allow_non_contiguous_dma(reason="an index each partition"):
                sp.dma_start(self.index[:, i:i + 1], rows.rearrange("(p o) -> p o", o=1)).then_inc(self.index_in[i], 16)

    def wait_index(self, eng, it):
        for i in range(2):
            wait(eng, self.index_in[i], it.after(0, 16))

    def floats(self, dve, it):
        self.wait_index(dve, it)
        dve.tensor_scalar(self.index_f[:], self.index[:], 0.0, None, ALU.max).then_inc(self.cast, 1)

    def kvy_rows(self, dve, it):
        dve.tensor_scalar(self.in_block[:], self.index[:, 1:2], P - 1, None, ALU.bitwise_and).then_inc(self.split, 1)
        dve.tensor_scalar(self.block_no[:], self.index[:, 1:2], 7, None, ALU.arith_shift_right).then_inc(self.split, 1)
        wait(dve, self.split, it.after(0, 2))
        dve.scalar_tensor_tensor(out=self.kvy_row[:], in0=self.in_block[:], scalar=float(BLOCKS), in1=self.block_no[:],
                                 op0=ALU.mult, op1=ALU.add).then_inc(self.row_set, 1)

    def spread(self, pe, sh, it, ps):
        wait(pe, self.cast, it.after())
        for i in range(2):
            ins = pe.transpose(ps[:, i * P:(i + 1) * P], self.index_f[:, i:i + 1].to_broadcast([P, P]), sh.ident[:])
        ins.then_inc(self.spread_set, 1)

    def masks(self, dve, it, ps):
        wait(dve, self.spread_set, it.after())
        for i in range(2):
            ins = dve.tensor_scalar(self.same[:, i, :], ps[:, i * P:(i + 1) * P], self.index_f[:, i:i + 1], None,
                                    ALU.is_equal)
        ins.then_inc(self.same_set, 1)

    def gather(self, pool, to, table, i, done):
        at = self.kvy_row[:] if i == 2 else self.index[:, i:i + 1]
        pool.indirect_dma_start(to, None, table, bass.IndirectOffsetOnAxis(ap=at, axis=0)).then_inc(done, 16)

    def scatter(self, pool, table, i, rows, done):
        pool.indirect_dma_start(table, bass.IndirectOffsetOnAxis(ap=self.index[:, i:i + 1], axis=0), rows, None)\
            .then_inc(done, 16)


def run_tiles(eng, tile, until=TILES):
    tile(Pass(eng, 0))
    with eng.Fori(1, until) as q:
        tile(Pass(eng, q, counts=(1,), dmas=(0, 1), several=((2, 1),)))


def fill_table(sp, table, values, done):
    sp.dma_start(table.rearrange("(p b) c -> p b c", p=P),
                 values[:, None, :].to_broadcast([P, table.shape[0] // P, table.shape[1]])).then_inc(done, 16)


def general_aggregate(nc, sh, src, dst, x, edge_attr, w, x_tab, in_sum):
    with Scope(nc, "ga_") as sc:
        gen = General(nc, sc, src, dst)
        feats = sc.sb("feats", [P, 2, ROW])
        old = sc.sb("old", [P, 2, ROW])
        new = sc.sb("new", [P, 2, ROW])
        zeros = sc.sb("zeros", [P, ROW])
        attr = sc.sb("attr", [P, P])
        attr_t = sc.sb("attr_t", [P, P])
        curv = sc.sb("curv", [P, HEADS])
        wc = sc.sb("wc", [P, HEADS])
        bc = sc.sb("bc", [P, HEADS])
        spread_ps, comb_ps, turn_ps, score_ps = (sc.ps(n) for n in ("spread_ps", "comb_ps", "turn_ps", "score_ps"))
        loaded, ready, zeroed, tables_in, combined, new_set, attr_in, turned, turn_out, scored, curv_set, curv_stored = (
            sc.sem(n) for n in ("loaded", "ready", "zeroed", "tables_in", "combined", "new_set", "attr_in", "turned",
                                "turn_out", "scored", "curv_set", "curv_stored"))
        feats_in, old_in, stored = (sc.sem_each(n, 2) for n in ("feats_in", "old_in", "stored"))
        block = sc.enter_context(nc.Block())
        tables = (sh.sum_tabs[0], sh.in_tab)

        @block.sync
        def _(sp):
            sp.dma_start(wc[:], w["L1_gnn_Wc"]).then_inc(loaded, 16)
            sp.dma_start(bc[:], w["L1_gnn_bc"].rearrange("(o h) -> o h", o=1).to_broadcast([P, HEADS]))\
                .then_inc(loaded, 16)
            for b in range(0, BLOCKS, LOAD_BLOCKS):
                sp.dma_start(x_tab[:, b:b + LOAD_BLOCKS, 0:D], x[b * P:(b + LOAD_BLOCKS) * P]
                             .rearrange("(b p) c -> p b c", p=P)).then_inc(loaded, 16)
            sp.wait_ge(loaded, 16 * (2 + BLOCKS // LOAD_BLOCKS))
            sp.wait_ge(ready, 3)
            fill_table(sp, sh.in_tab, zeros, zeroed)
            zero_tables(sp, sh, sh.msg_tabs, zeroed)
            sp.wait_ge(zeroed, 16 * (1 + MSG_TABS))

            def tile(it):
                for i in range(2):
                    wait(sp, stored[i], it.before(0, 16))
                wait(sp, curv_stored, it.before(0, 16))
                gen.load(sp, it)
                at = it.q * P
                if not isinstance(it.q, int):
                    sp.dma_start(attr[:], edge_attr[bass.ds(at, P), :]).then_inc(attr_in, 16)
                elif it.q < FULL_TILES:
                    sp.dma_start(attr[:], edge_attr[at:at + P, :]).then_inc(attr_in, 16)
                else:
                    sp.dma_start(attr[0:LAST_EDGES, :], edge_attr[FULL_TILES * P:N_EDGES, :]).then_inc(attr_in, 16)
                wait(sp, curv_set, it.after())
                t = slice(it.q, it.q + 1) if isinstance(it.q, int) else bass.ds(it.q, 1)
                sp.dma_start(sh.curv_dram[:, t, :].rearrange("p o h -> p (o h)"), curv[:]).then_inc(curv_stored, 16)
            run_tiles(sp, tile, FULL_TILES)
            for q in range(FULL_TILES, TILES):
                tile(Pass(sp, q))
            for i in range(2):
                sp.wait_ge(stored[i], 16 * TILES)
            sp.wait_ge(curv_stored, 16 * TILES)
            for b in range(0, BLOCKS, LOAD_BLOCKS):
                sp.dma_start(in_sum[:, b:b + LOAD_BLOCKS, :], sh.in_tab[b * P:(b + LOAD_BLOCKS) * P, :]
                             .rearrange("(b p) c -> p b c", p=P)).then_inc(tables_in, 16)
            sp.wait_ge(tables_in, 16 * (BLOCKS // LOAD_BLOCKS))

        @block.gpsimd
        def _(pool):
            pool.wait_ge(ready, 3)

            def tile(it):
                gen.wait_index(pool, it)
                settle(pool, gen.issued)
                for i in range(2):
                    gen.gather(pool, feats[:, i, 0:D], x, 1 - i, feats_in[i])
                    gen.gather(pool, old[:, i, :], tables[i], i, old_in[i])
                wait(pool, new_set, it.after())
                settle(pool, gen.issued)
                for i in range(2):
                    gen.scatter(pool, tables[i], i, new[:, i, :], stored[i])
            run_tiles(pool, tile)

        @block.tensor
        def _(pe):
            pe.wait_ge(loaded, 16 * (2 + BLOCKS // LOAD_BLOCKS))

            def tile(it):
                gen.spread(pe, sh, it, spread_ps)
                wait(pe, gen.same_set, it.after())
                for i in range(2):
                    wait(pe, feats_in[i], it.after(0, 16))
                    ins = pe.matmul(comb_ps[:, i * ROW:(i + 1) * ROW], gen.same[:, i, :], feats[:, i, :], start=True,
                                    stop=True)
                ins.then_inc(combined, 1)
                wait(pe, attr_in, it.after(0, 16))
                pe.transpose(turn_ps[:, 0:P], attr[:], sh.ident[:]).then_inc(turned, 1)
                wait(pe, turn_out, it.after())
                pe.matmul(score_ps[:, 0:HEADS], attr_t[:], wc[:], start=True, stop=True).then_inc(scored, 1)
            run_tiles(pe, tile)

        @block.scalar
        def _(act):
            def tile(it):
                wait(act, turned, it.after())
                act.activation(attr_t[:], turn_ps[:, 0:P], ACT.Copy).then_inc(turn_out, 1)
            run_tiles(act, tile)

        @block.vector
        def _(dve):
            dve.memset(zeros[:], 0.0).then_inc(ready, 1)
            dve.memset(feats[:, :, D:D + 1], 1.0).then_inc(ready, 1)
            dve.memset(feats[:, :, D + 1:ROW], 0.0).then_inc(ready, 1)
            dve.wait_ge(loaded, 16 * (2 + BLOCKS // LOAD_BLOCKS))

            def tile(it):
                gen.floats(dve, it)
                gen.masks(dve, it, spread_ps)
                for i in range(2):
                    wait(dve, old_in[i], it.after(0, 16))
                wait(dve, combined, it.after())
                dve.tensor_tensor(new[:], old[:], comb_ps[:, 0:2 * ROW].rearrange("p (i c) -> p i c", c=ROW),
                                  ALU.add).then_inc(new_set, 1)
                wait(dve, scored, it.after())
                dve.tensor_tensor(curv[:], score_ps[:, 0:HEADS], bc[:], ALU.add).then_inc(curv_set, 1)
            run_tiles(dve, tile)


def general_scores(nc, sh, src, dst, scores):
    with Scope(nc, "gb_") as sc:
        gen = General(nc, sc, src, dst)
        curv = sc.sb("curv", [P, HEADS])
        q_row = sc.sb("q_row", [P, D])
        kvy = sc.sb("kvy", [P, 3 * D])
        prod = sc.sb("prod", [P, D])
        dots = sc.sb("dots", [P, HEADS])
        score = sc.sb("score", [P, HEADS])
        drop = sc.sb("drop", [P, P])
        masked = sc.sb("masked", [P, HEADS, P])
        tile_max = sc.sb("tile_max", [P, HEADS])
        old = sc.sb("old", [P, HEADS])
        new = sc.sb("new", [P, HEADS])
        low = sc.sb("low", [P, HEADS])
        spread_ps = sc.ps("spread_ps")
        row_ps = [sc.ps(f"row_ps{i}", (P, 4, P)) for i in range(2)]
        (ready, filled, curv_in, q_in, kvy_in, old_in, prod_set, dot_set, score_set, kept, rows_set, drop_set,
         masked_set, max_set, new_set, stored) = (sc.sem(n) for n in (
             "ready", "filled", "curv_in", "q_in", "kvy_in", "old_in", "prod_set", "dot_set", "score_set", "kept",
             "rows_set", "drop_set", "masked_set", "max_set", "new_set", "stored"))
        block = sc.enter_context(nc.Block())

        @block.sync
        def _(sp):
            sp.wait_ge(ready, 1)
            with nc.allow_non_contiguous_dma(reason="short rows"):
                fill_table(sp, sh.max_tab, low, filled)
            sp.wait_ge(filled, 16)

            def tile(it):
                wait(sp, stored, it.before(0, 16))
                wait(sp, kept, it.before())
                gen.load(sp, it)
                t = slice(it.q, it.q + 1) if isinstance(it.q, int) else bass.ds(it.q, 1)
                sp.dma_start(curv[:], sh.curv_dram[:, t, :].rearrange("p o h -> p (o h)")).then_inc(curv_in, 16)
            run_tiles(sp, tile)

        @block.gpsimd
        def _(pool):
            def tile(it):
                gen.wait_index(pool, it)
                settle(pool, gen.issued)
                gen.gather(pool, q_row[:], sh.q_tab, 0, q_in)
                gen.gather(pool, old[:], sh.max_tab, 1, old_in)
                wait(pool, gen.row_set, it.after())
                settle(pool, gen.issued)
                gen.gather(pool, kvy[:], sh.kvy.rearrange("p b i c -> (p b) (i c)"), 2, kvy_in)
                wait(pool, new_set, it.after())
                settle(pool, gen.issued)
                gen.scatter(pool, sh.max_tab, 1, new[:], stored)
            run_tiles(pool, tile)
            pool.wait_ge(stored, 16 * TILES)

        @block.tensor
        def _(pe):
            def tile(it):
                gen.spread(pe, sh, it, spread_ps)
                wait(pe, score_set, it.after())
                for h in range(HEADS):
                    ins = pe.transpose(row_ps[h // 4][:, h % 4, :], score[:, h:h + 1].to_broadcast([P, P]), sh.ident[:])
                ins.then_inc(rows_set, 1)
            run_tiles(pe, tile)

        @block.vector
        def _(dve):
            dve.memset(low[:], -2 * BIG).then_inc(ready, 1)

            def tile(it):
                gen.floats(dve, it)
                gen.kvy_rows(dve, it)
                gen.masks(dve, it, spread_ps)
                wait(dve, gen.same_set, it.after())
                dve.tensor_scalar(drop[:], gen.same[:, 1, :], 1.0, BIG, ALU.subtract, ALU.mult).then_inc(drop_set, 1)
                wait(dve, q_in, it.after(0, 16))
                wait(dve, kvy_in, it.after(0, 16))
                dve.tensor_tensor(prod[:], q_row[:], kvy[:, 0:D], ALU.mult).then_inc(prod_set, 1)
                wait(dve, prod_set, it.after())
                dve.tensor_reduce(dots[:], prod[:].rearrange("p (h c) -> p h c", c=HEAD_D), AX.X, ALU.add)\
                    .then_inc(dot_set, 1)
                wait(dve, dot_set, it.after())
                wait(dve, curv_in, it.after(0, 16))
                dve.tensor_tensor(score[:], dots[:], curv[:], ALU.add).then_inc(score_set, 1)
                wait(dve, score_set, it.after())
                t = slice(it.q, it.q + 1) if isinstance(it.q, int) else bass.ds(it.q, 1)
                dve.tensor_scalar(scores[:, t, :].rearrange("p o h -> p (o h)"), score[:], 1.0, None, ALU.mult)\
                    .then_inc(kept, 1)
                wait(dve, rows_set, it.after())
                wait(dve, drop_set, it.after())
                for i in range(2):
                    ins = dve.tensor_tensor(masked[:, 4 * i:4 * i + 4, :], row_ps[i][:],
                                            drop[:, None, :].to_broadcast([P, 4, P]), ALU.add)
                ins.then_inc(masked_set, 1)
                wait(dve, masked_set, it.after())
                dve.tensor_reduce(tile_max[:], masked[:], AX.X, ALU.max).then_inc(max_set, 1)
                wait(dve, max_set, it.after())
                wait(dve, old_in, it.after(0, 16))
                dve.tensor_tensor(new[:], old[:], tile_max[:], ALU.max).then_inc(new_set, 1)
            run_tiles(dve, tile)

        @block.scalar
        def _(act):
            act.wait_ge(ready, 1)


def general_sums(nc, sh, src, dst, scores):
    with Scope(nc, "gc_") as sc:
        gen = General(nc, sc, src, dst)
        peak = sc.sb("peak", [P, HEADS])
        shifted = sc.sb("shifted", [P, HEADS])
        weight = sc.sb("weight", [P, HEADS])
        old = sc.sb("old", [P, HEADS])
        new = sc.sb("new", [P, HEADS])
        zeros = sc.sb("zeros", [P, HEADS])
        spread_ps, comb_ps = sc.ps("spread_ps"), sc.ps("comb_ps")
        ready, filled, peak_in, old_in, shift_set, exp_set, kept, combined, new_set, stored = (sc.sem(n) for n in (
            "ready", "filled", "peak_in", "old_in", "shift_set", "exp_set", "kept", "combined", "new_set", "stored"))
        block = sc.enter_context(nc.Block())

        @block.sync
        def _(sp):
            sp.wait_ge(ready, 1)
            with nc.allow_non_contiguous_dma(reason="short rows"):
                fill_table(sp, sh.weight_tab, zeros, filled)
            sp.wait_ge(filled, 16)

            def tile(it):
                wait(sp, stored, it.before(0, 16))
                wait(sp, kept, it.before())
                gen.load(sp, it)
            run_tiles(sp, tile)

        @block.gpsimd
        def _(pool):
            def tile(it):
                gen.wait_index(pool, it)
                settle(pool, gen.issued)
                gen.gather(pool, peak[:], sh.max_tab, 1, peak_in)
                gen.gather(pool, old[:], sh.weight_tab, 1, old_in)
                wait(pool, new_set, it.after())
                settle(pool, gen.issued)
                gen.scatter(pool, sh.weight_tab, 1, new[:], stored)
            run_tiles(pool, tile)
            pool.wait_ge(stored, 16 * TILES)

        @block.tensor
        def _(pe):
            def tile(it):
                gen.spread(pe, sh, it, spread_ps)
                wait(pe, gen.same_set, it.after())
                wait(pe, exp_set, it.after())
                pe.matmul(comb_ps[:, 0:HEADS], gen.same[:, 1, :], weight[:], start=True, stop=True)\
                    .then_inc(combined, 1)
            run_tiles(pe, tile)

        @block.scalar
        def _(act):
            def tile(it):
                wait(act, shift_set, it.after())
                act.activation(weight[:], shifted[:], ACT.Exp).then_inc(exp_set, 1)
            run_tiles(act, tile)

        @block.vector
        def _(dve):
            dve.memset(zeros[:], 0.0).then_inc(ready, 1)

            def tile(it):
                gen.floats(dve, it)
                gen.masks(dve, it, spread_ps)
                t = slice(it.q, it.q + 1) if isinstance(it.q, int) else bass.ds(it.q, 1)
                mine = scores[:, t, :].rearrange("p o h -> p (o h)")
                wait(dve, peak_in, it.after(0, 16))
                dve.tensor_tensor(shifted[:], mine, peak[:], ALU.subtract).then_inc(shift_set, 1)
                wait(dve, exp_set, it.after())
                dve.tensor_scalar(mine, weight[:], 1.0, None, ALU.mult).then_inc(kept, 1)
                wait(dve, old_in, it.after(0, 16))
                wait(dve, combined, it.after())
                dve.tensor_tensor(new[:], old[:], comb_ps[:, 0:HEADS], ALU.add).then_inc(new_set, 1)
            run_tiles(dve, tile)


def general_messages(nc, sh, src, dst, scores):
    with Scope(nc, "gd_") as sc:
        gen = General(nc, sc, src, dst)
        total = sc.sb("total", [P, HEADS])
        inverse = sc.sb("inverse", [P, HEADS])
        prob = sc.sb("prob", [P, HEADS])
        kvy = sc.sb("kvy", [P, 3 * D])
        message = sc.sb("message", [P, D])
        old = sc.sb("old", [P, D])
        new = sc.sb("new", [P, D])
        spread_ps, comb_ps = sc.ps("spread_ps"), sc.ps("comb_ps")
        total_in, kvy_in, old_in, inverted, prob_set, message_set, combined, new_set, stored = (
            sc.sem(n) for n in ("total_in", "kvy_in", "old_in", "inverted", "prob_set", "message_set", "combined",
                                "new_set", "stored"))
        block = sc.enter_context(nc.Block())

        @block.sync
        def _(sp):
            def tile(it):
                wait(sp, stored, it.before(0, 16))
                gen.load(sp, it)
            run_tiles(sp, tile)

        @block.gpsimd
        def _(pool):
            def tile(it):
                gen.wait_index(pool, it)
                settle(pool, gen.issued)
                gen.gather(pool, total[:], sh.weight_tab, 1, total_in)
                gen.gather(pool, old[:], sh.msg_tabs[0], 0, old_in)
                wait(pool, gen.row_set, it.after())
                settle(pool, gen.issued)
                gen.gather(pool, kvy[:], sh.kvy.rearrange("p b i c -> (p b) (i c)"), 2, kvy_in)
                wait(pool, new_set, it.after())
                settle(pool, gen.issued)
                gen.scatter(pool, sh.msg_tabs[0], 0, new[:], stored)
            run_tiles(pool, tile)
            pool.wait_ge(stored, 16 * TILES)

        @block.tensor
        def _(pe):
            def tile(it):
                gen.spread(pe, sh, it, spread_ps)
                wait(pe, gen.same_set, it.after())
                wait(pe, message_set, it.after())
                pe.matmul(comb_ps[:, 0:D], gen.same[:, 0, :], message[:], start=True, stop=True).then_inc(combined, 1)
            run_tiles(pe, tile)

        @block.vector
        def _(dve):
            def tile(it):
                gen.floats(dve, it)
                gen.kvy_rows(dve, it)
                gen.masks(dve, it, spread_ps)
                wait(dve, total_in, it.after(0, 16))
                dve.reciprocal(inverse[:], total[:]).then_inc(inverted, 1)
                wait(dve, inverted, it.after())
                t = slice(it.q, it.q + 1) if isinstance(it.q, int) else bass.ds(it.q, 1)
                dve.tensor_tensor(prob[:], scores[:, t, :].rearrange("p o h -> p (o h)"), inverse[:], ALU.mult)\
                    .then_inc(prob_set, 1)
                wait(dve, prob_set, it.after())
                wait(dve, kvy_in, it.after(0, 16))
                dve.tensor_tensor(message[:].rearrange("p (h c) -> p h c", c=HEAD_D),
                                  kvy[:, D:2 * D].rearrange("p (h c) -> p h c", c=HEAD_D),
                                  prob[:, :, None].to_broadcast([P, HEADS, HEAD_D]), ALU.mult)\
                    .then_inc(message_set, 1)
                wait(dve, old_in, it.after(0, 16))
                wait(dve, combined, it.after())
                dve.tensor_tensor(new[:], old[:], comb_ps[:, 0:D], ALU.add).then_inc(new_set, 1)
            run_tiles(dve, tile)

        @block.scalar
        def _(act):
            act.wait_ge(new_set, TILES)


_OUT_SHAPE = (N_NODES, D)


def kernel(**inputs):
    import concourse.bacc as bacc
    from concourse.bass_utils import run_bass_kernel_spmd

    nc = bacc.Bacc("TRN2", target_bir_lowering=False, num_devices=1)
    arrays, aps = {}, {}
    for name, a in inputs.items():
        a = np.ascontiguousarray(a)
        if name == "x":
            a = np.pad(a, ((0, NODES_PAD - N_NODES), (0, 0)))
        elif name == "src":
            a = np.pad(a, (0, EDGES_PAD - N_EDGES), constant_values=NODES_PAD - 1).reshape(TILES, P)
        elif name == "dst":
            a = np.pad(a, (1, EDGES_PAD - N_EDGES + 1), constant_values=(-1, NODES_PAD - 1))
            a[-1] = NODES_PAD
        arrays[name] = a
        aps[name] = nc.dram_tensor(f"{name}", a.shape, mybir.dt.from_np(a.dtype), kind="ExternalInput").ap()
    out = nc.dram_tensor("out", _OUT_SHAPE, F32, kind="ExternalOutput").ap()
    x, src, dst, edge_attr = (aps.pop(n) for n in ("x", "src", "dst", "edge_attr_128"))
    build(nc, x, src, dst, edge_attr, aps, out)
    return run_bass_kernel_spmd(nc, [arrays], core_ids=[0]).results[0]["out"]
```
